# Optimizing a Trainium2 kernel written in Bass

```python
import numpy as np
import jax
import jax.numpy as jnp

def _softmax(x, axis=-1):
    return jax.nn.softmax(x, axis=axis)

def _gelu(x):
    return jax.nn.gelu(x, approximate=True)

def _silu(x):
    return jax.nn.silu(x)

def _sigmoid(x):
    return jax.nn.sigmoid(x)

def _layernorm(x, axis=-1, eps=1e-05):
    m = jnp.mean(x, axis=axis, keepdims=True)
    v = jnp.var(x, axis=axis, keepdims=True)
    return (x - m) / jnp.sqrt(v + eps)

def _scatter_add(tgt, idx, src, axis=0):
    return tgt.at[idx].add(src)

def _segment_sum(src, seg, n):
    return jax.ops.segment_sum(src, seg, n)
kernel_name = 'mk_adaln_attn_ffn_d2_seqx_r8_0fa919'

def setup_inputs(seed: int=0):
    np.random.seed(seed)
    _w = jnp.asarray

    def _rec_inputs():
        import jax
        import jax.numpy as jnp
        _rk = jax.random.key(seed)
        x = 7.22e-05 + 1 * jax.random.normal(jax.random.fold_in(_rk, 1), (16, 128, 128), jnp.float32)
        _lenS = 128 - jax.random.randint(jax.random.fold_in(_rk, 7), (16,), 0, max(1, 128 // 4) + 1, jnp.int32)
        _lenS2 = 128 - jax.random.randint(jax.random.fold_in(_rk, 8), (16,), 0, max(1, 128 // 4) + 1, jnp.int32)
        cond_8 = -0.104238 + 1.01173 * jax.random.normal(jax.random.fold_in(_rk, 11), (16, 8), jnp.float32)
        return (x, cond_8)
    x, cond_8 = _rec_inputs()

    def _L0_cond_setup():
        import jax, jax.numpy as jnp
        import numpy as np
        TOP_K = 2
        NUM_MOE_LAYERS = 12

        def _gemma_mlp(x, gate_w, up_w, down_w):
            g = jnp.einsum('bsh,hi->bsi', x, gate_w)
            u = jnp.einsum('bsh,hi->bsi', x, up_w)
            return jnp.einsum('bsi,ih->bsh', jax.nn.gelu(g, approximate=True) * u, down_w)
        key = jax.random.key(seed)
        ks = jax.random.split(key, 8)
        B, S, H, I, E = (32, 32, 128, 512, 8)
        std = 0.02
        return {'x': jax.random.normal(ks[0], (B, S, H), jnp.float32), 'router_logits': jax.random.normal(ks[1], (B, E), jnp.float32), 'skill_gate': jax.random.normal(ks[2], (E, H, I), jnp.float32) * std, 'skill_up': jax.random.normal(ks[3], (E, H, I), jnp.float32) * std, 'skill_down': jax.random.normal(ks[4], (E, I, H), jnp.float32) * std, 'shared_gate': jax.random.normal(ks[5], (H, I), jnp.float32) * std, 'shared_up': jax.random.normal(ks[6], (H, I), jnp.float32) * std, 'shared_down': jax.random.normal(ks[7], (I, H), jnp.float32) * std}
    _L0_cond_all = _L0_cond_setup()
    _L0_cond_in = {k: v for k, v in _L0_cond_all.items() if k in ('skill_gate', 'skill_up', 'skill_down', 'shared_gate', 'shared_up', 'shared_down')}
    del _L0_cond_all

    def _L0_attn_setup():
        import jax, jax.numpy as jnp
        import numpy as np
        L, B, E = (256, 4, 128)
        S = 128
        EH = 2 * E
        CHUNK = 64
        MAXPOS = 64
        EPS = 1e-05

        def rope(x, axes):
            shape = x.shape
            spatial = [shape[i] for i in axes]
            total = int(np.prod(spatial))
            pos = jnp.arange(total, dtype=x.dtype).reshape(spatial)
            for _ in range(axes[-1] + 1, len(shape) - 1):
                pos = pos[..., None]
            half = shape[-1] // 2
            inv_freq = 10000.0 ** (-jnp.arange(half, dtype=x.dtype) / half)
            sinusoid = pos[..., None] * inv_freq
            sin, cos = (jnp.sin(sinusoid), jnp.cos(sinusoid))
            x1, x2 = jnp.split(x, 2, axis=-1)
            return jnp.concatenate([x1 * cos - x2 * sin, x2 * cos + x1 * sin], axis=-1)

        def rel_pos_bias(w, seq_len):
            t = jnp.pad(w[:2 * seq_len - 1], (0, seq_len))
            t = jnp.tile(t, seq_len)[:-seq_len].reshape(seq_len, 3 * seq_len - 2)
            r = (2 * seq_len - 1) // 2
            return t[:, r:-r]
        key = jax.random.key(seed)
        ks = jax.random.split(key, 12)

        def n(k, shape, std):
            return jax.random.normal(k, shape, dtype=jnp.float32) * std
        query = jax.random.normal(ks[0], (L, B, E), dtype=jnp.float32)
        return dict(query=query, key_in=query, value_in=query, ln_g=jnp.ones((E,), jnp.float32), ln_b=jnp.zeros((E,), jnp.float32), Wu=n(ks[1], (EH, E), 1.0 / np.sqrt(E)), bu=jnp.zeros((EH,), jnp.float32), Wv=n(ks[2], (EH, E), 1.0 / np.sqrt(E)), bv=jnp.zeros((EH,), jnp.float32), Wb=n(ks[3], (S, E), 1.0 / np.sqrt(E)), bb=jnp.zeros((S,), jnp.float32), qqw=n(ks[4], (S,), 0.02), qqb=jnp.zeros((S,), jnp.float32), qkw=n(ks[5], (S,), 0.02), qkb=jnp.zeros((S,), jnp.float32), lqw=n(ks[6], (S,), 0.02), lqb=jnp.zeros((S,), jnp.float32), lkw=n(ks[7], (S,), 0.02), lkb=jnp.zeros((S,), jnp.float32), Wo=n(ks[8], (E, EH), 1.0 / np.sqrt(EH)), bo=jnp.zeros((E,), jnp.float32), w_rel=n(ks[9], (2 * MAXPOS - 1,), 0.02))
    _L0_attn_all = _L0_attn_setup()
    _L0_attn_in = {k: v for k, v in _L0_attn_all.items() if k in ('key_in', 'value_in', 'ln_g', 'ln_b', 'Wu', 'bu', 'Wv', 'bv', 'Wb', 'bb', 'qqw', 'qqb', 'qkw', 'qkb', 'lqw', 'lqb', 'lkw', 'lkb', 'Wo', 'bo', 'w_rel')}
    del _L0_attn_all

    def _L0_cond2_setup():
        import jax, jax.numpy as jnp
        import numpy as np
        R = 16
        ALPHA = 32.0
        SCALING = ALPHA / R
        key = jax.random.key(seed)
        ks = jax.random.split(key, 6)
        B, T, C, O, E = (16, 1500, 128, 128, 8)
        x = jax.random.normal(ks[0], (B, T, C), dtype=jnp.float32)
        w = jax.random.uniform(ks[1], (B, E), dtype=jnp.float32)
        W_base = jax.random.normal(ks[2], (O, C), dtype=jnp.float32) * 0.02
        b_base = jax.random.normal(ks[3], (O,), dtype=jnp.float32) * 0.02
        As = jax.random.normal(ks[4], (E, R, C), dtype=jnp.float32) * 0.02
        Bs = jax.random.normal(ks[5], (E, O, R), dtype=jnp.float32) * 0.02
        return {'x': x, 'w': w, 'W_base': W_base, 'b_base': b_base, 'As': As, 'Bs': Bs}
    _L0_cond2_all = _L0_cond2_setup()
    _L0_cond2_in = {k: v for k, v in _L0_cond2_all.items() if k in ('W_base', 'b_base', 'As', 'Bs')}
    del _L0_cond2_all

    def _L0_ffn_setup():
        import jax, jax.numpy as jnp
        import numpy as np
        BLOCK = 32
        W_BITS = 4
        ACT_BITS = 16

        def act_qdq(x):
            qmax = 2.0 ** (ACT_BITS - 1) - 1.0
            scale = jnp.maximum(jnp.max(jnp.abs(x)) / qmax, 1e-12)
            return jnp.clip(jnp.round(x / scale), -qmax - 1.0, qmax) * scale

        def fixed_qdq_u16(x):
            scale = 1.0 / 65536.0
            return jnp.clip(jnp.round(x / scale), 0.0, 65535.0) * scale

        def lpbq_dequant(w):
            O, I = w.shape
            qmax = 2.0 ** (W_BITS - 1) - 1.0
            wb = w.reshape(O, I // BLOCK, BLOCK)
            s = jnp.maximum(jnp.max(jnp.abs(wb), axis=-1, keepdims=True) / qmax, 1e-12)
            wq = jnp.clip(jnp.round(wb / s), -qmax - 1.0, qmax) * s
            return wq.reshape(O, I)
        key = jax.random.key(seed)
        k1, k2, k3, k4 = jax.random.split(key, 4)
        B, S, H, I = (2, 512, 128, 384)
        x = jax.random.normal(k1, (B, S, H), jnp.float32)
        w_gate = jax.random.normal(k2, (I, H), jnp.float32) * 0.02
        w_up = jax.random.normal(k3, (I, H), jnp.float32) * 0.02
        w_down = jax.random.normal(k4, (H, I), jnp.float32) * 0.02
        return {'x': x, 'w_gate': w_gate, 'w_up': w_up, 'w_down': w_down}
    _L0_ffn_all = _L0_ffn_setup()
    _L0_ffn_in = {k: v for k, v in _L0_ffn_all.items() if k in ('w_gate', 'w_up', 'w_down')}
    del _L0_ffn_all

    def _L1_cond_setup():
        import jax, jax.numpy as jnp
        import numpy as np
        key = jax.random.key(seed)
        k1, k2, k3, k4, k5 = jax.random.split(key, 5)
        B, N, T, O, G = (32, 32, 128, 128, 8)
        x = jax.random.normal(k1, (B, N, T), dtype=jnp.float32)
        y = jax.random.uniform(k2, (B, G), dtype=jnp.float32)
        weight = jax.random.normal(k3, (G, O, T), dtype=jnp.float32) * (1.0 / np.sqrt(T))
        mask = jax.random.uniform(k4, (O, T), dtype=jnp.float32)
        bias = jax.random.normal(k5, (O,), dtype=jnp.float32)
        return {'x': x, 'y': y, 'weight': weight, 'mask': mask, 'bias': bias}
    _L1_cond_all = _L1_cond_setup()
    _L1_cond_in = {k: v for k, v in _L1_cond_all.items() if k in ('weight', 'mask', 'bias')}
    del _L1_cond_all

    def _L1_attn_setup():
        import jax, jax.numpy as jnp
        import numpy as np
        GAMMA = 0.96875
        H = 128
        B = 4
        L = 256
        key = jax.random.key(seed)
        k0, k1, k2, k3, k4 = jax.random.split(key, 5)
        x = jax.random.normal(k0, (B, L, H), dtype=jnp.float32)
        weight_q = jax.random.normal(k1, (H, H), dtype=jnp.float32) / H
        weight_k = jax.random.normal(k2, (H, H), dtype=jnp.float32) / H
        weight_v = jax.random.normal(k3, (H, H), dtype=jnp.float32) / H
        theta = jax.random.normal(k4, (H,), dtype=jnp.float32) / H
        return {'x': x, 'weight_q': weight_q, 'weight_k': weight_k, 'weight_v': weight_v, 'theta': theta}
    _L1_attn_all = _L1_attn_setup()
    _L1_attn_in = {k: v for k, v in _L1_attn_all.items() if k in ('weight_q', 'weight_k', 'weight_v', 'theta')}
    del _L1_attn_all

    def _L1_cond2_setup():
        import jax, jax.numpy as jnp
        import numpy as np
        B, S, D = (16, 256, 128)
        E, H = (8, 256)
        key = jax.random.key(seed)
        ks = jax.random.split(key, 8)
        scale = 0.02
        x = jax.random.normal(ks[0], (B, S, D), dtype=jnp.float32)
        opcode_onehot = jax.random.uniform(ks[1], (B, E), dtype=jnp.float32)
        W_up = jax.random.normal(ks[2], (E, H, D), dtype=jnp.float32) * scale
        b_up = jnp.zeros((E, H), dtype=jnp.float32)
        W_gate = jax.random.normal(ks[3], (E, H, D), dtype=jnp.float32) * scale
        b_gate = jnp.zeros((E, H), dtype=jnp.float32)
        W_down = jax.random.normal(ks[4], (E, D, H), dtype=jnp.float32) * scale
        b_down = jnp.zeros((E, D), dtype=jnp.float32)
        return {'x': x, 'opcode_onehot': opcode_onehot, 'W_up': W_up, 'b_up': b_up, 'W_gate': W_gate, 'b_gate': b_gate, 'W_down': W_down, 'b_down': b_down}
    _L1_cond2_all = _L1_cond2_setup()
    _L1_cond2_in = {k: v for k, v in _L1_cond2_all.items() if k in ('W_up', 'b_up', 'W_gate', 'b_gate', 'W_down', 'b_down')}
    del _L1_cond2_all

    def _L1_ffn_setup():
        import jax, jax.numpy as jnp
        import numpy as np
        B, T, C, H, E, MIN_E = (4, 256, 128, 128, 16, 2)
        IS_CAUSAL = False

        def _forward(hidden_states, sim_matrix, gates, q_proj, k_proj, v_proj, o_proj):
            b, t, c = hidden_states.shape
            n = b * t
            x = hidden_states.reshape(n, c)
            xn = x / jnp.maximum(jnp.linalg.norm(x, axis=-1, keepdims=True), 1e-12)
            sn = sim_matrix / jnp.maximum(jnp.linalg.norm(sim_matrix, axis=0, keepdims=True), 1e-12)
            logits = xn @ sn - jax.nn.sigmoid(gates)
            gated = jax.nn.relu(logits)
            hard = (gated > 0).astype(gated.dtype)
            mask = gated + jax.lax.stop_gradient(hard - gated)
            inactive = jnp.sum(hard, axis=1) == 0
            _, fb_idx = jax.lax.top_k(logits, MIN_E)
            fb = jnp.zeros((n, logits.shape[1]), gated.dtype).at[jnp.arange(n)[:, None], fb_idx].set(1.0)
            put = jax.lax.stop_gradient(inactive[:, None].astype(gated.dtype) * fb)
            mask = mask * (1.0 - put) + put
            masked = jnp.where(mask > 0, gated, -jnp.inf)
            w = jax.nn.softmax(masked, axis=-1)

            def moe_proj(p):
                y = jnp.einsum('nc,ech->neh', x, p)
                return jnp.einsum('ne,neh->nh', w, y)
            q = moe_proj(q_proj).reshape(b, t, -1)
            k = moe_proj(k_proj).reshape(b, t, -1)
            v = moe_proj(v_proj).reshape(b, t, -1)
            h = q.shape[-1]
            scores = jnp.einsum('bth,bsh->bts', q, k) / jnp.sqrt(jnp.asarray(h, q.dtype))
            if IS_CAUSAL and t > 1:
                causal = jnp.tril(jnp.ones((t, t), bool))
                scores = jnp.where(causal[None], scores, -jnp.inf)
            attn = jax.nn.softmax(scores, axis=-1)
            o = jnp.einsum('bts,bsh->bth', attn, v).reshape(n, h)
            z = jnp.einsum('ne,nh->enh', w, o)
            out = jnp.einsum('enh,ehc->nc', z, o_proj)
            return out.reshape(b, t, c)
        key = jax.random.key(seed)
        ks = jax.random.split(key, 6)
        lim_qkv = float(np.sqrt(6.0 / (C + H)))
        inp = {'hidden_states': jax.random.normal(ks[0], (B, T, C), jnp.float32), 'sim_matrix': jax.random.normal(ks[1], (C, E), jnp.float32), 'gates': jnp.zeros((E,), jnp.float32), 'q_proj': jax.random.uniform(ks[2], (E, C, H), jnp.float32, -lim_qkv, lim_qkv), 'k_proj': jax.random.uniform(ks[3], (E, C, H), jnp.float32, -lim_qkv, lim_qkv), 'v_proj': jax.random.uniform(ks[4], (E, C, H), jnp.float32, -lim_qkv, lim_qkv), 'o_proj': jax.random.uniform(ks[5], (E, H, C), jnp.float32, -lim_qkv, lim_qkv)}
        return inp
    _L1_ffn_all = _L1_ffn_setup()
    _L1_ffn_in = {k: v for k, v in _L1_ffn_all.items() if k in ('sim_matrix', 'gates', 'q_proj', 'k_proj', 'v_proj', 'o_proj')}
    del _L1_ffn_all
    return {'x': x, 'cond_8': cond_8, 'L0_cond_skill_gate': _L0_cond_in['skill_gate'], 'L0_cond_skill_up': _L0_cond_in['skill_up'], 'L0_cond_skill_down': _L0_cond_in['skill_down'], 'L0_cond_shared_gate': _L0_cond_in['shared_gate'], 'L0_cond_shared_up': _L0_cond_in['shared_up'], 'L0_cond_shared_down': _L0_cond_in['shared_down'], 'L0_attn_key_in': _L0_attn_in['key_in'], 'L0_attn_value_in': _L0_attn_in['value_in'], 'L0_attn_ln_g': _L0_attn_in['ln_g'], 'L0_attn_ln_b': _L0_attn_in['ln_b'], 'L0_attn_Wu': _L0_attn_in['Wu'], 'L0_attn_bu': _L0_attn_in['bu'], 'L0_attn_Wv': _L0_attn_in['Wv'], 'L0_attn_bv': _L0_attn_in['bv'], 'L0_attn_Wb': _L0_attn_in['Wb'], 'L0_attn_bb': _L0_attn_in['bb'], 'L0_attn_qqw': _L0_attn_in['qqw'], 'L0_attn_qqb': _L0_attn_in['qqb'], 'L0_attn_qkw': _L0_attn_in['qkw'], 'L0_attn_qkb': _L0_attn_in['qkb'], 'L0_attn_lqw': _L0_attn_in['lqw'], 'L0_attn_lqb': _L0_attn_in['lqb'], 'L0_attn_lkw': _L0_attn_in['lkw'], 'L0_attn_lkb': _L0_attn_in['lkb'], 'L0_attn_Wo': _L0_attn_in['Wo'], 'L0_attn_bo': _L0_attn_in['bo'], 'L0_attn_w_rel': _L0_attn_in['w_rel'], 'L0_cond2_W_base': _L0_cond2_in['W_base'], 'L0_cond2_b_base': _L0_cond2_in['b_base'], 'L0_cond2_As': _L0_cond2_in['As'], 'L0_cond2_Bs': _L0_cond2_in['Bs'], 'L0_ffn_w_gate': _L0_ffn_in['w_gate'], 'L0_ffn_w_up': _L0_ffn_in['w_up'], 'L0_ffn_w_down': _L0_ffn_in['w_down'], 'L1_cond_weight': _L1_cond_in['weight'], 'L1_cond_mask': _L1_cond_in['mask'], 'L1_cond_bias': _L1_cond_in['bias'], 'L1_attn_weight_q': _L1_attn_in['weight_q'], 'L1_attn_weight_k': _L1_attn_in['weight_k'], 'L1_attn_weight_v': _L1_attn_in['weight_v'], 'L1_attn_theta': _L1_attn_in['theta'], 'L1_cond2_W_up': _L1_cond2_in['W_up'], 'L1_cond2_b_up': _L1_cond2_in['b_up'], 'L1_cond2_W_gate': _L1_cond2_in['W_gate'], 'L1_cond2_b_gate': _L1_cond2_in['b_gate'], 'L1_cond2_W_down': _L1_cond2_in['W_down'], 'L1_cond2_b_down': _L1_cond2_in['b_down'], 'L1_ffn_sim_matrix': _L1_ffn_in['sim_matrix'], 'L1_ffn_gates': _L1_ffn_in['gates'], 'L1_ffn_q_proj': _L1_ffn_in['q_proj'], 'L1_ffn_k_proj': _L1_ffn_in['k_proj'], 'L1_ffn_v_proj': _L1_ffn_in['v_proj'], 'L1_ffn_o_proj': _L1_ffn_in['o_proj']}

def reference(x, cond_8, L0_cond_skill_gate, L0_cond_skill_up, L0_cond_skill_down, L0_cond_shared_gate, L0_cond_shared_up, L0_cond_shared_down, L0_attn_key_in, L0_attn_value_in, L0_attn_ln_g, L0_attn_ln_b, L0_attn_Wu, L0_attn_bu, L0_attn_Wv, L0_attn_bv, L0_attn_Wb, L0_attn_bb, L0_attn_qqw, L0_attn_qqb, L0_attn_qkw, L0_attn_qkb, L0_attn_lqw, L0_attn_lqb, L0_attn_lkw, L0_attn_lkb, L0_attn_Wo, L0_attn_bo, L0_attn_w_rel, L0_cond2_W_base, L0_cond2_b_base, L0_cond2_As, L0_cond2_Bs, L0_ffn_w_gate, L0_ffn_w_up, L0_ffn_w_down, L1_cond_weight, L1_cond_mask, L1_cond_bias, L1_attn_weight_q, L1_attn_weight_k, L1_attn_weight_v, L1_attn_theta, L1_cond2_W_up, L1_cond2_b_up, L1_cond2_W_gate, L1_cond2_b_gate, L1_cond2_W_down, L1_cond2_b_down, L1_ffn_sim_matrix, L1_ffn_gates, L1_ffn_q_proj, L1_ffn_k_proj, L1_ffn_v_proj, L1_ffn_o_proj):
    import jax
    import jax.numpy as jnp

    def _L0_cond_ref(x, router_logits, skill_gate, skill_up, skill_down, shared_gate, shared_up, shared_down):
        import jax, jax.numpy as jnp
        import numpy as np
        TOP_K = 2
        NUM_MOE_LAYERS = 12

        def _gemma_mlp(x, gate_w, up_w, down_w):
            g = jnp.einsum('bsh,hi->bsi', x, gate_w)
            u = jnp.einsum('bsh,hi->bsi', x, up_w)
            return jnp.einsum('bsi,ih->bsh', jax.nn.gelu(g, approximate=True) * u, down_w)
        B = x.shape[0]
        E = skill_gate.shape[0]
        rw = jax.nn.softmax(router_logits.astype(jnp.float32), axis=-1)
        w, sel = jax.lax.top_k(rw, TOP_K)
        w = w / w.sum(axis=-1, keepdims=True)
        w = w.astype(x.dtype)
        scale = 1.0 / NUM_MOE_LAYERS
        w = scale * w + (1.0 - scale) * jax.lax.stop_gradient(w)
        dense_w = jnp.zeros((B, E), x.dtype).at[jnp.arange(B)[:, None], sel].add(w)

        def step(acc, params):
            g, u, d, we = params
            return (acc + we[:, None, None] * _gemma_mlp(x, g, u, d), None)
        out, _ = jax.lax.scan(step, jnp.zeros_like(x), (skill_gate, skill_up, skill_down, dense_w.T))
        out = out + _gemma_mlp(x, shared_gate, shared_up, shared_down)
        return out

    def _L0_attn_ref(query, key_in, value_in, ln_g, ln_b, Wu, bu, Wv, bv, Wb, bb, qqw, qqb, qkw, qkb, lqw, lqb, lkw, lkb, Wo, bo, w_rel):
        import jax, jax.numpy as jnp
        import numpy as np
        L, B, E = (256, 4, 128)
        S = 128
        EH = 2 * E
        CHUNK = 64
        MAXPOS = 64
        EPS = 1e-05

        def rope(x, axes):
            shape = x.shape
            spatial = [shape[i] for i in axes]
            total = int(np.prod(spatial))
            pos = jnp.arange(total, dtype=x.dtype).reshape(spatial)
            for _ in range(axes[-1] + 1, len(shape) - 1):
                pos = pos[..., None]
            half = shape[-1] // 2
            inv_freq = 10000.0 ** (-jnp.arange(half, dtype=x.dtype) / half)
            sinusoid = pos[..., None] * inv_freq
            sin, cos = (jnp.sin(sinusoid), jnp.cos(sinusoid))
            x1, x2 = jnp.split(x, 2, axis=-1)
            return jnp.concatenate([x1 * cos - x2 * sin, x2 * cos + x1 * sin], axis=-1)

        def rel_pos_bias(w, seq_len):
            t = jnp.pad(w[:2 * seq_len - 1], (0, seq_len))
            t = jnp.tile(t, seq_len)[:-seq_len].reshape(seq_len, 3 * seq_len - 2)
            r = (2 * seq_len - 1) // 2
            return t[:, r:-r]
        tgt_len = query.shape[0]
        len_pad = (CHUNK - tgt_len % CHUNK) % CHUNK
        q = jnp.pad(query, ((0, len_pad), (0, 0), (0, 0)))
        Lp = q.shape[0]
        nc = Lp // CHUNK
        q = q.transpose(1, 0, 2)
        shortcut = q
        mu = q.mean(-1, keepdims=True)
        var = q.var(-1, keepdims=True)
        xn = (q - mu) / jnp.sqrt(var + EPS) * ln_g + ln_b
        u = jax.nn.silu(xn @ Wu.T + bu)
        v = jax.nn.silu(xn @ Wv.T + bv)
        base = jax.nn.silu(xn @ Wb.T + bb)
        bsz = q.shape[0]

        def mk(wt, bi):
            t = (base * wt + bi).reshape(bsz, nc, CHUNK, S)
            return rope(t, [1, 2])
        quad_q, quad_k = (mk(qqw, qqb), mk(qkw, qkb))
        lin_q, lin_k = (mk(lqw, lqb), mk(lkw, lkb))
        vch = v.reshape(bsz, nc, CHUNK, EH)
        quad_qk = jnp.einsum('bgne,bgme->bgnm', quad_q, quad_k)
        bias = rel_pos_bias(w_rel, MAXPOS)[:CHUNK, :CHUNK]
        kernel = jnp.square(jax.nn.relu(quad_qk / CHUNK + bias))
        causal = jnp.tril(jnp.ones((CHUNK, CHUNK), dtype=bool))
        kernel = jnp.where(causal, kernel, 0.0)
        quadratic = jnp.einsum('bgnm,bgme->bgne', kernel, vch)
        lin_kv = jnp.einsum('bgnk,bgne->bgke', lin_k, vch) / CHUNK
        cmask = jnp.tril(jnp.ones((nc, nc), dtype=lin_kv.dtype), k=-1)
        lin_kv = jnp.einsum('bhke,gh->bgke', lin_kv, cmask)
        linear = jnp.einsum('bgnk,bgke->bgne', lin_q, lin_kv)
        x = (u.reshape(bsz, nc, CHUNK, EH) * (linear + quadratic)).reshape(bsz, Lp, EH)
        x = x @ Wo.T + bo
        out = (x + shortcut).transpose(1, 0, 2)[:tgt_len]
        return out

    def _L0_cond2_ref(x, w, W_base, b_base, As, Bs):
        import jax, jax.numpy as jnp
        import numpy as np
        R = 16
        ALPHA = 32.0
        SCALING = ALPHA / R
        out = jnp.einsum('btc,oc->bto', x, W_base) + b_base
        h = jnp.einsum('btc,erc->bter', x, As)
        lora = jnp.einsum('bter,eor,be->bto', h, Bs, w)
        return out + lora * SCALING

    def _L0_ffn_ref(x, w_gate, w_up, w_down):
        import jax, jax.numpy as jnp
        import numpy as np
        BLOCK = 32
        W_BITS = 4
        ACT_BITS = 16

        def act_qdq(x):
            qmax = 2.0 ** (ACT_BITS - 1) - 1.0
            scale = jnp.maximum(jnp.max(jnp.abs(x)) / qmax, 1e-12)
            return jnp.clip(jnp.round(x / scale), -qmax - 1.0, qmax) * scale

        def fixed_qdq_u16(x):
            scale = 1.0 / 65536.0
            return jnp.clip(jnp.round(x / scale), 0.0, 65535.0) * scale

        def lpbq_dequant(w):
            O, I = w.shape
            qmax = 2.0 ** (W_BITS - 1) - 1.0
            wb = w.reshape(O, I // BLOCK, BLOCK)
            s = jnp.maximum(jnp.max(jnp.abs(wb), axis=-1, keepdims=True) / qmax, 1e-12)
            wq = jnp.clip(jnp.round(wb / s), -qmax - 1.0, qmax) * s
            return wq.reshape(O, I)
        x = act_qdq(x)
        up = act_qdq(x @ lpbq_dequant(w_up).T)
        gate = act_qdq(x @ lpbq_dequant(w_gate).T)
        sig = fixed_qdq_u16(jax.nn.sigmoid(gate))
        gate = act_qdq(gate * sig)
        o = act_qdq(gate * up)
        return o @ lpbq_dequant(w_down).T

    def _L1_cond_ref(x, y, weight, mask, bias):
        import jax, jax.numpy as jnp
        import numpy as np
        masked_w = weight * mask[None, :, :]
        w_bot = jnp.einsum('bg,got->bot', y, masked_w)
        return jnp.einsum('bnt,bot->bno', x, w_bot) + bias

    def _L1_attn_ref(x, weight_q, weight_k, weight_v, theta):
        import jax, jax.numpy as jnp
        import numpy as np
        GAMMA = 0.96875
        H = 128
        B = 4
        L = 256
        Bb, Ll, Hh = x.shape
        dt = x.dtype
        seq = jnp.arange(1, Ll + 1, dtype=dt)
        zero = jnp.asarray(0.0, dtype=dt)
        thetas = jnp.exp(zero * seq[:, None] * theta[None, :])
        theta_conj = thetas
        q = jnp.matmul(x, weight_q) * thetas[None]
        k = jnp.matmul(x, weight_k) * theta_conj[None]
        v = jnp.matmul(x, weight_v)
        n = jnp.arange(Ll)
        diff = n[:, None] - n[None, :]
        D = jnp.where(diff >= 0, jnp.asarray(GAMMA, dt) ** diff.astype(dt), jnp.zeros((), dt))
        scores = jnp.einsum('bid,bjd->bij', q, k) * D[None]
        return jnp.einsum('bij,bjd->bid', scores, v)

    def _L1_cond2_ref(x, opcode_onehot, W_up, b_up, W_gate, b_gate, W_down, b_down):
        import jax, jax.numpy as jnp
        import numpy as np
        B, S, D = (16, 256, 128)
        E, H = (8, 256)
        expert = jnp.argmax(opcode_onehot, axis=-1)
        wu, bu = (W_up[expert], b_up[expert])
        wg, bg = (W_gate[expert], b_gate[expert])
        wd, bd = (W_down[expert], b_down[expert])
        up = jnp.einsum('bsd,bhd->bsh', x, wu) + bu[:, None, :]
        gate = jnp.einsum('bsd,bhd->bsh', x, wg) + bg[:, None, :]
        hidden = jax.nn.silu(up) * gate
        out = jnp.einsum('bsh,bdh->bsd', hidden, wd) + bd[:, None, :]
        return out

    def _L1_ffn_ref(hidden_states, sim_matrix, gates, q_proj, k_proj, v_proj, o_proj):
        import jax, jax.numpy as jnp
        import numpy as np
        B, T, C, H, E, MIN_E = (4, 256, 128, 128, 16, 2)
        IS_CAUSAL = False

        def _forward(hidden_states, sim_matrix, gates, q_proj, k_proj, v_proj, o_proj):
            b, t, c = hidden_states.shape
            n = b * t
            x = hidden_states.reshape(n, c)
            xn = x / jnp.maximum(jnp.linalg.norm(x, axis=-1, keepdims=True), 1e-12)
            sn = sim_matrix / jnp.maximum(jnp.linalg.norm(sim_matrix, axis=0, keepdims=True), 1e-12)
            logits = xn @ sn - jax.nn.sigmoid(gates)
            gated = jax.nn.relu(logits)
            hard = (gated > 0).astype(gated.dtype)
            mask = gated + jax.lax.stop_gradient(hard - gated)
            inactive = jnp.sum(hard, axis=1) == 0
            _, fb_idx = jax.lax.top_k(logits, MIN_E)
            fb = jnp.zeros((n, logits.shape[1]), gated.dtype).at[jnp.arange(n)[:, None], fb_idx].set(1.0)
            put = jax.lax.stop_gradient(inactive[:, None].astype(gated.dtype) * fb)
            mask = mask * (1.0 - put) + put
            masked = jnp.where(mask > 0, gated, -jnp.inf)
            w = jax.nn.softmax(masked, axis=-1)

            def moe_proj(p):
                y = jnp.einsum('nc,ech->neh', x, p)
                return jnp.einsum('ne,neh->nh', w, y)
            q = moe_proj(q_proj).reshape(b, t, -1)
            k = moe_proj(k_proj).reshape(b, t, -1)
            v = moe_proj(v_proj).reshape(b, t, -1)
            h = q.shape[-1]
            scores = jnp.einsum('bth,bsh->bts', q, k) / jnp.sqrt(jnp.asarray(h, q.dtype))
            if IS_CAUSAL and t > 1:
                causal = jnp.tril(jnp.ones((t, t), bool))
                scores = jnp.where(causal[None], scores, -jnp.inf)
            attn = jax.nn.softmax(scores, axis=-1)
            o = jnp.einsum('bts,bsh->bth', attn, v).reshape(n, h)
            z = jnp.einsum('ne,nh->enh', w, o)
            out = jnp.einsum('enh,ehc->nc', z, o_proj)
            return out.reshape(b, t, c)
        return _forward(hidden_states, sim_matrix, gates, q_proj, k_proj, v_proj, o_proj)
    x = x + _L0_attn_ref(_L0_cond_ref(x, cond_8, L0_cond_skill_gate, L0_cond_skill_up, L0_cond_skill_down, L0_cond_shared_gate, L0_cond_shared_up, L0_cond_shared_down), L0_attn_key_in, L0_attn_value_in, L0_attn_ln_g, L0_attn_ln_b, L0_attn_Wu, L0_attn_bu, L0_attn_Wv, L0_attn_bv, L0_attn_Wb, L0_attn_bb, L0_attn_qqw, L0_attn_qqb, L0_attn_qkw, L0_attn_qkb, L0_attn_lqw, L0_attn_lqb, L0_attn_lkw, L0_attn_lkb, L0_attn_Wo, L0_attn_bo, L0_attn_w_rel)
    x = x + _L0_ffn_ref(_L0_cond2_ref(x, cond_8, L0_cond2_W_base, L0_cond2_b_base, L0_cond2_As, L0_cond2_Bs), L0_ffn_w_gate, L0_ffn_w_up, L0_ffn_w_down)
    x = x + _L1_attn_ref(_L1_cond_ref(x, cond_8, L1_cond_weight, L1_cond_mask, L1_cond_bias), L1_attn_weight_q, L1_attn_weight_k, L1_attn_weight_v, L1_attn_theta)
    x = x + _L1_ffn_ref(_L1_cond2_ref(x, cond_8, L1_cond2_W_up, L1_cond2_b_up, L1_cond2_W_gate, L1_cond2_b_gate, L1_cond2_W_down, L1_cond2_b_down), L1_ffn_sim_matrix, L1_ffn_gates, L1_ffn_q_proj, L1_ffn_k_proj, L1_ffn_v_proj, L1_ffn_o_proj)
    return x

_drawn_inputs = setup_inputs


def setup_inputs(seed=0):
    import zlib

    import numpy as np

    out = dict(_drawn_inputs(seed))
    spreads = {'L0_attn_ln_g': (1.0, 0.2),
     'L0_attn_ln_b': (0.0, 0.1),
     'L0_attn_bu': (0.0, 0.1),
     'L0_attn_bv': (0.0, 0.1),
     'L0_attn_bb': (0.0, 0.1),
     'L0_attn_qqb': (0.0, 0.1),
     'L0_attn_qkb': (0.0, 0.1),
     'L0_attn_lqb': (0.0, 0.1),
     'L0_attn_lkb': (0.0, 0.1),
     'L0_attn_bo': (0.0, 0.1),
     'L1_cond2_b_up': (0.0, 0.1),
     'L1_cond2_b_gate': (0.0, 0.1),
     'L1_cond2_b_down': (0.0, 0.1),
     'L1_ffn_gates': (0.0, 0.1)}
    factors = {}
    for name, (base, spread) in spreads.items():
        noise = np.random.default_rng([zlib.crc32(name.encode()), seed]).standard_normal(out[name].shape)
        drawn = base * np.exp(spread * noise) if base else spread * noise
        out[name] = jnp.asarray(drawn.astype(out[name].dtype))
    for name, factor in factors.items():
        out[name] = (out[name] * factor).astype(out[name].dtype)
    return out
```

```python
from contextlib import ExitStack

import numpy as np

import concourse.bass as bass
from concourse import mybir

F32 = mybir.dt.float32
F16 = mybir.dt.float16
BF16 = mybir.dt.bfloat16
I32 = mybir.dt.int32
ALU = mybir.AluOpType
ACT = mybir.ActivationFunctionType
X_AX = mybir.AxisListType.X

NB, S, D = 16, 128, 128
N = NB * S
I0, E0 = 512, 8
WE = 3 * I0
H2 = 256
CE = 3 * H2
E1 = 16
WS = 256.0
MAGIC = 12582912.0
QMAX = 32767.0
NEG = -3.0e38
ISC = float(1.0 / np.sqrt(np.float32(D)))

COLS = ["ln_g", "ln_b", "bu0", "bu1", "bb", "bbs", "qqw", "qqb", "qkw", "qkb", "qqws", "qqbs", "qkws",
        "qkbs", "bo", "b_base", "cbias", "theta"]
CI = {n: i for i, n in enumerate(COLS)}
PK0 = {"WuT": (0, 256), "WvT": (256, 512), "WbT": (512, 640), "WbsT": (640, 768), "WoT": (768, 1024),
       "As": (1024, 1152), "BsT": (1152, 1280), "WbaseT": (1280, 1408), "relb": (1408, 1536)}
PK1 = {"ident": (0, 128), "decT": (128, 256), "amask": (256, 384), "cos": (384, 400), "sin": (400, 416),
       "condR": (416, 432), "sim": (432, 448), "gates": (448, 464), "iota8": (464, 592), "iota16": (592, 848),
       "kmask": (848, 864)}
PK1N = 864
PK2 = {"WqT": (0, 128), "WkT": (128, 256), "Wv1": (256, 384)}


class Tok:
    def __init__(self, sem, val):
        self.sem, self.val = sem, val


class Queue:

    def __init__(self, new_sem, name):
        self.new_sem, self.name = new_sem, name
        self.todo, self.seen = [], {}
        self.part(0)

    def part(self, n):
        self.sem, self.val = self.new_sem(f"s_{self.name}{n}"), 0

    def op(self, fn, after=(), inc=True):
        for t in after:
            if t is not None and self.seen.get(t.sem, 0) < t.val:
                self.seen[t.sem] = t.val
                self.todo.append(lambda e, t=t: e.wait_ge(t.sem, t.val))
        if not inc:
            self.todo.append(fn)
            return None
        self.val += 1
        sem = self.sem
        self.todo.append(lambda e: fn(e).then_inc(sem, 1))
        return Tok(sem, self.val)

    def run(self, e):
        for f in self.todo:
            f(e)


def program(nc, A, out):
    with ExitStack() as ctx:
        def sb(name, shape, dt=F32):
            return ctx.enter_context(nc.sbuf_tensor(name, shape, dt))

        nsem = [0]

        def sem(name):
            nsem[0] += 1
            return ctx.enter_context(nc.semaphore(f"{name}_{nsem[0]}"))

        pe, act, dve, pool, sp = (Queue(sem, n) for n in ("pe", "act", "dve", "pool", "sp"))

        def part(n):
            for q in (pe, act, dve, pool):
                q.part(n)

        stores = []

        def dma(dst, src, after=(), q=None, store=False):
            q = q or sp
            s = sem("d")
            for t in after:
                q.op(lambda e, t=t: e.wait_ge(t.sem, t.val), inc=False)
            q.op(lambda e: e.dma_start(dst, src).then_inc(s, 16), inc=False)
            t = Tok(s, 16)
            if store:
                stores.append(t)
            return t

        BK = [ctx.enter_context(nc.psum_tensor(f"bk{i}", [128, 512], F32)) for i in range(8)]
        free = [() for _ in range(8)]

        RA = sb("RA", [128, 13824])
        RB = sb("RB", [128, 8192])
        RC = sb("RC", [128, 6144])
        STG = sb("STG", [128, 2, 1536])
        XT = sb("XT", [128, N])
        X16 = sb("X16", [128, 2, N], F16)
        QT = sb("QT", [128, N])
        WK = sb("WK", [128, 2, 2048])
        PK0T = sb("PK0T", [128, 1536])
        PK1T = sb("PK1T", [128, PK1N])
        PK2T = sb("PK2T", [128, 384])
        COL = sb("COL", [128, len(COLS)])
        C2B = sb("C2B", [128, 5, 8])
        BV = sb("BV", [1, 256])
        WEFF = sb("WEFF", [128, N])
        WBOT = sb("WBOT", [128, N])
        FW = RB[:, 6656:7808].rearrange("p (k n) -> p k n", k=9)
        FWT = sb("FWT", [128, 9, 128])
        CONDB = sb("CONDB", [128, 16, 8])
        SM = sb("SM", [128, 40, 16])
        SL = RB[:, 1536:3072].rearrange("p (k n) -> p k n", k=12)
        ROPE = sb("ROPE", [128, 8, 16])
        ONESK = sb("ONESK", [128, 128])
        ONES = sb("ONES", [128, 128])
        ATT = sb("ATT", [128, 3, 128])
        WCOL = sb("WCOL", [128, 2, 16])
        EIX = sb("EIX", [128, 3, 16], I32)
        BSEL = sb("BSEL", [128, 5, 16])
        QS = sb("QS", [128, 64])
        ROW = sb("ROW", [1, 16])

        def pk0(n):
            return PK0T[:, PK0[n][0]:PK0[n][1]]

        def pk1(n):
            return PK1T[:, PK1[n][0]:PK1[n][1]]

        def pk2(n):
            return PK2T[:, PK2[n][0]:PK2[n][1]]

        def col(n):
            return COL[:, CI[n]:CI[n] + 1]

        def cc(c):
            return slice(512 * c, 512 * c + 512)

        def bb_(b):
            return slice(128 * b, 128 * b + 128)

        def big(j):
            return RA[:, 2048 * j:2048 * j + 2048]

        def root(dst, src, tmp, add, least, after):
            v, s = tmp[:, 0, :], tmp[:, 1, :]
            t = dve.op(lambda e: e.tensor_scalar(v, src, add, None, ALU.add), after)
            t = act.op(lambda e: e.activation(s, v, ACT.Sqrt), [t])
            t = dve.op(lambda e: e.tensor_scalar(s, s, least, None, ALU.max), [t])
            t = dve.op(lambda e: e.reciprocal(dst, s), [t])
            t = dve.op(lambda e: e.tensor_tensor(dst, dst, v, ALU.mult), [t])
            t = dve.op(lambda e: e.tensor_tensor(dst, dst, s, ALU.add), [t])
            return dve.op(lambda e: e.tensor_scalar(dst, dst, 0.5, least, ALU.mult, ALU.max), [t])

        d_cond = dma(CONDB[:, :, :], A["condB"], q=act)
        d_pk1 = dma(PK1T[:, :], A["pk1"], q=act)
        d_col = dma(COL[:, :], A["cols"], q=act)
        d_c2b = dma(C2B[:, :, :], A["c2b"], q=act)
        d_bv = dma(BV[:, :], A["bv"], q=act)
        d_x = [dma(XT[:, cc(c)], A["xT"][:, cc(c)]) for c in range(2)]
        d_stg = [None] * 18
        d_stg[0] = dma(STG[:, 0, :], A["w0"][0])
        d_x += [dma(XT[:, cc(c)], A["xT"][:, cc(c)]) for c in range(2, 4)]
        d_stg[1] = dma(STG[:, 1, :], A["w0"][1])
        d_pk0 = dma(PK0T[:, :], A["pk0"])
        d_fw = dma(FW[:, :, :], A["fw"])
        d_pk2 = dma(PK2T[:, :], A["pk2"])
        L1W = WK[:, 0, 0:1024]
        L1M = WK[:, 0, 1024:2048]

        c_ones = dve.op(lambda e: e.memset(ONES[:, :], 1.0))
        c_onesk = dve.op(lambda e: e.memset(ONESK[:, :], 1.0 / 128))

        iota8 = pk1("iota8").rearrange("p (b e) -> p b e", e=8)

        def first_max(q, lg, iota, m, eq, ix, oh, after):
            nb, ne = lg.shape[1], lg.shape[2]
            t = q.op(lambda e: e.tensor_reduce(m, lg, X_AX, ALU.max), after)
            t = q.op(lambda e: e.tensor_tensor(eq, lg, m.unsqueeze(2).to_broadcast([128, nb, ne]), ALU.is_equal), [t])
            t = q.op(lambda e: e.tensor_tensor(eq, eq, iota, ALU.mult), [t])
            t = q.op(lambda e: e.tensor_reduce(ix, eq, X_AX, ALU.min), [t])
            return q.op(lambda e: e.tensor_tensor(oh, iota, ix.unsqueeze(2).to_broadcast([128, nb, ne]), ALU.is_equal), [t])

        def sl8(i):
            return SL[:, i, :].rearrange("p (b e) -> p b e", e=8)

        t = first_max(dve, CONDB[:, :, :], iota8, SM[:, 0, :], sl8(0), SM[:, 1, :], sl8(1), [d_cond, d_pk1])
        oh1_t = t
        t = dve.op(lambda e: e.scalar_tensor_tensor(sl8(2), sl8(1), NEG, CONDB[:, :, :], ALU.mult, ALU.add), [t])
        t = first_max(dve, sl8(2), iota8, SM[:, 2, :], sl8(0), SM[:, 3, :], sl8(3), [t])
        t = dve.op(lambda e: e.tensor_scalar(EIX[:, 0:2, :], SM[:, 1:4:2, :], 99.0, 3072.0, ALU.add, ALU.mult), [t])
        t_eix = dve.op(lambda e: e.tensor_scalar(EIX[:, 2, :], SM[:, 1, :], 99.0, 1536.0, ALU.add, ALU.mult), [t])
        t = dve.op(lambda e: e.tensor_tensor(sl8(4), CONDB[:, :, :], SM[:, 0, :].unsqueeze(2).to_broadcast([128, 16, 8]),
                                             ALU.subtract), [t_eix])
        t2 = dve.op(lambda e: e.tensor_tensor(SM[:, 4, :], SM[:, 2, :], SM[:, 0, :], ALU.subtract), [t])
        t = act.op(lambda e: e.activation(sl8(5), sl8(4), ACT.Exp), [t2])
        t = act.op(lambda e: e.activation(SM[:, 5, :], SM[:, 4, :], ACT.Exp), [t])
        t = dve.op(lambda e: e.tensor_reduce(SM[:, 6, :], sl8(5), X_AX, ALU.add), [t])
        t = dve.op(lambda e: e.reciprocal(SM[:, 7, :], SM[:, 6, :]), [t])
        t = dve.op(lambda e: e.tensor_tensor(SM[:, 8, :], SM[:, 5, :], SM[:, 7, :], ALU.mult), [t])
        t = dve.op(lambda e: e.tensor_tensor(SM[:, 9, :], SM[:, 7, :], SM[:, 8, :], ALU.add), [t])
        t = dve.op(lambda e: e.reciprocal(SM[:, 9, :], SM[:, 9, :]), [t])
        t = dve.op(lambda e: e.tensor_tensor(SM[:, 10:12, :], SM[:, 7:9, :], SM[:, 9, :].unsqueeze(1).to_broadcast([128, 2, 16]),
                                             ALU.mult), [t])
        t = dve.op(lambda e: e.tensor_scalar(SM[:, 12:14, :], SM[:, 10:12, :], 1.0 / 12, None, ALU.mult), [t])
        t = dve.op(lambda e: e.scalar_tensor_tensor(SM[:, 10:12, :], SM[:, 10:12, :], 1.0 - 1.0 / 12, SM[:, 12:14, :],
                                                    ALU.mult, ALU.add), [t])
        t_w = dve.op(lambda e: e.tensor_scalar(WCOL[:, :, :], SM[:, 10:12, :], 1.0 / WS, None, ALU.mult), [t])
        t = t_w
        t_bsel = []
        for k in range(5):
            tk = pool.op(lambda e, k=k: e.tensor_tensor(sl8(6 + k), sl8(1), C2B[:, k, :].unsqueeze(1).to_broadcast([128, 16, 8]),
                                                        ALU.mult), [oh1_t, d_c2b])
            t_bsel.append(dve.op(lambda e, k=k: e.tensor_reduce(BSEL[:, k, :], sl8(6 + k), X_AX, ALU.add), [tk]))
        t_sl = t_bsel[-1]
        t_bsel = dve.op(lambda e: e.tensor_scalar(BSEL[:, 2:4, :], BSEL[:, 2:4, :], WS, None, ALU.mult), [t_bsel[-1]])

        W16 = RA[:, :].bitcast(F16)

        def split_weights(g, dst_hi, dst_lo, n, slot, eng, after=()):
            src = STG[:, slot, 0:n]
            th = act.op(lambda e: e.activation(dst_hi, src, ACT.Copy, scale=WS), [d_stg[g], *after])
            return eng.op(lambda e: e.scalar_tensor_tensor(dst_lo, src, WS, dst_hi, ALU.mult, ALU.subtract), [th])

        x_lo = []
        for c in range(4):
            if c == 1:
                w_ready = [split_weights(0, W16[:, 8 * 3072:8 * 3072 + 1536], W16[:, 8 * 3072 + 1536:9 * 3072], 1536, 0, dve)]
            th = act.op(lambda e, c=c: e.activation(X16[:, 0, cc(c)], XT[:, cc(c)], ACT.Copy), [d_x[c]])
            x_lo.append(dve.op(lambda e, c=c: e.tensor_tensor(X16[:, 1, cc(c)], XT[:, cc(c)], X16[:, 0, cc(c)],
                                                              ALU.subtract), [th]))
        stg_free = [w_ready[0], None]

        def next_expert(e):
            g = e + 1
            w_ready.append(split_weights(g, W16[:, e * 3072:e * 3072 + 1536], W16[:, e * 3072 + 1536:(e + 1) * 3072],
                                         1536, g % 2, dve))
            stg_free[g % 2] = w_ready[-1]
            if g + 1 < 9:
                d_stg[g + 1] = dma(STG[:, (g + 1) % 2, :], A["w0"][g + 1], [stg_free[(g + 1) % 2]])

        units = []
        for g in range(4):
            units.append([("sh", g, j) for j in range(4)])
        order = units[0] + units[1]
        for g in range(4):
            order += [("ex", 4 * g + bi, s) for bi in range(4) for s in range(2)]
            if g + 2 < 4:
                order += units[g + 2]
        ge = [WK[:, 1, 512 * i:512 * i + 512] for i in range(3)]
        hf = [RB[:, 512 * i:512 * i + 512] for i in range(3)]
        H16 = RB[:, 3072:4608].bitcast(F16).rearrange("p (r h n) -> p r h n", r=3, h=2)
        ybank = {}
        up_t, ge_t, st_t, hi_t, lo_t, dn_t = {}, {}, {}, {}, {}, {}
        regs = {}

        def w_ap(kind, v, off, part):
            if kind == "sh":
                o = 8 * 3072 + part * 1536 + off
                return W16[:, o:o + 128]
            return W16[:, bass.ds(v + (part * 1536 + off), 128)]

        def up(k):
            kind, a, j = order[k]
            gb, ub = BK[2 * (k % 3)], BK[2 * (k % 3) + 1]
            waits = [st_t.get(k - 3), *(w_ready[0:1] if kind == "sh" else w_ready), *([x_lo[a]] if kind == "sh" else x_lo)]
            if kind == "ex":
                def load(e, a=a, j=j):
                    regs[(a, j)] = nc.tensor.value_load(EIX[0:1, j, a:a + 1], min_val=0, max_val=7 * 3072)
                pe.op(load, [*waits, t_eix], inc=False)
            for half, bank in ((0, gb), (1, ub)):
                if kind == "sh":
                    tiles = [(j, slice(0, 512), slice(512 * a, 512 * a + 512))]
                else:
                    tiles = [(jj, slice(128 * jj, 128 * jj + 128), bb_(a)) for jj in range(4)]
                for jj, oc, xc in tiles:
                    for n, (wp, xp) in enumerate(((0, 0), (0, 1), (1, 0))):
                        last = half == 1 and n == 2 and oc.stop == 512

                        def mm(e, bank=bank, oc=oc, xc=xc, wp=wp, xp=xp, off=half * 512 + jj * 128, n=n, kind=kind, a=a, j=j):
                            return e.matmul(bank[:, oc], w_ap(kind, regs.get((a, j)), off, wp), X16[:, xp, xc],
                                            start=(n == 0), stop=(n == 2))
                        tk = pe.op(mm, waits, inc=last)
                        waits = ()
            up_t[k] = tk

        def down(k):
            kind, a, j = order[k]
            g = a if kind == "sh" else a // 4
            if kind == "sh" and j == 0:
                ybank[g] = 6 + g % 2
            bk = ybank[g]
            waits = [lo_t[k], *free[bk]]
            if kind == "sh":
                tiles = [(j, slice(0, 512), slice(0, 512))]
            else:
                tiles = [(jj, slice(128 * jj, 128 * jj + 128), bb_(a % 4)) for jj in range(4)]
            for jj, hc, oc in tiles:
                for n, (wp, xp) in enumerate(((0, 0), (0, 1), (1, 0))):
                    first = kind == "sh" and j == 0 and n == 0
                    final = kind == "ex" and a % 4 == 3 and j == 1 and jj == 3 and n == 2
                    last = n == 2 and (kind == "sh" or jj == 3)

                    def mm(e, wp=wp, xp=xp, off=1024 + jj * 128, hc=hc, oc=oc, first=first, final=final, kind=kind, a=a, j=j, bk=bk, k=k):
                        return e.matmul(BK[bk][:, oc], w_ap(kind, regs.get((a, j)), off, wp), H16[:, k % 3, xp, hc],
                                        start=first, stop=final, skip_group_check=True)
                    tk = pe.op(mm, waits, inc=last)
                    waits = ()
            dn_t[k] = tk
            if kind == "ex" and a % 4 == 3 and j == 1:
                tq = act.op(lambda e, g=g, bk=bk: e.activation(QT[:, cc(g)], BK[bk][:, :], ACT.Copy, scale=1.0 / WS), [tk])
                free[bk] = (tq,)
                q_t.append(tq)

        q_t = []
        nu = len(order)
        for k in range(nu + 2):
            if k < nu:
                kind, a, j = order[k]
                r = k % 3
                up(k)
                ge_t[k] = act.op(lambda e, k=k, r=r: e.activation(ge[r], BK[2 * r][:, :], ACT.Gelu_apprx_tanh, scale=1.0 / WS),
                                 [up_t[k], st_t.get(k - 3)])
                w = (1.0 / WS) if kind == "sh" else WCOL[:, j, a:a + 1]
                st_t[k] = dve.op(lambda e, r=r, w=w: e.scalar_tensor_tensor(hf[r], ge[r], w, BK[2 * r + 1][:, :], ALU.mult, ALU.mult),
                                 [ge_t[k], t_w, lo_t.get(k - 3)])
                if k < 8:
                    next_expert(k)
            if 0 <= k - 1 < nu:
                p = k - 1
                r = p % 3
                hi_t[p] = act.op(lambda e, r=r: e.activation(H16[:, r, 0, :], hf[r], ACT.Copy), [st_t[p], dn_t.get(p - 3)])
                lo_t[p] = dve.op(lambda e, r=r: e.tensor_tensor(H16[:, r, 1, :], hf[r], H16[:, r, 0, :], ALU.subtract), [hi_t[p]])
            if 0 <= k - 2 < nu:
                down(k - 2)
        q_all = [q_t[-1]]
        moe_end = [dn_t[nu - 1], q_t[-1]]
        for i in range(6):
            free[i] = (st_t[nu - 1], st_t[nu - 2], st_t[nu - 3])

        part(1)
        g_stg = [9]

        def stage_load(src, n):
            g = g_stg[0]
            d_stg[g] = dma(STG[:, g % 2, 0:n], src, [stg_free[g % 2]])
            g_stg[0] += 1
            return g

        C16 = RC[:, :].bitcast(F16)
        c_ready = []
        for i in range(4):
            g = stage_load(A["w1"][i], 1536)
            hi = C16[:, 3072 * i:3072 * i + 3072].rearrange("p (e h n) -> p e h n", e=2, h=2)
            src = STG[:, g % 2, :].rearrange("p (e n) -> p e n", e=2)
            th = pool.op(lambda e, hi=hi, src=src: e.tensor_scalar(hi[:, :, 0, :], src, WS, None, ALU.mult), [d_stg[g]])
            tl = pool.op(lambda e, hi=hi, src=src: e.tensor_scalar(src, src, WS, None, ALU.mult), [th])
            tl = pool.op(lambda e, hi=hi, src=src: e.tensor_tensor(hi[:, :, 1, :], src, hi[:, :, 0, :], ALU.subtract), [tl])
            stg_free[g % 2] = tl
            c_ready.append(tl)

        condR = pk1("condR")
        BSC = WK[:, 1, :]
        t = dve.op(lambda e: e.scalar_tensor_tensor(BSC.rearrange("p (b o) -> p b o", b=16),
                                                    pk0("BsT").unsqueeze(1).to_broadcast([128, 16, 128]), 2.0,
                                                    condR.unsqueeze(2).to_broadcast([128, 16, 128]), ALU.mult, ALU.mult),
                   [d_pk0, d_pk1, st_t[nu - 1], ge_t[nu - 1]])
        weff_t = []
        for c in range(4):
            tp = pe.op(lambda e, c=c: e.matmul(BK[c][:, :], pk0("As"), BSC[:, cc(c)], start=True, stop=True), [t, *free[c]])
            tv = dve.op(lambda e, c=c: e.tensor_tensor(WEFF[:, cc(c)].rearrange("p (b o) -> p b o", b=4),
                                                       BK[c][:, :].rearrange("p (b o) -> p b o", b=4),
                                                       pk0("WbaseT").unsqueeze(1).to_broadcast([128, 4, 128]), ALU.add), [tp])
            free[c] = (tv,)
            weff_t.append(tv)
        bsc_free = weff_t[-1]

        d_l1 = [dma(L1W, A["l1w"]), dma(L1M, A["l1m"])]
        KR = WK[:, 1, 0:256].rearrange("p (b j) -> p b j", b=16)
        t1 = dve.op(lambda e: e.tensor_tensor(KR, pk1("kmask").unsqueeze(1).to_broadcast([128, 16, 16]),
                                              condR.unsqueeze(2).to_broadcast([128, 16, 16]), ALU.mult), [bsc_free, Tok(weff_t[0].sem, weff_t[0].val)])
        t2 = dve.op(lambda e: e.tensor_tensor(L1W, L1W, L1M, ALU.mult), d_l1)
        wbot_t = []
        for o in range(8):
            bk = BK[4 + o % 4]
            tp = pe.op(lambda e, o=o, bk=bk: e.matmul(bk[:, 0:256], L1W[:, 128 * o:128 * o + 128], WK[:, 1, 0:256], start=True, stop=True),
                       [t1, t2, *free[4 + o % 4]])
            tv = act.op(lambda e, o=o, bk=bk: e.activation(
                WBOT[:, :].rearrange("p (b o j) -> p b o j", b=16, o=8)[:, :, o, :],
                bk[:, 0:256].rearrange("p (b j) -> p b j", b=16), ACT.Copy), [tp])
            free[4 + o % 4] = (tv,)
            wbot_t.append(tv)

        t = dve.op(lambda e: e.tensor_scalar(QS[:, 0:1], col("theta"), 0.0, None, ALU.mult), [d_col])
        t = act.op(lambda e: e.activation(QS[:, 1:2], QS[:, 0:1], ACT.Exp), [t])
        t = dve.op(lambda e: e.tensor_scalar(ATT[:, 1, :], pk2("WkT"), QS[:, 1:2], QS[:, 1:2], ALU.mult, ALU.mult), [t, d_pk2])
        tp = pe.op(lambda e: e.matmul(BK[0][:, 0:128], pk2("WqT"), ATT[:, 1, :], start=True, stop=True), [t, *free[0]])
        a_t = act.op(lambda e: e.activation(ATT[:, 2, :], BK[0][:, 0:128], ACT.Copy), [tp])
        free[0] = (a_t,)

        fw_t = []
        FB = QS[:, 16:52]
        t = dve.op(lambda e: e.tensor_reduce(FB, FW[:, :, :].rearrange("p t (k i) -> p (t k) i", i=32), X_AX, ALU.max,
                                             apply_absolute_value=True), [d_fw])
        FR = SM[:, 36:39, :].rearrange("p a b -> p (a b)")[:, 0:36]
        t = dve.op(lambda e: e.tensor_scalar(FB, FB, 1.0 / 7.0, 1e-12, ALU.mult, ALU.max), [t])
        t = dve.op(lambda e: e.reciprocal(FR, FB), [t])
        fw3 = FW[:, :, :].rearrange("p t (k i) -> p (t k) i", i=32)
        fbb = FB.unsqueeze(2).to_broadcast([128, 36, 32])
        t = dve.op(lambda e: e.tensor_tensor(fw3, fw3, FR.unsqueeze(2).to_broadcast([128, 36, 32]), ALU.mult), [t])
        t = dve.op(lambda e: e.tensor_scalar(fw3, fw3, MAGIC, MAGIC, ALU.add, ALU.subtract), [t])
        t = dve.op(lambda e: e.tensor_scalar(fw3, fw3, -8.0, 7.0, ALU.max, ALU.min), [t])
        t = dve.op(lambda e: e.tensor_tensor(fw3, fw3, fbb, ALU.mult), [t])
        for i in range(3):
            for k in range(3):
                tp = pe.op(lambda e, i=i, k=k: e.transpose(BK[1 + i][:, 128 * k:128 * k + 128], FW[:, 3 * i + k, :], pk1("ident")),
                           [t, d_pk1, *free[1 + i]], inc=(k == 2))
            tv = act.op(lambda e, i=i: e.activation(FWT[:, 3 * i:3 * i + 3, :], BK[1 + i][:, 0:384].rearrange("p (k n) -> p k n", k=3),
                                                    ACT.Copy), [tp])
            free[1 + i] = (tv,)
            fw_t.append(tv)

        rp = ROPE
        cosT, sinT = pk1("cos"), pk1("sin")
        rope_t = []
        for i, q in enumerate(("qq", "qk")):
            o = 4 * i
            pool.op(lambda e, q=q, o=o: e.tensor_scalar(rp[:, o, :], cosT, col(q + "w"), None, ALU.mult), [d_pk1, d_col])
            pool.op(lambda e, q=q, o=o: e.tensor_scalar(rp[:, o + 1, :], sinT, col(q + "ws"), None, ALU.mult))
            ta = pool.op(lambda e, q=q, o=o: e.tensor_scalar(rp[:, o + 2, :], cosT, col(q + "b"), None, ALU.mult))
            tb = pool.op(lambda e, q=q, o=o: e.tensor_scalar(rp[:, o + 3, :], sinT, col(q + "bs"), None, ALU.mult))
            rope_t.append(pool.op(lambda e, o=o: e.tensor_tensor(rp[:, o + 2, :], rp[:, o + 2, :], rp[:, o + 3, :], ALU.add), [tb]))
        relm_t = pool.op(lambda e: e.tensor_tensor(ATT[:, 0, :], pk0("relb"), pk1("amask"), ALU.add), [d_pk0, d_pk1])

        SNR = SM[:, 20, :]
        SNT = SM[:, 21, :]
        SIG = SM[:, 22, :]
        t = dve.op(lambda e: e.tensor_tensor(SNR, pk1("sim"), pk1("sim"), ALU.mult), [d_pk1])
        tp = pe.op(lambda e: e.matmul(BK[0][:, 0:16], ONES[:, :], SNR, start=True, stop=True), [t, c_ones, *free[0]])
        t = root(SNR, BK[0][:, 0:16], SM[:, 34:36, :], 0.0, 1e-12, [tp])
        free[0] = (t,)
        t = dve.op(lambda e: e.reciprocal(SNR, SNR), [t])
        sn_t = dve.op(lambda e: e.tensor_tensor(SNT, pk1("sim"), SNR, ALU.mult), [t])
        sg_t = act.op(lambda e: e.activation(SIG, pk1("gates"), ACT.Sigmoid), [d_pk1])

        part(2)
        dT, U0, U1, BASE, BSW, QQ = (big(j) for j in range(6))
        XF = X16[:, :, :].rearrange("p a n -> p (a n)").bitcast(F32)
        QK = XF
        VT = WK[:, :, :].rearrange("p a n -> p (a n)").rearrange("p (t f) -> p t f", t=16)
        U = [U0, U1]
        xn_t, pj_t = [], []
        xq_t = []
        for c in range(4):
            xq_t.append(pool.op(lambda e, c=c: e.tensor_tensor(XT[:, cc(c)], XT[:, cc(c)], QT[:, cc(c)], ALU.add), [*q_all, *x_lo]))
        for c in range(4):
            m = c % 2
            tp = pe.op(lambda e, c=c, m=m: e.matmul(BK[m][:, :], ONESK[:, :], QT[:, cc(c)], start=True, stop=True),
                       [*q_all, c_onesk, *free[m]])
            td = dve.op(lambda e, c=c, m=m: e.tensor_tensor(dT[:, cc(c)], QT[:, cc(c)], BK[m][:, :], ALU.subtract), [tp, *moe_end])
            free[m] = (td,)
            ts = act.op(lambda e, c=c: e.activation(BASE[:, cc(c)], dT[:, cc(c)], ACT.Square), [td])
            for i in range(4):
                t_ = 4 * c + i
                tp = pe.op(lambda e, t_=t_: e.matmul(BK[7][:, t_:t_ + 1], BASE[:, bb_(t_)], ONESK[:, 0:1], start=True, stop=True), [ts, *free[7]])
        LNS = SM[:, 14, :]
        t = root(LNS, BK[7][:, 0:16], SM[:, 15:17, :], 1e-5, 0.0, [tp])
        free[7] = (t,)
        t = dve.op(lambda e: e.reciprocal(LNS, LNS), [t])
        t = dve.op(lambda e: e.tensor_tensor(BSW.rearrange("p (t n) -> p t n", t=16), pk1("ident").unsqueeze(1).to_broadcast([128, 16, 128]),
                                             LNS.unsqueeze(2).to_broadcast([128, 16, 128]), ALU.mult), [t])
        for c in range(4):
            tp = pe.op(lambda e, c=c: e.matmul(BK[4 + c % 2][:, :], ONES[:, :], BSW[:, cc(c)], start=True, stop=True), [t, *free[4 + c % 2]])
            tx = dve.op(lambda e, c=c: e.scalar_tensor_tensor(dT[:, cc(c)], dT[:, cc(c)], col("ln_g"), BK[4 + c % 2][:, :], ALU.mult, ALU.mult), [tp, ts])
            free[4 + c % 2] = (tx,)
            xn_t.append(act.op(lambda e, c=c: e.activation(dT[:, cc(c)], dT[:, cc(c)], ACT.Identity, bias=col("ln_b")), [tx]))
        base_t = []
        for c in range(4):
            for i, (w, b, dst) in enumerate(((pk0("WbT"), "bb", BASE), (pk0("WbsT"), "bbs", BSW),
                                             (pk0("WuT")[:, 0:128], "bu0", U0), (pk0("WuT")[:, 128:256], "bu1", U1))):
                bk = 4 + i
                tp = pe.op(lambda e, c=c, w=w, bk=bk: e.matmul(BK[bk][:, :], w, dT[:, cc(c)], start=True, stop=True), [xn_t[c], *free[bk]])
                tv = act.op(lambda e, c=c, b=b, dst=dst, bk=bk: e.activation(dst[:, cc(c)], BK[bk][:, :], ACT.Silu, bias=col(b)), [tp])
                free[bk] = (tv,)
                if i == 1:
                    base_t.append(tv)
        u_t = tv
        xnv = dT.rearrange("p (m t) -> p t m", t=16)
        v_t = []
        for t2_ in range(8):
            bk = t2_ % 4
            for h in range(2):
                t_ = 2 * t2_ + h
                pe.op(lambda e, t_=t_, bk=bk, h=h: e.matmul(BK[bk][:, 256 * h:256 * h + 256], xnv[:, t_, :], pk0("WvT"), start=True, stop=False),
                      [*xn_t, *free[bk]], inc=False)
                tp = pe.op(lambda e, bk=bk, h=h: e.matmul(BK[bk][:, 256 * h:256 * h + 256], ONES[0:1, :], BV[:, :], start=False, stop=True),
                           [d_bv], inc=(h == 1))
            tv = act.op(lambda e, t2_=t2_, bk=bk: e.activation(VT[:, 2 * t2_:2 * t2_ + 2, :], BK[bk][:, :].rearrange("p (t f) -> p t f", t=2), ACT.Silu),
                        [tp, wbot_t[-1]])
            free[bk] = (tv,)
            v_t.append(tv)
        quad_t = []
        for c in range(4):
            def bc(i, c=c):
                return rp[:, i, 4 * c:4 * c + 4].unsqueeze(2).to_broadcast([128, 4, 128])

            def v3(ap, c=c):
                return ap[:, cc(c)].rearrange("p (l b) -> p l b", l=4)
            for o, dst in ((0, QQ), (4, QK)):
                ta = dve.op(lambda e, o=o, dst=dst, v3=v3, bc=bc: e.tensor_tensor(v3(dst), v3(BASE), bc(o), ALU.mult), [base_t[c], rope_t[1], *moe_end])
                tmp = RB[:, 4608 + 512 * c:5120 + 512 * c].rearrange("p (l b) -> p l b", l=4)
                tb = pool.op(lambda e, o=o, tmp=tmp, v3=v3, bc=bc: e.tensor_tensor(tmp, v3(BSW), bc(o + 1), ALU.mult),
                             [base_t[c], quad_t[-1] if quad_t else None, lo_t[nu - 1]])
                tb = pool.op(lambda e, o=o, tmp=tmp, bc=bc: e.tensor_tensor(tmp, tmp, bc(o + 2), ALU.add), [tb])
                quad_t.append(dve.op(lambda e, dst=dst, tmp=tmp, v3=v3: e.tensor_tensor(v3(dst), v3(dst), tmp, ALU.add), [ta, tb]))
        qqv = QQ.rearrange("p (m t) -> p t m", t=16)
        qkv = QK.rearrange("p (m t) -> p t m", t=16)
        KT = BASE.rearrange("p (t n) -> p t n", t=16)
        k_t = []
        for c in range(4):
            for i in range(4):
                t_ = 4 * c + i
                tp = pe.op(lambda e, t_=t_, i=i, c=c: e.matmul(BK[c % 2][:, bb_(i)], qkv[:, t_, :], qqv[:, t_, :], start=True, stop=True),
                           [quad_t[-1], quad_t[-2], *free[c % 2]], inc=(i == 3))
            ta = dve.op(lambda e, c=c: e.scalar_tensor_tensor(KT[:, 4 * c:4 * c + 4, :], BK[c % 2][:, :].rearrange("p (t n) -> p t n", t=4),
                                                              1.0 / 64, ATT[:, 0, :].unsqueeze(1).to_broadcast([128, 4, 128]), ALU.mult, ALU.add),
                        [tp, relm_t, quad_t[-1]])
            free[c % 2] = (ta,)
            k_t.append(dve.op(lambda e, c=c: e.scalar_tensor_tensor(KT[:, 4 * c:4 * c + 4, :], KT[:, 4 * c:4 * c + 4, :], 0.0,
                                                                    KT[:, 4 * c:4 * c + 4, :], ALU.max, ALU.mult), [ta]))
        g_t = []
        for c in range(4):
            for ch in range(2):
                bk = 2 + 2 * (c % 2) + ch
                for i in range(4):
                    t_ = 4 * c + i
                    tp = pe.op(lambda e, t_=t_, i=i, ch=ch, bk=bk: e.matmul(BK[bk][:, bb_(i)], VT[:, t_, 128 * ch:128 * ch + 128], KT[:, t_, :],
                                                                           start=True, stop=True), [k_t[c], v_t[-1], *free[bk]], inc=(i == 3))
                uv = U[ch].rearrange("p (m t) -> p t m", t=16)[:, 4 * c:4 * c + 4, :]
                tg = dve.op(lambda e, uv=uv, bk=bk: e.tensor_tensor(uv, uv, BK[bk][:, :].rearrange("p (t m) -> p t m", t=4), ALU.mult), [tp, u_t])
                free[bk] = (tg,)
                g_t.append(tg)
        x1_t = []
        for c in range(4):
            bk = 6 + c % 2
            for ch in range(2):
                tp = pe.op(lambda e, c=c, ch=ch, bk=bk: e.matmul(BK[bk][:, :], pk0("WoT")[:, 128 * ch:128 * ch + 128], U[ch][:, cc(c)],
                                                                 start=(ch == 0), stop=(ch == 1)), [g_t[-1], *free[bk]], inc=(ch == 1))
            tv = dve.op(lambda e, c=c, bk=bk: e.scalar_tensor_tensor(XT[:, cc(c)], BK[bk][:, :], col("bo"), XT[:, cc(c)], ALU.add, ALU.add),
                        [tp, xq_t[c]])
            free[bk] = (tv,)
            x1_t.append(tv)

        rb_free = [quad_t[-1], fw_t[-1], dn_t[nu - 1], t_sl]
        P16 = RB[:, :].bitcast(F16).rearrange("p (h n) -> p h n", h=2)
        p_ready = []
        for i in range(8):
            g = len(d_stg)
            d_stg.append(dma(STG[:, g % 2, 0:1024], A["w2"][:, 1024 * i:1024 * i + 1024], [stg_free[g % 2]]))
            src = STG[:, g % 2, 0:1024]
            hi, lo = P16[:, 0, 1024 * i:1024 * i + 1024], P16[:, 1, 1024 * i:1024 * i + 1024]
            th = pool.op(lambda e, hi=hi, src=src: e.tensor_copy(hi, src), [d_stg[g], *rb_free])
            tl = pool.op(lambda e, hi=hi, lo=lo, src=src: e.tensor_tensor(lo, src, hi, ALU.subtract), [th])
            stg_free[g % 2] = tl
            p_ready.append(tl)

        part(3)
        LT = XF
        MX = QS
        RQ = sb("RQ", [128, 4])

        def batch_mm(W, src, evac, waits, banks):
            toks = []
            for c in range(4):
                bk = banks[c % len(banks)]
                for i in range(4):
                    b = 4 * c + i
                    tp = pe.op(lambda e, b=b, i=i, bk=bk: e.matmul(BK[bk][:, bb_(i)], W[:, bb_(b)], src[:, bb_(b)], start=True, stop=True),
                               [*waits[c], *free[bk]], inc=(i == 3))
                tv = evac(c, BK[bk], tp)
                free[bk] = (tv,)
                toks.append(tv)
            return toks

        def lora_evac(c, bk, tp):
            return act.op(lambda e: e.activation(LT[:, cc(c)], bk[:, :], ACT.Identity, bias=col("b_base")), [tp, k_t[-1]])

        l_t = batch_mm(WEFF, XT, lora_evac, [[x1_t[c], weff_t[-1], k_t[-1]] for c in range(4)], [0, 1, 2, 3])

        def absmax(dst, src, after):
            return dve.op(lambda e: e.tensor_reduce(dst, src, X_AX, ALU.max, apply_absolute_value=True), after)

        def quant_scale(parts, k, after):
            b0 = k - 60
            t = dve.op(lambda e: e.tensor_reduce(QS[:, 56 + b0:57 + b0], parts, X_AX, ALU.max), after)
            tp = pe.op(lambda e: e.transpose(BK[7][0:1, 0:128], QS[:, 56 + b0:57 + b0], pk1("ident")), [t, *free[7]])
            t = dve.op(lambda e: e.tensor_reduce(ROW[:, b0:b0 + 1], BK[7][0:1, 0:128], X_AX, ALU.max), [tp])
            tp = pe.op(lambda e: e.matmul(BK[7][:, 128:129], ONES[0:1, :], ROW[:, b0:b0 + 1], start=True, stop=True), [t])
            t = dve.op(lambda e: e.tensor_scalar(QS[:, k:k + 1], BK[7][:, 128:129], 1.0 / QMAX, 1e-12, ALU.mult, ALU.max), [tp])
            free[7] = (t,)
            return dve.op(lambda e: e.reciprocal(RQ[:, b0:b0 + 1], QS[:, k:k + 1]), [t])

        def qdq(ap, k, after):
            t = dve.op(lambda e: e.tensor_scalar(ap, ap, RQ[:, k - 60:k - 59], MAGIC, ALU.mult, ALU.add), after)
            return dve.op(lambda e: e.tensor_scalar(ap, ap, MAGIC, QS[:, k:k + 1], ALU.subtract, ALU.mult), [t])

        mx = [absmax(MX[:, c:c + 1], LT[:, cc(c)], [l_t[c], fw_t[-1]]) for c in range(4)]
        s = quant_scale(MX[:, 0:4], 60, mx)
        lq_t = [qdq(LT[:, cc(c)], 60, [s]) for c in range(4)]
        UP = [big(j) for j in range(3)]
        GT = [big(j) for j in range(3, 6)]

        def project(dst, wi, mx0):
            toks = []
            for j in range(3):
                for c in range(4):
                    bk = (4 * j + c) % 7
                    tp = pe.op(lambda e, j=j, c=c, bk=bk: e.matmul(BK[bk][:, :], FWT[:, 3 * wi + j, :], LT[:, cc(c)], start=True, stop=True),
                               [lq_t[c], fw_t[wi], *free[bk]])
                    tv = act.op(lambda e, j=j, c=c, bk=bk: e.activation(dst[j][:, cc(c)], BK[bk][:, :], ACT.Copy), [tp, x1_t[-1]])
                    free[bk] = (tv,)
                    toks.append(absmax(MX[:, mx0 + 4 * j + c:mx0 + 4 * j + c + 1], dst[j][:, cc(c)], [tv]))
            return toks

        um = project(UP, 0, 0)
        gm = project(GT, 1, 12)
        s = quant_scale(MX[:, 12:24], 61, [gm[-1]])
        gq = [qdq(GT[j], 61, [s]) for j in range(3)]
        TS = [WK[:, 0, :], WK[:, 1, :], QT[:, :]]
        sg = [act.op(lambda e, j=j: e.activation(TS[j], GT[j], ACT.Sigmoid), [gq[j]]) for j in range(3)]
        s_up = quant_scale(MX[:, 0:12], 62, [um[-1]])
        uq = [qdq(UP[0], 62, [s_up])]
        g2m = []
        for j in range(3):
            t = dve.op(lambda e, j=j: e.tensor_scalar(TS[j], TS[j], 65536.0, MAGIC, ALU.mult, ALU.add), [sg[j]])
            t = dve.op(lambda e, j=j: e.tensor_scalar(TS[j], TS[j], MAGIC, 65535.0, ALU.subtract, ALU.min), [t])
            t = dve.op(lambda e, j=j: e.scalar_tensor_tensor(GT[j], TS[j], 1.0 / 65536, GT[j], ALU.mult, ALU.mult), [t])
            g2m.append(absmax(MX[:, 24 + j:25 + j], GT[j], [t]))
        s = quant_scale(MX[:, 24:27], 63, [g2m[-1]])
        uq += [qdq(UP[j], 62, [s_up]) for j in (1, 2)]
        om = []
        for j in range(3):
            t = qdq(GT[j], 63, [s])
            t = dve.op(lambda e, j=j: e.tensor_tensor(GT[j], GT[j], UP[j], ALU.mult), [t, uq[j]])
            om.append(absmax(MX[:, 27 + j:28 + j], GT[j], [t]))
        s = quant_scale(MX[:, 27:30], 60, [om[-1], lq_t[-1]])
        oq = [qdq(GT[j], 60, [s]) for j in range(3)]
        x2_t = []
        for c in range(4):
            for j in range(3):
                tp = pe.op(lambda e, c=c, j=j: e.matmul(BK[c][:, :], FWT[:, 6 + j, :], GT[j][:, cc(c)], start=(j == 0), stop=(j == 2)),
                           [oq[j], fw_t[2], *free[c]], inc=(j == 2))
            tv = dve.op(lambda e, c=c: e.tensor_tensor(XT[:, cc(c)], XT[:, cc(c)], BK[c][:, :], ALU.add), [tp])
            free[c] = (tv,)
            x2_t.append(tv)

        part(4)
        X3, ZT, PT, VV = big(0), big(1), big(2), big(3)

        def mix_evac(c, bk, tp):
            return act.op(lambda e: e.activation(X3[:, cc(c)], bk[:, :], ACT.Identity, bias=col("cbias")), [tp, x2_t[-1]])

        x3_t = batch_mm(WBOT, XT, mix_evac, [[x2_t[c], wbot_t[-1]] for c in range(4)], [4, 5])
        x4_t = []
        for c in range(4):
            tp = pe.op(lambda e, c=c: e.matmul(BK[0][:, :], ATT[:, 2, :], X3[:, cc(c)], start=True, stop=True), [x3_t[c], a_t, *free[0]])
            z_t = act.op(lambda e, c=c: e.activation(ZT[:, cc(c)], BK[0][:, :], ACT.Copy), [tp])
            free[0] = (z_t,)
            for i in range(4):
                tp = pe.op(lambda e, c=c, i=i: e.matmul(BK[1][:, bb_(i)], X3[:, bb_(4 * c + i)], pk2("Wv1"), start=True, stop=True), [*free[1]], inc=(i == 3))
            vv = act.op(lambda e, c=c: e.activation(VV[:, cc(c)], BK[1][:, :], ACT.Copy), [tp])
            free[1] = (vv,)
            for i in range(4):
                tp = pe.op(lambda e, c=c, i=i: e.matmul(BK[2][:, bb_(i)], X3[:, bb_(4 * c + i)], ZT[:, bb_(4 * c + i)], start=True, stop=True),
                           [z_t, *free[2]], inc=(i == 3))
            tpp = dve.op(lambda e, c=c: e.tensor_tensor(PT[:, cc(c)].rearrange("p (b n) -> p b n", b=4), BK[2][:, :].rearrange("p (b n) -> p b n", b=4),
                                                        pk1("decT").unsqueeze(1).to_broadcast([128, 4, 128]), ALU.mult), [tp])
            free[2] = (tpp,)
            for i in range(4):
                tp = pe.op(lambda e, c=c, i=i: e.matmul(BK[3][:, bb_(i)], VV[:, bb_(4 * c + i)], PT[:, bb_(4 * c + i)], start=True, stop=True),
                           [vv, tpp, *free[3]], inc=(i == 3))
            tv = dve.op(lambda e, c=c: e.tensor_tensor(XT[:, cc(c)], XT[:, cc(c)], BK[3][:, :], ALU.add), [tp])
            free[3] = (tv,)
            x4_t.append(tv)

        part(5)
        xs = []
        for c in range(4):
            th = act.op(lambda e, c=c: e.activation(X16[:, 0, cc(c)], XT[:, cc(c)], ACT.Copy), [x4_t[c], *lq_t])
            xs.append(dve.op(lambda e, c=c: e.tensor_tensor(X16[:, 1, cc(c)], XT[:, cc(c)], X16[:, 0, cc(c)], ALU.subtract), [th]))
        X5 = big(4)
        SU = [WK[:, 0, 256 * i:256 * i + 256] for i in range(3)]
        HG = [WK[:, 1, 256 * i:256 * i + 256] for i in range(3)]
        H16B = big(5)[:, 0:768].bitcast(F16).rearrange("p (r h n) -> p r h n", r=3, h=2)
        eg, hid, hlo, dn2, x5_t = {}, {}, {}, {}, []
        r2 = {}

        def c_ap(b, part_, off):
            return C16[:, bass.ds(r2[b] + (part_ * 768 + off), 128)]

        def mlp_up(b):
            bk = b % 3
            def load(e, b=b):
                r2[b] = nc.tensor.value_load(EIX[0:1, 2, b:b + 1], min_val=0, max_val=7 * 1536)
            pe.op(load, [*c_ready, xs[b // 4], *free[bk]], inc=False)
            for q in range(4):
                for n, (wp, xp) in enumerate(((0, 0), (0, 1), (1, 0))):
                    tp = pe.op(lambda e, b=b, q=q, n=n, wp=wp, xp=xp, bk=bk: e.matmul(
                        BK[bk][:, bb_(q)], c_ap(b, wp, 128 * q), X16[:, xp, bb_(b)], start=(n == 0), stop=(n == 2)), inc=(q == 3 and n == 2))
            for q in range(2):
                ts = act.op(lambda e, b=b, q=q, bk=bk: e.activation(SU[b % 3][:, bb_(q)], BK[bk][:, bb_(q)], ACT.Silu, bias=BSEL[:, q, b:b + 1],
                                                                    scale=1.0 / WS), [tp, t_bsel, hid.get(b - 3), oq[-1]])
            for q in range(2):
                th = dve.op(lambda e, b=b, q=q, bk=bk: e.scalar_tensor_tensor(HG[b % 3][:, bb_(q)], BK[bk][:, bb_(2 + q)], BSEL[:, 2 + q, b:b + 1],
                                                                             SU[b % 3][:, bb_(q)], ALU.add, ALU.mult), [ts, hlo.get(b - 3)])
            hid[b] = th
            free[bk] = (th,)

        def mlp_mid(b):
            h16 = H16B[:, b % 3, :, :]
            th = act.op(lambda e, b=b, h16=h16: e.activation(h16[:, 0, :], HG[b % 3], ACT.Copy, scale=1.0 / WS), [hid[b], dn2.get(b - 3)])
            hlo[b] = dve.op(lambda e, b=b, h16=h16: e.scalar_tensor_tensor(h16[:, 1, :], HG[b % 3], 1.0 / WS, h16[:, 0, :], ALU.mult, ALU.subtract), [th])

        def mlp_down(b):
            h16 = H16B[:, b % 3, :, :]
            bk = 4 + (b // 4) % 2
            waits = [hlo[b], *(free[bk] if b % 4 == 0 else ())]
            for q in range(2):
                for n, (wp, xp) in enumerate(((0, 0), (0, 1), (1, 0))):
                    tp = pe.op(lambda e, b=b, q=q, n=n, wp=wp, xp=xp, bk=bk, h16=h16: e.matmul(
                        BK[bk][:, bb_(b % 4)], c_ap(b, wp, 512 + 128 * q), h16[:, xp, bb_(q)], start=(q == 0 and n == 0), stop=(q == 1 and n == 2)),
                        waits, inc=(q == 1 and n == 2))
                    waits = ()
            dn2[b] = tp
            if b % 4 == 3:
                for i in range(4):
                    bb2 = b - 3 + i
                    tv = act.op(lambda e, bb2=bb2, i=i, bk=bk: e.activation(X5[:, bb_(bb2)], BK[bk][:, bb_(i)], ACT.Identity,
                                                                            bias=BSEL[:, 4, bb2:bb2 + 1], scale=1.0 / WS), [tp])
                free[bk] = (tv,)
                x5_t.append(tv)

        for b in range(18):
            if b < 16:
                mlp_up(b)
            if 0 <= b - 1 < 16:
                mlp_mid(b - 1)
            if 0 <= b - 2:
                mlp_down(b - 2)

        part(6)
        XSQ = big(0)
        RT = WK[:, :, :].rearrange("p a n -> p (a n)")

        def r16(i):
            return RT[:, 256 * i:256 * i + 256].rearrange("p (t e) -> p t e", e=16)
        for c in range(4):
            tq = act.op(lambda e, c=c: e.activation(XSQ[:, cc(c)], X5[:, cc(c)], ACT.Square), [x5_t[c]])
        for t_ in range(16):
            pe.op(lambda e, t_=t_: e.matmul(BK[0][:, 16 * t_:16 * t_ + 16], X5[:, bb_(t_)], SNT, start=True, stop=True), [x5_t[t_ // 4], sn_t, *free[0]], inc=False)
            tp = pe.op(lambda e, t_=t_: e.matmul(BK[1][:, t_:t_ + 1], XSQ[:, bb_(t_)], ONES[:, 0:1], start=True, stop=True), [tq, *free[1]])
        NR = SM[:, 23, :]
        iota16 = pk1("iota16").rearrange("p (t e) -> p t e", e=16)

        def b16(ap):
            return ap.unsqueeze(2).to_broadcast([128, 16, 16])
        t = root(NR, BK[1][:, 0:16], SM[:, 34:36, :], 0.0, 1e-12, [tp])
        free[1] = (t,)
        t = dve.op(lambda e: e.reciprocal(NR, NR), [t])
        L, EQ, O1, L2, O2, HD, GA = (r16(i) for i in range(7))
        t = dve.op(lambda e: e.tensor_tensor(L, BK[0][:, 0:256].rearrange("p (t e) -> p t e", e=16), b16(NR), ALU.mult), [t, dn2[15], hlo[15]])
        free[0] = (t,)
        t = dve.op(lambda e: e.tensor_tensor(L, L, SIG.unsqueeze(1).to_broadcast([128, 16, 16]), ALU.subtract), [t, sg_t])
        M1, J1, M2, J2, RM, IN, SU1 = (SM[:, 24 + i, :] for i in range(7))
        t = first_max(dve, L, iota16, M1, EQ, J1, O1, [t])
        t = dve.op(lambda e: e.scalar_tensor_tensor(L2, O1, NEG, L, ALU.mult, ALU.add), [t])
        t = first_max(dve, L2, iota16, M2, EQ, J2, O2, [t])
        t = dve.op(lambda e: e.tensor_scalar(IN, M1, 0.0, None, ALU.is_le), [t])
        t = dve.op(lambda e: e.tensor_scalar(RM, M1, 0.0, None, ALU.max), [t])
        t = dve.op(lambda e: e.tensor_scalar(HD, L, 0.0, None, ALU.is_gt), [t])
        t = dve.op(lambda e: e.tensor_tensor(O1, O1, O2, ALU.add), [t])
        t = dve.op(lambda e: e.tensor_tensor(O1, O1, b16(IN), ALU.mult), [t])
        t = dve.op(lambda e: e.tensor_tensor(HD, HD, O1, ALU.add), [t])
        t = dve.op(lambda e: e.scalar_tensor_tensor(GA, L, 0.0, b16(RM), ALU.max, ALU.subtract), [t])
        t = act.op(lambda e: e.activation(GA, GA, ACT.Exp), [t])
        t = dve.op(lambda e: e.tensor_tensor(GA, GA, HD, ALU.mult), [t])
        t = dve.op(lambda e: e.tensor_reduce(SU1, GA, X_AX, ALU.add), [t])
        t = dve.op(lambda e: e.reciprocal(SU1, SU1), [t])
        t = dve.op(lambda e: e.tensor_tensor(GA, GA, b16(SU1), ALU.mult), [t])
        W48 = sb("W48", [128, 16, 48], BF16)
        t = dve.op(lambda e: e.tensor_copy(W48[:, :, 0:16], GA), [t])
        t = dve.op(lambda e: e.tensor_tensor(GA, GA, W48[:, :, 0:16], ALU.subtract), [t])
        t = dve.op(lambda e: e.tensor_copy(W48[:, :, 16:32], GA), [t])
        t = dve.op(lambda e: e.tensor_tensor(GA, GA, W48[:, :, 16:32], ALU.subtract), [t])
        t = dve.op(lambda e: e.tensor_copy(W48[:, :, 32:48], GA), [t])
        IDB = sb("IDB", [128, 128], BF16)
        tid = act.op(lambda e: e.activation(IDB[:, :], pk1("ident"), ACT.Copy), [d_pk1])
        W48T = QT[0:48, 0:1024].bitcast(BF16)
        SEL = QT[0:48, 1024:2048].bitcast(F16).rearrange("p (e n) -> p e n", e=16)
        d_sel = dma(SEL, A["sel"], [x2_t[-1]])
        w48_t = []
        for c in range(4):
            bv_ = BK[2 + c][:, :].bitcast(BF16)
            for i in range(4):
                tp = pe.op(lambda e, c=c, i=i, bv_=bv_: e.transpose(bv_[0:48, bb_(i)], W48[:, 4 * c + i, :], IDB[:, :]), [t, tid, *free[2 + c]], inc=(i == 3))
            tv = act.op(lambda e, c=c, bv_=bv_: e.activation(W48T[:, cc(c)], bv_[0:48, 0:512], ACT.Copy), [tp])
            free[2 + c] = (tv,)
            w48_t.append(tv)

        part(7)
        QP, KP, VP = big(0), big(1), big(2)
        OT = big(3)
        ZB = big(5)
        zf = [ZB[:, 512 * i:512 * i + 512] for i in range(4)]
        ZH = X16[:, :, :].rearrange("p a (r n) -> p r a n", n=512)
        zf_free, zh_free = [None] * 4, [None] * 4
        step = [0]

        def scaled(e1, c, src, after):
            k = step[0]
            step[0] += 1
            r, wb = k % 4, 6 + k % 2
            tp = pe.op(lambda e: e.matmul(BK[wb][:, :], SEL[:, e1, :], W48T[:, cc(c)], start=True, stop=True), [d_sel, w48_t[c], *free[wb]])
            tz = dve.op(lambda e: e.tensor_tensor(zf[r], src[:, cc(c)], BK[wb][:, :], ALU.mult), [tp, zf_free[r], *after])
            free[wb] = (tz,)
            th = act.op(lambda e: e.activation(ZH[:, r, 0, :], zf[r], ACT.Copy), [tz, zh_free[r]])
            return r, tz, th

        def scaled_lo(st):
            r, tz, th = st
            tl = dve.op(lambda e: e.tensor_tensor(ZH[:, r, 1, :], zf[r], ZH[:, r, 0, :], ALU.subtract), [th])
            zf_free[r] = tl
            return r, tl

        def mix_mm(r, tl, e1, outs, waits):
            for n, (wp, xp) in enumerate(((0, 0), (1, 0), (0, 1))):
                for m, bk in outs:
                    wo = (m * 16 + e1) * 128
                    tk = pe.op(lambda e, wo=wo, bk=bk, wp=wp, xp=xp, n=n: e.matmul(
                        BK[bk][:, :], P16[:, wp, wo:wo + 128], ZH[:, r, xp, :], start=(e1 == 0 and n == 0), stop=(e1 == 15 and n == 2)),
                        [tl, *waits], inc=(n == 2 and (m, bk) == outs[-1]))
                    waits = ()
            zh_free[r] = tk
            return tk

        def mixture(src, mats, evac, after, banks):
            items = [(c, e1) for c in range(4) for e1 in range(16)]
            stt, lo = {}, {}
            for k in range(len(items) + 3):
                if k < len(items):
                    stt[k] = scaled(items[k][1], items[k][0], src, after(items[k][0]))
                if 0 <= k - 1 < len(items):
                    lo[k - 1] = scaled_lo(stt[k - 1])
                if 0 <= k - 3:
                    c, e1 = items[k - 3]
                    outs = [(m, banks(c, i)) for i, m in enumerate(mats)]
                    waits = [w for _, bk in outs for w in free[bk]] if e1 == 0 else []
                    tk = mix_mm(*lo[k - 3], e1, outs, [*waits, p_ready[-1]])
                    if e1 == 15:
                        evac(c, outs, tk)

        qkv_t = []

        def qkv_evac(c, outs, tk):
            for (m, bk), dst in zip(outs, (QP, KP, VP)):
                tv = act.op(lambda e, bk=bk, dst=dst: e.activation(dst[:, cc(c)], BK[bk][:, :], ACT.Copy), [tk])
                free[bk] = (tv,)
            qkv_t.append(tv)

        mixture(X5, (0, 1, 2), qkv_evac, lambda c: [x5_t[-1], tq, dn2[15], xs[-1]], lambda c, i: 3 * (c % 2) + i)

        part(8)
        RT2 = WK[:, :, :]
        PP, VS = RT2[:, 0, :], RT2[:, 1, :]
        PTT = X5
        NM = SM[:, 31, :]
        SS = SM[:, 32, :]
        RS = SM[:, 33, :]
        o_t = []
        for c in range(4):
            for i in range(4):
                b = 4 * c + i
                tp = pe.op(lambda e, b=b, i=i: e.transpose(BK[0][:, bb_(i)], VP[:, bb_(b)], pk1("ident")), [qkv_t[c], *free[0]], inc=(i == 3))
            tvs = act.op(lambda e, c=c: e.activation(VS[:, cc(c)], BK[0][:, :], ACT.Copy), [tp, w48_t[-1]])
            free[0] = (tvs,)
            sb_ = 1 + c % 2
            for i in range(4):
                b = 4 * c + i
                tp = pe.op(lambda e, b=b, i=i, sb_=sb_: e.matmul(BK[sb_][:, bb_(i)], QP[:, bb_(b)], KP[:, bb_(b)], start=True, stop=True), [*free[sb_]], inc=(i == 3))
            t = dve.op(lambda e, c=c, sb_=sb_: e.tensor_reduce(NM[:, 4 * c:4 * c + 4], BK[sb_][:, :].rearrange("p (b n) -> p b n", b=4), X_AX, ALU.max), [tp])
            t = dve.op(lambda e, c=c: e.tensor_scalar(NM[:, 4 * c:4 * c + 4], NM[:, 4 * c:4 * c + 4], -ISC, None, ALU.mult), [t])
            for i in range(4):
                b = 4 * c + i
                te = act.op(lambda e, b=b, i=i, sb_=sb_: e.activation(PP[:, bb_(b)], BK[sb_][:, bb_(i)], ACT.Exp, bias=NM[:, b:b + 1], scale=ISC,
                                                                      accum_out=SS[:, b:b + 1]), [t])
            free[sb_] = (te,)
            t = dve.op(lambda e, c=c: e.reciprocal(RS[:, 4 * c:4 * c + 4], SS[:, 4 * c:4 * c + 4]), [te])
            t = dve.op(lambda e, c=c: e.tensor_tensor(PP[:, cc(c)].rearrange("p (b n) -> p b n", b=4), PP[:, cc(c)].rearrange("p (b n) -> p b n", b=4),
                                                      RS[:, 4 * c:4 * c + 4].unsqueeze(2).to_broadcast([128, 4, 128]), ALU.mult), [t])
            for i in range(4):
                b = 4 * c + i
                tp = pe.op(lambda e, b=b, i=i: e.transpose(BK[3][:, bb_(i)], PP[:, bb_(b)], pk1("ident")), [t, *free[3]], inc=(i == 3))
            tpt = dve.op(lambda e, c=c: e.tensor_copy(PTT[:, cc(c)], BK[3][:, :]), [tp])
            free[3] = (tpt,)
            for i in range(4):
                b = 4 * c + i
                tp = pe.op(lambda e, b=b, i=i: e.matmul(BK[4][:, bb_(i)], VS[:, bb_(b)], PTT[:, bb_(b)], start=True, stop=True), [tvs, tpt, *free[4]], inc=(i == 3))
            to = act.op(lambda e, c=c: e.activation(OT[:, cc(c)], BK[4][:, :], ACT.Copy), [tp])
            free[4] = (to,)
            o_t.append(to)

        def out_evac(c, outs, tk):
            bk = outs[0][1]
            tv = dve.op(lambda e: e.tensor_tensor(XT[:, cc(c)], XT[:, cc(c)], BK[bk][:, :], ALU.add), [tk])
            free[bk] = (tv,)
            dma(out[:, cc(c)], XT[:, cc(c)], [tv], store=True)

        mixture(OT, (3,), out_evac, lambda c: [o_t[c]], lambda c, i: c % 2)
        for t in stores:
            sp.op(lambda e, t=t: e.wait_ge(t.sem, t.val), inc=False)

        block = ctx.enter_context(nc.Block())
        block.sync(sp.run)
        block.gpsimd(pool.run)
        block.scalar(act.run)
        block.vector(dve.run)
        block.tensor(pe.run)


def layout(i):
    f = np.float32
    g = {k: np.asarray(v) for k, v in i.items()}
    A = {}
    A["xT"] = g["x"].reshape(N, D).T
    A["condB"] = np.broadcast_to(g["cond_8"][None], (128, 16, 8))

    def moe(gate, up, down):
        return np.concatenate([gate, up, down.reshape(4, 128, 128).transpose(1, 0, 2).reshape(128, 512)], 1)
    A["w0"] = np.stack([moe(g["L0_cond_shared_gate"], g["L0_cond_shared_up"], g["L0_cond_shared_down"])] +
                       [moe(g["L0_cond_skill_gate"][e], g["L0_cond_skill_up"][e], g["L0_cond_skill_down"][e]) for e in range(8)])
    sw = np.r_[64:128, 0:64]
    a = "L0_attn_"
    m = np.arange(128)
    l_, b_ = m // 8, m % 8
    idx = np.clip(63 + l_[:, None] - l_[None, :], 0, 126)
    p0 = {"WuT": g[a + "Wu"].T, "WvT": g[a + "Wv"].T, "WbT": g[a + "Wb"].T, "WbsT": g[a + "Wb"][sw].T,
          "WoT": g[a + "Wo"].T.reshape(2, 128, 128).transpose(1, 0, 2).reshape(128, 256),
          "As": g["L0_cond2_As"].reshape(128, 128), "BsT": g["L0_cond2_Bs"].transpose(0, 2, 1).reshape(128, 128),
          "WbaseT": g["L0_cond2_W_base"].T, "relb": g[a + "w_rel"][idx]}
    A["pk0"] = np.concatenate([p0[k] for k in PK0], 1)
    half = 64
    pos = np.arange(16, dtype=f)
    inv = (f(10000.0) ** (-np.arange(half, dtype=f) / f(half))).astype(f)
    ang = (pos[None, :] * inv[:, None]).astype(f)
    cos, sin = np.cos(ang).astype(f), np.sin(ang).astype(f)
    diff = m[None, :] - m[:, None]
    p1 = {"ident": np.eye(128, dtype=f),
          "decT": np.where(diff >= 0, f(0.96875) ** diff.astype(f), f(0)).astype(f),
          "amask": np.where((b_[:, None] == b_[None, :]) & (l_[:, None] <= l_[None, :]), f(0), f(-1e30)).astype(f),
          "cos": np.concatenate([cos, cos]), "sin": np.concatenate([-sin, sin]),
          "condR": np.repeat(g["cond_8"].T, 16, axis=0), "sim": g["L1_ffn_sim_matrix"],
          "gates": np.broadcast_to(g["L1_ffn_gates"][None], (128, 16)),
          "iota8": np.broadcast_to(np.tile(np.arange(8, dtype=f) - 99, 16)[None], (128, 128)),
          "iota16": np.broadcast_to(np.tile(np.arange(16, dtype=f) - 99, 16)[None], (128, 256)),
          "kmask": np.tile(np.eye(16, dtype=f), (8, 1))}
    A["pk1"] = np.concatenate([p1[k] for k in PK1], 1)
    b = "L1_attn_weight_"
    A["pk2"] = np.concatenate([g[b + "q"].T, g[b + "k"].T, g[b + "v"]], 1)
    c = {"ln_g": g[a + "ln_g"], "ln_b": g[a + "ln_b"], "bu0": g[a + "bu"][:128], "bu1": g[a + "bu"][128:], "bb": g[a + "bb"],
         "bbs": g[a + "bb"][sw], "bo": g[a + "bo"], "b_base": g["L0_cond2_b_base"], "cbias": g["L1_cond_bias"], "theta": g["L1_attn_theta"]}
    for q in ("qq", "qk"):
        for w in "wb":
            c[q + w] = g[a + q + w]
            c[q + w + "s"] = g[a + q + w][sw]
    A["cols"] = np.stack([c[k] for k in COLS], 1)
    d = "L1_cond2_b_"
    A["c2b"] = np.stack([g[d + "up"][:, :128].T, g[d + "up"][:, 128:].T, g[d + "gate"][:, :128].T, g[d + "gate"][:, 128:].T, g[d + "down"].T], 1)
    A["bv"] = g[a + "bv"][None]
    A["fw"] = np.concatenate([g["L0_ffn_w_up"].reshape(3, 128, 128), g["L0_ffn_w_gate"].reshape(3, 128, 128),
                              g["L0_ffn_w_down"].reshape(128, 3, 128).transpose(1, 0, 2)]).transpose(1, 0, 2)
    A["l1w"] = g["L1_cond_weight"].reshape(8, 8, 16, 128).transpose(0, 2, 1, 3).reshape(128, 1024)
    A["l1m"] = np.tile(g["L1_cond_mask"].reshape(8, 16, 128).transpose(1, 0, 2).reshape(16, 1024), (8, 1))
    w = "L1_cond2_W_"
    per = [np.concatenate([g[w + "up"][e].T, g[w + "gate"][e].T, g[w + "down"][e].T.reshape(2, 128, 128).transpose(1, 0, 2).reshape(128, 256)], 1)
           for e in range(8)]
    A["w1"] = np.stack([np.concatenate(per[2 * k:2 * k + 2], 1) for k in range(4)])
    A["w2"] = np.concatenate([g["L1_ffn_" + k].transpose(1, 0, 2).reshape(128, 2048) for k in ("q_proj", "k_proj", "v_proj", "o_proj")], 1)
    A["sel"] = np.broadcast_to(np.tile(np.eye(16, dtype=np.float16), (3, 1))[:, :, None], (48, 16, 128))
    return {k: np.ascontiguousarray(v) for k, v in A.items()}


def kernel(**inputs):
    import concourse.bacc as bacc
    from concourse.bass_utils import run_bass_kernel_spmd

    nc = bacc.Bacc("TRN2", target_bir_lowering=False, num_devices=1)
    arrays = {f"in_{k}": v for k, v in layout(inputs).items()}
    A = {k[3:]: nc.dram_tensor(k, v.shape, mybir.dt.from_np(v.dtype), kind="ExternalInput").ap() for k, v in arrays.items()}
    out = nc.dram_tensor("out_0", (128, N), F32, kind="ExternalOutput").ap()
    program(nc, A, out)
    r = run_bass_kernel_spmd(nc, [arrays], core_ids=[0])
    return np.ascontiguousarray(r.results[0]["out_0"].T.reshape(NB, S, D))
```

```python
from contextlib import ExitStack

import numpy as np

import concourse.bass as bass
from concourse import mybir

F32 = mybir.dt.float32
F16 = mybir.dt.float16
BF16 = mybir.dt.bfloat16
I32 = mybir.dt.int32
ALU = mybir.AluOpType
ACT = mybir.ActivationFunctionType
X_AX = mybir.AxisListType.X

NB, S, D = 16, 128, 128
N = NB * S
I0, E0 = 512, 8
WE = 3 * I0
H2 = 256
CE = 3 * H2
E1 = 16
WS = 256.0
MAGIC = 12582912.0
QMAX = 32767.0
NEG = -3.0e38
ISC = float(1.0 / np.sqrt(np.float32(D)))

COLS = ["ln_g", "ln_b", "bu0", "bu1", "bb", "bbs", "qqw", "qqb", "qkw", "qkb", "qqws", "qqbs", "qkws",
        "qkbs", "bo", "b_base", "cbias", "theta"]
CI = {n: i for i, n in enumerate(COLS)}
PK0 = {"WuT": (0, 256), "WvT": (256, 512), "WbT": (512, 640), "WbsT": (640, 768), "WoT": (768, 1024),
       "As": (1024, 1152), "BsT": (1152, 1280), "WbaseT": (1280, 1408), "relb": (1408, 1536)}
PK1 = {"ident": (0, 128), "decT": (128, 256), "amask": (256, 384), "cos": (384, 400), "sin": (400, 416),
       "condR": (416, 432), "sim": (432, 448), "iota16": (448, 704), "kmask": (704, 720)}
PK1N = 720
PKA = {"iota8": (0, 128), "gates": (128, 144)}
PK2 = {"WqT": (0, 128), "WkT": (128, 256), "Wv1": (256, 384)}


class Tok:
    def __init__(self, sem, val):
        self.sem, self.val = sem, val


class Queue:

    def __init__(self, new_sem, name):
        self.new_sem, self.name = new_sem, name
        self.todo, self.seen = [], {}
        self.part(0)

    def part(self, n):
        self.sem, self.val = self.new_sem(f"s_{self.name}{n}"), 0

    def op(self, fn, after=(), inc=True):
        for t in after:
            if t is not None and self.seen.get(t.sem, 0) < t.val:
                self.seen[t.sem] = t.val
                self.todo.append(lambda e, t=t: e.wait_ge(t.sem, t.val))
        if not inc:
            self.todo.append(fn)
            return None
        self.val += 1
        sem = self.sem
        self.todo.append(lambda e: fn(e).then_inc(sem, 1))
        return Tok(sem, self.val)

    def run(self, e):
        for f in self.todo:
            f(e)


def program(nc, A, out):
    with ExitStack() as ctx:
        def sb(name, shape, dt=F32):
            return ctx.enter_context(nc.sbuf_tensor(name, shape, dt))

        nsem = [0]

        def sem(name):
            nsem[0] += 1
            return ctx.enter_context(nc.semaphore(f"{name}_{nsem[0]}"))

        pe, act, dve, pool, sp = (Queue(sem, n) for n in ("pe", "act", "dve", "pool", "sp"))

        def part(n):
            for q in (pe, act, dve, pool):
                q.part(n)

        stores = []

        def dma(dst, src, after=(), q=None, store=False):
            q = q or sp
            s = sem("d")
            for t in after:
                if t is not None:
                    q.op(lambda e, t=t: e.wait_ge(t.sem, t.val), inc=False)
            q.op(lambda e: e.dma_start(dst, src).then_inc(s, 16), inc=False)
            t = Tok(s, 16)
            if store:
                stores.append(t)
            return t

        BK = [ctx.enter_context(nc.psum_tensor(f"bk{i}", [128, 512], F32)) for i in range(8)]
        free = [() for _ in range(8)]

        RA = sb("RA", [128, 13824])
        RB = sb("RB", [128, 8192])
        RC = sb("RC", [128, 6144])
        STG = sb("STG", [128, 2, 1536])
        XT = sb("XT", [128, N])
        X16 = sb("X16", [128, 2, N], F16)
        QT = sb("QT", [128, N])
        WK = sb("WK", [128, 2, 2048])
        PK0T = sb("PK0T", [128, 1536])
        PK1T = sb("PK1T", [128, PK1N])
        PKAT = sb("PKAT", [128, 144])
        PK2T = sb("PK2T", [128, 384])
        COL = sb("COL", [128, len(COLS)])
        C2B = sb("C2B", [128, 5, 8])
        BV = sb("BV", [1, 256])
        WEFF = sb("WEFF", [128, N])
        WBOT = sb("WBOT", [128, N])
        FW = RB[:, 6656:7808].rearrange("p (k n) -> p k n", k=9)
        FWT = sb("FWT", [128, 9, 128])
        CONDB = sb("CONDB", [128, 16, 8])
        SM = sb("SM", [128, 40, 16])
        SL = RB[:, 1536:3072].rearrange("p (k n) -> p k n", k=12)
        ROPE = sb("ROPE", [128, 8, 16])
        ONESK = sb("ONESK", [128, 128])
        ONES = sb("ONES", [128, 128])
        ATT = sb("ATT", [128, 3, 128])
        WCOL = sb("WCOL", [128, 2, 16])
        EIX = sb("EIX", [128, 3, 16], I32)
        BSEL = sb("BSEL", [128, 5, 16])
        QS = sb("QS", [128, 64])
        ROW = sb("ROW", [1, 16])

        def pk0(n):
            return PK0T[:, PK0[n][0]:PK0[n][1]]

        def pk1(n):
            return PK1T[:, PK1[n][0]:PK1[n][1]]

        def pka(n):
            return PKAT[:, PKA[n][0]:PKA[n][1]]

        def pk2(n):
            return PK2T[:, PK2[n][0]:PK2[n][1]]

        def col(n):
            return COL[:, CI[n]:CI[n] + 1]

        def cc(c):
            return slice(512 * c, 512 * c + 512)

        def bb_(b):
            return slice(128 * b, 128 * b + 128)

        def big(j):
            return RA[:, 2048 * j:2048 * j + 2048]

        def root(dst, src, tmp, add, least, after):
            v, s = tmp[:, 0, :], tmp[:, 1, :]
            t = dve.op(lambda e: e.tensor_scalar(v, src, add, None, ALU.add), after)
            t = act.op(lambda e: e.activation(s, v, ACT.Sqrt), [t])
            t = dve.op(lambda e: e.tensor_scalar(s, s, least, None, ALU.max), [t])
            t = dve.op(lambda e: e.reciprocal(dst, s), [t])
            t = dve.op(lambda e: e.tensor_tensor(dst, dst, v, ALU.mult), [t])
            t = dve.op(lambda e: e.tensor_tensor(dst, dst, s, ALU.add), [t])
            return dve.op(lambda e: e.tensor_scalar(dst, dst, 0.5, least, ALU.mult, ALU.max), [t])

        d_cond = dma(CONDB[:, :, :], A["condB"], q=act)
        d_pka = dma(PKAT[:, :], A["pka"], q=act)
        d_col = dma(COL[:, :], A["cols"], q=act)
        d_c2b = dma(C2B[:, :, :], A["c2b"], q=act)
        d_bv = dma(BV[:, :], A["bv"], q=act)
        slots = [STG[:, 0, :], STG[:, 1, :], WK[:, 0, 0:1536]] + [RC[:, 1536 * i:1536 * i + 1536] for i in range(4)]
        d_x, d_w = [], []
        d_sh = [dma(slots[0][:, 0:768], A["w0"][0][:, 0:768])]
        d_x.append(dma(XT[:, cc(0)], A["xT"][:, cc(0)]))
        d_sh.append(dma(slots[0][:, 768:1536], A["w0"][0][:, 768:1536]))
        d_x.append(dma(XT[:, cc(1)], A["xT"][:, cc(1)]))
        d_w.append(dma(slots[1], A["w0"][1]))
        d_x.append(dma(XT[:, cc(2)], A["xT"][:, cc(2)]))
        d_w.append(dma(slots[2], A["w0"][2]))
        d_x.append(dma(XT[:, cc(3)], A["xT"][:, cc(3)]))
        L1W = RB[:, 4608:5632]
        L1M = RB[:, 5632:6656]
        BSC = WBOT[:, :]
        KRF = RB[:, 7808:8064]

        c_ones = dve.op(lambda e: e.memset(ONES[:, :], 1.0))
        c_onesk = dve.op(lambda e: e.memset(ONESK[:, :], 1.0 / 128))

        W16 = RA[:, :].bitcast(F16)

        def split_hi(dst, src, after):
            return act.op(lambda e: e.activation(dst, src, ACT.Copy, scale=WS), after)

        x_lo, w_ready = [], []

        def split_x(c):
            th = act.op(lambda e: e.activation(X16[:, 0, cc(c)], XT[:, cc(c)], ACT.Copy), [d_x[c]])
            x_lo.append(dve.op(lambda e: e.tensor_tensor(X16[:, 1, cc(c)], XT[:, cc(c)], X16[:, 0, cc(c)], ALU.subtract), [th]))

        def split_shared(h):
            src = slots[0][:, 768 * h:768 * h + 768]
            o = 8 * 3072 + 768 * h
            th = split_hi(W16[:, o:o + 768], src, [d_sh[h]])
            return dve.op(lambda e: e.scalar_tensor_tensor(W16[:, o + 1536:o + 2304], src, WS, W16[:, o:o + 768], ALU.mult, ALU.subtract), [th])

        sh_ready = [split_shared(0)]
        split_x(0)
        sh_ready.append(split_shared(1))
        split_x(1)
        iota8 = pka("iota8").rearrange("p (b e) -> p b e", e=8)

        def first_max(q, lg, iota, m, eq, ix, oh, after):
            nb, ne = lg.shape[1], lg.shape[2]
            t = q.op(lambda e: e.tensor_reduce(m, lg, X_AX, ALU.max), after)
            t = q.op(lambda e: e.tensor_tensor(eq, lg, m.unsqueeze(2).to_broadcast([128, nb, ne]), ALU.is_equal), [t])
            t = q.op(lambda e: e.tensor_tensor(eq, eq, iota, ALU.mult), [t])
            t = q.op(lambda e: e.tensor_reduce(ix, eq, X_AX, ALU.min), [t])
            return q.op(lambda e: e.tensor_tensor(oh, iota, ix.unsqueeze(2).to_broadcast([128, nb, ne]), ALU.is_equal), [t])

        def sl8(i):
            return SL[:, i, :].rearrange("p (b e) -> p b e", e=8)

        t = first_max(dve, CONDB[:, :, :], iota8, SM[:, 0, :], sl8(0), SM[:, 1, :], sl8(1), [d_cond, d_pka])
        oh1_t = t
        t = dve.op(lambda e: e.scalar_tensor_tensor(sl8(2), sl8(1), NEG, CONDB[:, :, :], ALU.mult, ALU.add), [t])
        t = first_max(dve, sl8(2), iota8, SM[:, 2, :], sl8(0), SM[:, 3, :], sl8(3), [t])
        t = dve.op(lambda e: e.tensor_scalar(EIX[:, 0:2, :], SM[:, 1:4:2, :], 99.0, 3072.0, ALU.add, ALU.mult), [t])
        t_eix = dve.op(lambda e: e.tensor_scalar(EIX[:, 2, :], SM[:, 1, :], 99.0, 1536.0, ALU.add, ALU.mult), [t])
        t = dve.op(lambda e: e.tensor_tensor(sl8(4), CONDB[:, :, :], SM[:, 0, :].unsqueeze(2).to_broadcast([128, 16, 8]),
                                             ALU.subtract), [t_eix])
        t2 = dve.op(lambda e: e.tensor_tensor(SM[:, 4, :], SM[:, 2, :], SM[:, 0, :], ALU.subtract), [t])
        t = act.op(lambda e: e.activation(sl8(5), sl8(4), ACT.Exp), [t2])
        t = act.op(lambda e: e.activation(SM[:, 5, :], SM[:, 4, :], ACT.Exp), [t])
        t = dve.op(lambda e: e.tensor_reduce(SM[:, 6, :], sl8(5), X_AX, ALU.add), [t])
        t = dve.op(lambda e: e.reciprocal(SM[:, 7, :], SM[:, 6, :]), [t])
        t = dve.op(lambda e: e.tensor_tensor(SM[:, 8, :], SM[:, 5, :], SM[:, 7, :], ALU.mult), [t])
        t = dve.op(lambda e: e.tensor_tensor(SM[:, 9, :], SM[:, 7, :], SM[:, 8, :], ALU.add), [t])
        t = dve.op(lambda e: e.reciprocal(SM[:, 9, :], SM[:, 9, :]), [t])
        t = dve.op(lambda e: e.tensor_tensor(SM[:, 10:12, :], SM[:, 7:9, :], SM[:, 9, :].unsqueeze(1).to_broadcast([128, 2, 16]),
                                             ALU.mult), [t])
        t = dve.op(lambda e: e.tensor_scalar(SM[:, 12:14, :], SM[:, 10:12, :], 1.0 / 12, None, ALU.mult), [t])
        t = dve.op(lambda e: e.scalar_tensor_tensor(SM[:, 10:12, :], SM[:, 10:12, :], 1.0 - 1.0 / 12, SM[:, 12:14, :],
                                                    ALU.mult, ALU.add), [t])
        t_w = dve.op(lambda e: e.tensor_scalar(WCOL[:, :, :], SM[:, 10:12, :], 1.0 / WS, None, ALU.mult), [t])
        SIG = SM[:, 22, :]
        t = dve.op(lambda e: e.tensor_scalar(QS[:, 0:1], col("theta"), 0.0, None, ALU.mult), [d_col])
        t_th = act.op(lambda e: e.activation(QS[:, 1:2], QS[:, 0:1], ACT.Exp), [t])
        sg_t = act.op(lambda e: e.activation(SIG, pka("gates"), ACT.Sigmoid), [d_pka])
        t = t_w
        t_bsel = []
        for k in range(5):
            tk = pool.op(lambda e, k=k: e.tensor_tensor(sl8(6 + k), sl8(1), C2B[:, k, :].unsqueeze(1).to_broadcast([128, 16, 8]),
                                                        ALU.mult), [oh1_t, d_c2b])
            t_bsel.append(dve.op(lambda e, k=k: e.tensor_reduce(BSEL[:, k, :], sl8(6 + k), X_AX, ALU.add), [tk]))
        t_sl = t_bsel[-1]
        t_bsel = dve.op(lambda e: e.tensor_scalar(BSEL[:, 2:4, :], BSEL[:, 2:4, :], WS, None, ALU.mult), [t_bsel[-1]])

        regs = {}

        def load(g):
            _, v = nc.values_load_multi_w_load_instructions(EIX[0:1, 0:2, 4 * g:4 * g + 4], [mybir.EngineType.PE], min_val=0, max_val=7 * 3072)
            for j in range(2):
                for i in range(4):
                    regs[(4 * g + i, j)] = v[4 * j + i]

        slot_free = [sh_ready[1]] + [None] * 6

        def expert(e1):
            sl = (e1 + 1) % 7
            src = slots[sl]
            hi, lo = W16[:, e1 * 3072:e1 * 3072 + 1536], W16[:, e1 * 3072 + 1536:(e1 + 1) * 3072]
            th = split_hi(hi, src, [d_w[e1]])
            if e1 in (0, 2, 4):
                t = pool.op(lambda e: e.tensor_scalar(src, src, WS, None, ALU.mult), [th])
                t = pool.op(lambda e: e.tensor_tensor(lo, src, hi, ALU.subtract), [t])
            else:
                t = dve.op(lambda e: e.scalar_tensor_tensor(lo, src, WS, hi, ALU.mult, ALU.subtract), [th])
            w_ready.append(t)
            slot_free[sl] = t

        def fetch(e1):
            sl = (e1 + 1) % 7
            d_w.append(dma(slots[sl], A["w0"][e1 + 1], [slot_free[sl]]))

        for e1 in range(2, 7):
            fetch(e1)
        order = [("sh", g, j) for g in range(4) for j in range(4)]
        for g in range(4):
            ex = [("ex", 4 * g + bi, s) for bi in range(4) for s in range(2)]
            if g:
                ex[6:6] = [("var", g - 1, 0)]
                ex[4:4] = [("mean", g - 1, 0)]
            order += ex
        nu = len(order)
        real = [k for k in range(nu) if order[k][0] in ("sh", "ex")]
        idx = {k: u for u, k in enumerate(real)}
        ge = [WK[:, 1, 512 * i:512 * i + 512] for i in range(3)]
        hf = [RB[:, 512 * i:512 * i + 512] for i in range(3)]
        H16 = RB[:, 3072:4608].bitcast(F16).rearrange("p (r h n) -> p r h n", r=3, h=2)
        SQ = WK[:, 0, :]
        LNV = SM[:, 14, :]
        up_t, ge_t, mul_t, hi_t, lo_t, dn_t = {}, {}, {}, {}, {}, {}
        pair_free = {}
        q_t, mean_t, var_t, xq_t = [None] * 4, {}, {}, {}

        def w_ap(kind, v, off, part):
            if kind == "sh":
                o = 8 * 3072 + part * 1536 + off
                return W16[:, o:o + 128]
            return W16[:, bass.ds(v + (part * 1536 + off), 128)]

        def up(k):
            kind, a, j = order[k]
            gb, ub = BK[2 * (k % 3)], BK[2 * (k % 3) + 1]
            for g in {3: (2, 3), 16: (0, 1)}.get(k, ()):
                pe.op(lambda e, g=g: load(g), [t_eix], inc=False)
            waits = [pair_free.get(k - 3), *([sh_ready[j // 2], x_lo[a]] if kind == "sh" else [*w_ready, *x_lo])]
            for half, bank in ((0, gb), (1, ub)):
                if kind == "sh":
                    tiles = [(j, slice(0, 512), slice(512 * a, 512 * a + 512))]
                else:
                    tiles = [(jj, slice(128 * jj, 128 * jj + 128), bb_(a)) for jj in range(4)]
                for jj, oc, xc in tiles:
                    for n, (wp, xp) in enumerate(((0, 0), (0, 1), (1, 0))):
                        last = half == 1 and n == 2 and oc.stop == 512

                        def mm(e, bank=bank, oc=oc, xc=xc, wp=wp, xp=xp, off=384 * jj + half * 128, n=n):
                            return e.matmul(bank[:, oc], w_ap(kind, regs.get((a, j)), off, wp), X16[:, xp, xc],
                                            start=(n == 0), stop=(n == 2))
                        tk = pe.op(mm, waits, inc=last)
                        waits = ()
            up_t[k] = tk

        def down(k):
            kind, a, j = order[k]
            g = a if kind == "sh" else a // 4
            bk = 6 + g % 2
            waits = [lo_t[k], *free[bk]]
            if kind == "sh":
                tiles = [(j, slice(0, 512), slice(0, 512))]
                begin, end = j == 0, j == 3
            else:
                tiles = [(jj, slice(128 * jj, 128 * jj + 128), bb_(a % 4)) for jj in range(4)]
                begin, end = j == 0, j == 1
            h16 = H16[:, idx[k] % 3, :, :]
            for jj, hc, oc in tiles:
                for n, (wp, xp) in enumerate(((0, 0), (0, 1), (1, 0))):
                    first = begin and n == 0 and hc.start == 0
                    final = end and n == 2 and hc.stop == 512

                    def mm(e, wp=wp, xp=xp, off=384 * jj + 256, hc=hc, oc=oc, first=first, final=final):
                        return e.matmul(BK[bk][:, oc], w_ap(kind, regs.get((a, j)), off, wp), h16[:, xp, hc],
                                        start=first, stop=final, skip_group_check=True)
                    tk = pe.op(mm, waits, inc=(n == 2 and hc.stop == 512))
                    waits = ()
            dn_t[idx[k]] = tk
            if kind == "sh" and end:
                q_t[g] = act.op(lambda e: e.activation(QT[:, cc(g)], BK[bk][:, :], ACT.Copy, scale=1.0 / WS), [tk])
                free[bk] = (q_t[g],)
            if kind == "ex" and end and a % 4 == 3:
                q_t[g] = dve.op(lambda e: e.scalar_tensor_tensor(QT[:, cc(g)], BK[bk][:, :], 1.0 / WS, QT[:, cc(g)], ALU.mult, ALU.add),
                                [tk, q_t[g]])
                free[bk] = (q_t[g],)
                xq_t[g] = dve.op(lambda e: e.tensor_tensor(XT[:, cc(g)], XT[:, cc(g)], QT[:, cc(g)], ALU.add), [q_t[g], x_lo[g]])

        def mean(c, bank, after):
            tp = pe.op(lambda e: e.matmul(bank[:, :], ONESK[:, :], QT[:, cc(c)], start=True, stop=True), [q_t[c], c_onesk, *after])
            td = dve.op(lambda e: e.tensor_tensor(QT[:, cc(c)], QT[:, cc(c)], bank[:, :], ALU.subtract), [tp, xq_t[c]])
            mean_t[c] = (td, act.op(lambda e: e.activation(SQ[:, cc(c)], QT[:, cc(c)], ACT.Square), [td, *w_ready]))
            return td

        def var(c, bank, after):
            for i in range(4):
                tp = pe.op(lambda e, i=i: e.matmul(bank[:, i:i + 1], SQ[:, bb_(4 * c + i)], ONESK[:, 0:1], start=True, stop=True),
                           [mean_t[c][1], *after], inc=(i == 3))
            var_t[c] = dve.op(lambda e: e.tensor_copy(LNV[:, 4 * c:4 * c + 4], bank[:, 0:4]), [tp])
            return var_t[c]

        g_stg = [9]
        d_stg = {}
        stg_free = slot_free
        C16 = RC[:, :].bitcast(F16)
        c_ready = []
        late = {}

        def loads():
            late["pk1"] = dma(PK1T[:, :], A["pk1"])
            late["pk0"] = dma(PK0T[:, :], A["pk0"])
            late["fw"] = dma(FW[:, :, :], A["fw"])
            late["l1"] = [dma(L1W, A["l1w"]), dma(L1M, A["l1m"])]
            late["pk2"] = dma(PK2T[:, :], A["pk2"])

        def stage_load(src, n):
            g = g_stg[0]
            d_stg[g] = dma(STG[:, g % 2, 0:n], src, [stg_free[g % 2]])
            g_stg[0] += 1
            return g

        def split_c16(i):
            g = stage_load(A["w1"][i], 1536)
            hi = C16[:, 3072 * i:3072 * i + 3072].rearrange("p (e h n) -> p e h n", e=2, h=2)
            src = STG[:, g % 2, :].rearrange("p (e n) -> p e n", e=2)
            th = pool.op(lambda e: e.tensor_scalar(hi[:, :, 0, :], src, WS, None, ALU.mult), [d_stg[g], *w_ready])
            tl = pool.op(lambda e: e.tensor_scalar(src, src, WS, None, ALU.mult), [th])
            tl = pool.op(lambda e: e.tensor_tensor(hi[:, :, 1, :], src, hi[:, :, 0, :], ALU.subtract), [tl])
            stg_free[g % 2] = tl
            c_ready.append(tl)

        KR = KRF.rearrange("p (b j) -> p b j", b=16)

        def prep_pool():
            late["l1p"] = pool.op(lambda e: e.tensor_tensor(L1W, L1W, L1M, ALU.mult), late["l1"])

        def prep_lora():
            condR = pk1("condR")
            late["bsc"] = dve.op(lambda e: e.scalar_tensor_tensor(
                BSC.rearrange("p (b o) -> p b o", b=16), pk0("BsT").unsqueeze(1).to_broadcast([128, 16, 128]), 2.0,
                condR.unsqueeze(2).to_broadcast([128, 16, 128]), ALU.mult, ALU.mult), [late["pk0"], late["pk1"]])
            late["kr"] = dve.op(lambda e: e.tensor_tensor(KR, pk1("kmask").unsqueeze(1).to_broadcast([128, 16, 16]),
                                                          condR.unsqueeze(2).to_broadcast([128, 16, 16]), ALU.mult))

        FB = QS[:, 16:52]
        FR = SM[:, 36:39, :].rearrange("p a b -> p (a b)")[:, 0:36]
        fw3 = FW[:, :, :].rearrange("p t (k i) -> p (t k) i", i=32)

        def prep_fw(part_):
            if part_ == 0:
                t = dve.op(lambda e: e.tensor_reduce(FB, fw3, X_AX, ALU.max, apply_absolute_value=True), [late["fw"]])
                t = dve.op(lambda e: e.tensor_scalar(FB, FB, 1.0 / 7.0, 1e-12, ALU.mult, ALU.max), [t])
                t = dve.op(lambda e: e.reciprocal(FR, FB), [t])
            elif part_ == 1:
                t = dve.op(lambda e: e.tensor_tensor(fw3, fw3, FR.unsqueeze(2).to_broadcast([128, 36, 32]), ALU.mult), [late["fq"]])
            elif part_ == 2:
                t = dve.op(lambda e: e.tensor_scalar(fw3, fw3, MAGIC, MAGIC, ALU.add, ALU.subtract), [late["fq"]])
                t = dve.op(lambda e: e.tensor_scalar(fw3, fw3, -8.0, 7.0, ALU.max, ALU.min), [t])
            else:
                t = dve.op(lambda e: e.tensor_tensor(fw3, fw3, FB.unsqueeze(2).to_broadcast([128, 36, 32]), ALU.mult), [late["fq"]])
            late["fq"] = t

        def prep_theta():
            late["th"] = dve.op(lambda e: e.tensor_scalar(ATT[:, 1, :], pk2("WkT"), QS[:, 1:2], QS[:, 1:2], ALU.mult, ALU.mult), [t_th, late["pk2"]])
            late["sn"] = dve.op(lambda e: e.tensor_tensor(SM[:, 20, :], pk1("sim"), pk1("sim"), ALU.mult), [late["pk1"]])

        side = {0: [lambda: split_x(2)], 1: [lambda: split_x(3)]}
        for e1, k in enumerate((2, 4, 6, 8, 11, 13, 15, 15)):
            side.setdefault(k, []).append(lambda e1=e1: expert(e1))
        side[4].append(lambda: fetch(7))
        side[16] = [loads]
        for i in range(4):
            side[18 + 5 * i] = [lambda i=i: split_c16(i)]
        side[21] = [prep_pool]
        side[22] = [prep_lora]
        for i in range(4):
            side.setdefault(25 + i, []).append(lambda i=i: prep_fw(i))
        side[30] = [prep_theta]
        for k in range(nu + 3):
            if k < nu:
                kind, a, j = order[k]
                if kind in ("mean", "var"):
                    pair_free[k] = (mean if kind == "mean" else var)(a, BK[2 * (k % 3)], [pair_free.get(k - 3)])
                else:
                    u = idx[k]
                    r, gb, ub = u % 3, BK[2 * (k % 3)], BK[2 * (k % 3) + 1]
                    up(k)
                    ge_t[u] = act.op(lambda e, r=r, gb=gb: e.activation(ge[r], gb[:, :], ACT.Gelu_apprx_tanh, scale=1.0 / WS),
                                     [up_t[k], mul_t.get(u - 3)])
                    w = (1.0 / WS) if kind == "sh" else WCOL[:, j, a:a + 1]
                    mul_t[u] = dve.op(lambda e, r=r, w=w, ub=ub: e.scalar_tensor_tensor(hf[r], ge[r], w, ub[:, :], ALU.mult, ALU.mult),
                                      [ge_t[u], t_w, lo_t.get(real[u - 3]) if u >= 3 else None])
                    pair_free[k] = mul_t[u]
            p = k - 1
            if p in idx:
                r = idx[p] % 3
                hi_t[p] = act.op(lambda e, r=r: e.activation(H16[:, r, 0, :], hf[r], ACT.Copy), [mul_t[idx[p]], dn_t.get(idx[p] - 3)])
                lo_t[p] = dve.op(lambda e, r=r: e.tensor_tensor(H16[:, r, 1, :], hf[r], H16[:, r, 0, :], ALU.subtract), [hi_t[p]])
            for fn in side.get(k, ()):
                fn()
            if k - 3 in idx:
                down(k - 3)
        lu = len(real) - 1
        moe_end = [dn_t[lu], q_t[3]]
        for i in range(6):
            free[i] = tuple(pair_free[nu - 1 - n] for n in range(3))
        d_pk0, d_pk1, d_pk2 = late["pk0"], late["pk1"], late["pk2"]

        part(1)
        weff_t = []

        def weff(c):
            tp = pe.op(lambda e: e.matmul(BK[2 + c % 2][:, :], pk0("As"), BSC[:, cc(c)], start=True, stop=True), [late["bsc"], *free[2 + c % 2]])
            tv = dve.op(lambda e: e.tensor_tensor(WEFF[:, cc(c)].rearrange("p (b o) -> p b o", b=4),
                                                  BK[2 + c % 2][:, :].rearrange("p (b o) -> p b o", b=4),
                                                  pk0("WbaseT").unsqueeze(1).to_broadcast([128, 4, 128]), ALU.add), [tp])
            free[2 + c % 2] = (tv,)
            weff_t.append(tv)

        wbot_t = []

        def wbot(o):
            bi = 4 + o % 2
            tp = pe.op(lambda e: e.matmul(BK[bi][:, 0:256], L1W[:, 128 * o:128 * o + 128], KRF, start=True, stop=True),
                       [late["l1p"], late["kr"], *free[bi]])
            tv = act.op(lambda e: e.activation(WBOT[:, :].rearrange("p (b o j) -> p b o j", b=16, o=8)[:, :, o, :],
                                               BK[bi][:, 0:256].rearrange("p (b j) -> p b j", b=16), ACT.Copy), [tp, weff_t[-1]])
            free[bi] = (tv,)
            wbot_t.append(tv)

        fw_t = []

        def fwt(i):
            for k in range(3):
                tp = pe.op(lambda e, k=k: e.transpose(BK[i % 2][:, 128 * k:128 * k + 128], FW[:, 3 * i + k, :], pk1("ident")),
                           [late["fq"], *free[i % 2]], inc=(k == 2))
            tv = act.op(lambda e: e.activation(FWT[:, 3 * i:3 * i + 3, :], BK[i % 2][:, 0:384].rearrange("p (k n) -> p k n", k=3), ACT.Copy), [tp])
            free[i % 2] = (tv,)
            fw_t.append(tv)

        weff(0)
        free[0] = (mean(3, BK[0], free[0]),)
        weff(1)
        weff(2)
        weff(3)
        free[1] = (var(3, BK[1], free[1]),)
        LNS = SM[:, 39, :]
        ln_root = root(LNS, LNV, SM[:, 15:17, :], 1e-5, 0.0, [var_t[3]])
        SNR = SM[:, 20, :]
        SNT = SM[:, 21, :]
        tp = pe.op(lambda e: e.matmul(BK[7][:, 0:16], ONES[:, :], SNR, start=True, stop=True), [late["sn"], c_ones, *free[7]])
        t = dve.op(lambda e: e.reciprocal(LNS, LNS), [ln_root])
        BSW = big(4)
        diag_t = [dve.op(lambda e, c=c: e.tensor_tensor(BSW[:, cc(c)].rearrange("p (t n) -> p t n", t=4),
                                                        pk1("ident").unsqueeze(1).to_broadcast([128, 4, 128]),
                                                        LNS[:, 4 * c:4 * c + 4].unsqueeze(2).to_broadcast([128, 4, 128]), ALU.mult), [t, *moe_end])
                  for c in range(4)]
        sn_root = root(SNR, BK[7][:, 0:16], SM[:, 34:36, :], 0.0, 1e-12, [tp])
        free[7] = (sn_root,)
        t = dve.op(lambda e: e.reciprocal(SNR, SNR), [sn_root])
        sn_t = dve.op(lambda e: e.tensor_tensor(SNT, pk1("sim"), SNR, ALU.mult), [t])
        tp = pe.op(lambda e: e.matmul(BK[6][:, 0:128], pk2("WqT"), ATT[:, 1, :], start=True, stop=True), [late["th"], *free[6]])
        a_t = act.op(lambda e: e.activation(ATT[:, 2, :], BK[6][:, 0:128], ACT.Copy), [tp])
        free[6] = (a_t,)
        for o in range(8):
            wbot(o)
        for i in range(3):
            fwt(i)

        rp = ROPE
        cosT, sinT = pk1("cos"), pk1("sin")
        rope_t = []
        for i, q in enumerate(("qq", "qk")):
            o = 4 * i
            pool.op(lambda e, q=q, o=o: e.tensor_scalar(rp[:, o, :], cosT, col(q + "w"), None, ALU.mult), [d_pk1, d_col])
            pool.op(lambda e, q=q, o=o: e.tensor_scalar(rp[:, o + 1, :], sinT, col(q + "ws"), None, ALU.mult))
            ta = pool.op(lambda e, q=q, o=o: e.tensor_scalar(rp[:, o + 2, :], cosT, col(q + "b"), None, ALU.mult))
            tb = pool.op(lambda e, q=q, o=o: e.tensor_scalar(rp[:, o + 3, :], sinT, col(q + "bs"), None, ALU.mult))
            rope_t.append(pool.op(lambda e, o=o: e.tensor_tensor(rp[:, o + 2, :], rp[:, o + 2, :], rp[:, o + 3, :], ALU.add), [tb]))
        relm_t = pool.op(lambda e: e.tensor_tensor(ATT[:, 0, :], pk0("relb"), pk1("amask"), ALU.add), [d_pk0, d_pk1])

        part(2)
        dT, U0, U1, BASE, _, QQ = (big(j) for j in range(6))
        XF = X16[:, :, :].rearrange("p a n -> p (a n)").bitcast(F32)
        QK = XF
        VT = WK[:, :, :].rearrange("p a n -> p (a n)").rearrange("p (t f) -> p t f", t=16)
        U = [U0, U1]
        xn_t = []
        for c in range(4):
            tp = pe.op(lambda e, c=c: e.matmul(BK[2 + c % 2][:, :], ONES[:, :], BSW[:, cc(c)], start=True, stop=True), [diag_t[c], c_ones, *free[2 + c % 2]])
            tx = dve.op(lambda e, c=c: e.scalar_tensor_tensor(dT[:, cc(c)], QT[:, cc(c)], col("ln_g"), BK[2 + c % 2][:, :], ALU.mult, ALU.mult),
                        [tp, mean_t[c][1], *moe_end])
            free[2 + c % 2] = (tx,)
            xn_t.append(act.op(lambda e, c=c: e.activation(dT[:, cc(c)], dT[:, cc(c)], ACT.Identity, bias=col("ln_b")), [tx]))
        bsw_free = tp
        base_t = []
        for c in range(4):
            for i, (w, b, dst) in enumerate(((pk0("WbT"), "bb", BASE), (pk0("WbsT"), "bbs", BSW),
                                             (pk0("WuT")[:, 0:128], "bu0", U0), (pk0("WuT")[:, 128:256], "bu1", U1))):
                bk = 4 + i
                tp = pe.op(lambda e, c=c, w=w, bk=bk: e.matmul(BK[bk][:, :], w, dT[:, cc(c)], start=True, stop=True), [xn_t[c], *free[bk]])
                tv = act.op(lambda e, c=c, b=b, dst=dst, bk=bk: e.activation(dst[:, cc(c)], BK[bk][:, :], ACT.Silu, bias=col(b)), [tp, bsw_free])
                free[bk] = (tv,)
                if i == 1:
                    base_t.append(tv)
        u_t = tv
        xnv = dT.rearrange("p (m t) -> p t m", t=16)
        v_t = []
        for t2_ in range(8):
            bk = t2_ % 4
            for h in range(2):
                t_ = 2 * t2_ + h
                pe.op(lambda e, t_=t_, bk=bk, h=h: e.matmul(BK[bk][:, 256 * h:256 * h + 256], xnv[:, t_, :], pk0("WvT"), start=True, stop=False),
                      [*xn_t, *free[bk]], inc=False)
                tp = pe.op(lambda e, bk=bk, h=h: e.matmul(BK[bk][:, 256 * h:256 * h + 256], ONES[0:1, :], BV[:, :], start=False, stop=True),
                           [d_bv], inc=(h == 1))
            tv = act.op(lambda e, t2_=t2_, bk=bk: e.activation(VT[:, 2 * t2_:2 * t2_ + 2, :], BK[bk][:, :].rearrange("p (t f) -> p t f", t=2), ACT.Silu),
                        [tp, wbot_t[-1]])
            free[bk] = (tv,)
            v_t.append(tv)
        quad_t = []
        for c in range(4):
            def bc(i, c=c):
                return rp[:, i, 4 * c:4 * c + 4].unsqueeze(2).to_broadcast([128, 4, 128])

            def v3(ap, c=c):
                return ap[:, cc(c)].rearrange("p (l b) -> p l b", l=4)
            for o, dst in ((0, QQ), (4, QK)):
                ta = dve.op(lambda e, o=o, dst=dst, v3=v3, bc=bc: e.tensor_tensor(v3(dst), v3(BASE), bc(o), ALU.mult), [base_t[c], rope_t[1], *moe_end])
                tmp = RB[:, 4608 + 512 * c:5120 + 512 * c].rearrange("p (l b) -> p l b", l=4)
                tb = pool.op(lambda e, o=o, tmp=tmp, v3=v3, bc=bc: e.tensor_tensor(tmp, v3(BSW), bc(o + 1), ALU.mult),
                             [base_t[c], quad_t[-1] if quad_t else None, wbot_t[-1]])
                tb = pool.op(lambda e, o=o, tmp=tmp, bc=bc: e.tensor_tensor(tmp, tmp, bc(o + 2), ALU.add), [tb])
                quad_t.append(dve.op(lambda e, dst=dst, tmp=tmp, v3=v3: e.tensor_tensor(v3(dst), v3(dst), tmp, ALU.add), [ta, tb]))
        qqv = QQ.rearrange("p (m t) -> p t m", t=16)
        qkv = QK.rearrange("p (m t) -> p t m", t=16)
        KT = BASE.rearrange("p (t n) -> p t n", t=16)
        k_t = []
        for c in range(4):
            for i in range(4):
                t_ = 4 * c + i
                tp = pe.op(lambda e, t_=t_, i=i, c=c: e.matmul(BK[c % 2][:, bb_(i)], qkv[:, t_, :], qqv[:, t_, :], start=True, stop=True),
                           [quad_t[-1], quad_t[-2], *free[c % 2]], inc=(i == 3))
            ta = dve.op(lambda e, c=c: e.scalar_tensor_tensor(KT[:, 4 * c:4 * c + 4, :], BK[c % 2][:, :].rearrange("p (t n) -> p t n", t=4),
                                                              1.0 / 64, ATT[:, 0, :].unsqueeze(1).to_broadcast([128, 4, 128]), ALU.mult, ALU.add),
                        [tp, relm_t, quad_t[-1]])
            free[c % 2] = (ta,)
            k_t.append(dve.op(lambda e, c=c: e.scalar_tensor_tensor(KT[:, 4 * c:4 * c + 4, :], KT[:, 4 * c:4 * c + 4, :], 0.0,
                                                                    KT[:, 4 * c:4 * c + 4, :], ALU.max, ALU.mult), [ta]))
        g_t = []
        for c in range(4):
            for ch in range(2):
                bk = 2 + 2 * (c % 2) + ch
                for i in range(4):
                    t_ = 4 * c + i
                    tp = pe.op(lambda e, t_=t_, i=i, ch=ch, bk=bk: e.matmul(BK[bk][:, bb_(i)], VT[:, t_, 128 * ch:128 * ch + 128], KT[:, t_, :],
                                                                           start=True, stop=True), [k_t[c], v_t[-1], *free[bk]], inc=(i == 3))
                uv = U[ch].rearrange("p (m t) -> p t m", t=16)[:, 4 * c:4 * c + 4, :]
                tg = dve.op(lambda e, uv=uv, bk=bk: e.tensor_tensor(uv, uv, BK[bk][:, :].rearrange("p (t m) -> p t m", t=4), ALU.mult), [tp, u_t])
                free[bk] = (tg,)
                g_t.append(tg)
        x1_t = []
        for c in range(4):
            bk = 6 + c % 2
            for ch in range(2):
                tp = pe.op(lambda e, c=c, ch=ch, bk=bk: e.matmul(BK[bk][:, :], pk0("WoT")[:, 128 * ch:128 * ch + 128], U[ch][:, cc(c)],
                                                                 start=(ch == 0), stop=(ch == 1)), [g_t[-1], *free[bk]], inc=(ch == 1))
            tv = dve.op(lambda e, c=c, bk=bk: e.scalar_tensor_tensor(XT[:, cc(c)], BK[bk][:, :], col("bo"), XT[:, cc(c)], ALU.add, ALU.add),
                        [tp, xq_t[c]])
            free[bk] = (tv,)
            x1_t.append(tv)

        rb_free = [quad_t[-1], fw_t[-1], dn_t[lu], wbot_t[-1], t_sl]
        P16 = RB[:, :].bitcast(F16).rearrange("p (h n) -> p h n", h=2)
        p_ready = []
        for i in range(8):
            g = stage_load(A["w2"][:, 1024 * i:1024 * i + 1024], 1024)
            src = STG[:, g % 2, 0:1024]
            hi, lo = P16[:, 0, 1024 * i:1024 * i + 1024], P16[:, 1, 1024 * i:1024 * i + 1024]
            th = pool.op(lambda e, hi=hi, src=src: e.tensor_copy(hi, src), [d_stg[g], *rb_free])
            tl = pool.op(lambda e, hi=hi, lo=lo, src=src: e.tensor_tensor(lo, src, hi, ALU.subtract), [th])
            stg_free[g % 2] = tl
            p_ready.append(tl)

        part(3)
        LT = XF
        MX = QS
        RQ = sb("RQ", [128, 10])
        MG = RQ[:, 9:10]
        mg_t = dve.op(lambda e: e.memset(MG, MAGIC))

        def batch_mm(W, src, evac, waits, banks):
            toks = []
            for c in range(4):
                bk = banks[c % len(banks)]
                for i in range(4):
                    b = 4 * c + i
                    tp = pe.op(lambda e, b=b, i=i, bk=bk: e.matmul(BK[bk][:, bb_(i)], W[:, bb_(b)], src[:, bb_(b)], start=True, stop=True),
                               [*waits[c], *free[bk]], inc=(i == 3))
                tv = evac(c, BK[bk], tp)
                free[bk] = (tv,)
                toks.append(tv)
            return toks

        def lora_evac(c, bk, tp):
            return act.op(lambda e: e.activation(LT[:, cc(c)], bk[:, :], ACT.Identity, bias=col("b_base")), [tp, k_t[-1]])

        l_t = batch_mm(WEFF, XT, lora_evac, [[x1_t[c], weff_t[-1], k_t[-1]] for c in range(4)], [0, 1, 2, 3])

        def absmax(dst, src, after):
            return dve.op(lambda e: e.tensor_reduce(dst, src, X_AX, ALU.max, apply_absolute_value=True), after)

        def quant_scale(parts, k, after, unit=None):
            b0 = k - 60
            t = dve.op(lambda e: e.tensor_reduce(QS[:, 56 + b0:57 + b0], parts, X_AX, ALU.max), after)
            tp = pe.op(lambda e: e.transpose(BK[7][0:1, 0:128], QS[:, 56 + b0:57 + b0], pk1("ident")), [t, *free[7]])
            t = dve.op(lambda e: e.tensor_reduce(ROW[:, b0:b0 + 1], BK[7][0:1, 0:128], X_AX, ALU.max), [tp])
            tp = pe.op(lambda e: e.matmul(BK[7][:, 128:129], ONES[0:1, :], ROW[:, b0:b0 + 1], start=True, stop=True), [t])
            per = 1.0 / QMAX if unit is None else unit
            t = dve.op(lambda e: e.tensor_scalar(QS[:, k:k + 1], BK[7][:, 128:129], per, 1e-12, ALU.mult, ALU.max), [tp])
            free[7] = (t,)
            t = dve.op(lambda e: e.reciprocal(RQ[:, b0:b0 + 1], QS[:, k:k + 1]), [t])
            if unit is not None:
                t = dve.op(lambda e: e.tensor_scalar(RQ[:, b0:b0 + 1], RQ[:, b0:b0 + 1], unit, QMAX, ALU.mult, ALU.mult), [t])
            return t

        def step1(ap, k, after):
            return act.op(lambda e: e.activation(ap, ap, ACT.Identity, bias=MG, scale=RQ[:, k - 60:k - 59]), [*after, mg_t])

        def less_magic(ap, after):
            return dve.op(lambda e: e.tensor_scalar(ap, ap, MAGIC, None, ALU.subtract), after)

        mx = [absmax(MX[:, c:c + 1], LT[:, cc(c)], [l_t[c], fw_t[-1]]) for c in range(4)]
        s = quant_scale(MX[:, 0:4], 60, mx)
        lq_t = []
        for c in range(4):
            t = step1(LT[:, cc(c)], 60, [s])
            lq_t.append(dve.op(lambda e, c=c: e.tensor_scalar(LT[:, cc(c)], LT[:, cc(c)], MAGIC, QS[:, 60:61], ALU.subtract, ALU.mult), [t]))
        UP = [big(j) for j in range(3)]
        GT = [big(j) for j in range(3, 6)]
        TS = [WK[:, 0, :], WK[:, 1, :], QT[:, :]]
        npj = [0]

        def project(dst, wi, mx0, j):
            toks = []
            for c in range(4):
                bk = npj[0] % 7
                npj[0] += 1
                tp = pe.op(lambda e, c=c, bk=bk: e.matmul(BK[bk][:, :], FWT[:, 3 * wi + j, :], LT[:, cc(c)], start=True, stop=True),
                           [lq_t[c], fw_t[wi], *free[bk]])
                tv = act.op(lambda e, c=c, bk=bk: e.activation(dst[j][:, cc(c)], BK[bk][:, :], ACT.Copy), [tp, x1_t[-1]])
                free[bk] = (tv,)
                toks.append(absmax(MX[:, mx0 + 4 * j + c:mx0 + 4 * j + c + 1], dst[j][:, cc(c)], [tv]))
            return toks

        gm = [project(GT, 1, 12, j)[-1] for j in range(3)]
        s = quant_scale(MX[:, 12:24], 61, [gm[-1]])
        g1 = [step1(GT[j], 61, [s]) for j in range(3)]
        gq = [less_magic(GT[j], [g1[j]]) for j in range(3)]
        U2 = RQ[:, 5:6]
        U3 = RQ[:, 6:7]
        u2 = dve.op(lambda e: e.tensor_scalar(U2, QS[:, 61:62], 1.0 / 65536, 1.0 / QMAX, ALU.mult, ALU.mult), [s])
        sg, um = [], []
        for j in range(3):
            um.append(project(UP, 0, 0, j)[-1])
            sg.append(act.op(lambda e, j=j: e.activation(TS[j], GT[j], ACT.Sigmoid, scale=QS[:, 61:62]), [gq[j]]))
        s1 = [act.op(lambda e, j=j: e.activation(TS[j], TS[j], ACT.Identity, bias=MG, scale=65536.0), [sg[j]]) for j in range(3)]
        s_up = quant_scale(MX[:, 0:12], 62, [um[-1]])
        uq = [step1(UP[j], 62, [s_up]) for j in range(3)]
        g2m = []
        for j in range(3):
            t = dve.op(lambda e, j=j: e.tensor_scalar(TS[j], TS[j], MAGIC + 65535.0, MAGIC, ALU.min, ALU.subtract), [s1[j]])
            t = dve.op(lambda e, j=j: e.tensor_tensor(GT[j], GT[j], TS[j], ALU.mult), [t])
            g2m.append(absmax(MX[:, 24 + j:25 + j], GT[j], [t]))
        s2 = quant_scale(MX[:, 24:27], 63, [g2m[-1], u2], U2)
        u3 = dve.op(lambda e: e.tensor_scalar(U3, QS[:, 62:63], QS[:, 63:64], 1.0 / QMAX, ALU.mult, ALU.mult), [s2, s_up])
        uq = [less_magic(UP[j], [uq[j]]) for j in range(3)]
        g3 = [step1(GT[j], 63, [s2]) for j in range(3)]
        om = []
        for j in range(3):
            t = dve.op(lambda e, j=j: e.scalar_tensor_tensor(GT[j], GT[j], MAGIC, UP[j], ALU.subtract, ALU.mult), [g3[j], uq[j]])
            om.append(absmax(MX[:, 27 + j:28 + j], GT[j], [t]))
        s3 = quant_scale(MX[:, 27:30], 60, [om[-1], u3, lq_t[-1]], U3)
        oq = []
        for j in range(3):
            t = step1(GT[j], 60, [s3])
            oq.append(dve.op(lambda e, j=j: e.tensor_scalar(GT[j], GT[j], MAGIC, QS[:, 60:61], ALU.subtract, ALU.mult), [t]))
        x2_t = []
        for j in range(3):
            for c in range(4):
                tp = pe.op(lambda e, c=c, j=j: e.matmul(BK[c][:, :], FWT[:, 6 + j, :], GT[j][:, cc(c)], start=(j == 0), stop=(j == 2)),
                           [oq[j], fw_t[2], *(free[c] if j == 0 else ())])
                if j == 2:
                    tv = dve.op(lambda e, c=c: e.tensor_tensor(XT[:, cc(c)], XT[:, cc(c)], BK[c][:, :], ALU.add), [tp])
                    free[c] = (tv,)
                    x2_t.append(tv)

        part(4)
        X3, ZT, PT, VV = big(0), big(1), big(2), big(3)

        def mix_evac(c, bk, tp):
            return act.op(lambda e: e.activation(X3[:, cc(c)], bk[:, :], ACT.Identity, bias=col("cbias")), [tp, x2_t[-1]])

        x3_t = batch_mm(WBOT, XT, mix_evac, [[x2_t[c], wbot_t[-1]] for c in range(4)], [4, 5])
        x4_t = []
        for c in range(4):
            tp = pe.op(lambda e, c=c: e.matmul(BK[0][:, :], ATT[:, 2, :], X3[:, cc(c)], start=True, stop=True), [x3_t[c], a_t, *free[0]])
            z_t = act.op(lambda e, c=c: e.activation(ZT[:, cc(c)], BK[0][:, :], ACT.Copy), [tp])
            free[0] = (z_t,)
            for i in range(4):
                tp = pe.op(lambda e, c=c, i=i: e.matmul(BK[1][:, bb_(i)], X3[:, bb_(4 * c + i)], pk2("Wv1"), start=True, stop=True), [*free[1]], inc=(i == 3))
            vv = act.op(lambda e, c=c: e.activation(VV[:, cc(c)], BK[1][:, :], ACT.Copy), [tp])
            free[1] = (vv,)
            for i in range(4):
                tp = pe.op(lambda e, c=c, i=i: e.matmul(BK[2][:, bb_(i)], X3[:, bb_(4 * c + i)], ZT[:, bb_(4 * c + i)], start=True, stop=True),
                           [z_t, *free[2]], inc=(i == 3))
            tpp = dve.op(lambda e, c=c: e.tensor_tensor(PT[:, cc(c)].rearrange("p (b n) -> p b n", b=4), BK[2][:, :].rearrange("p (b n) -> p b n", b=4),
                                                        pk1("decT").unsqueeze(1).to_broadcast([128, 4, 128]), ALU.mult), [tp])
            free[2] = (tpp,)
            for i in range(4):
                tp = pe.op(lambda e, c=c, i=i: e.matmul(BK[3][:, bb_(i)], VV[:, bb_(4 * c + i)], PT[:, bb_(4 * c + i)], start=True, stop=True),
                           [vv, tpp, *free[3]], inc=(i == 3))
            tv = dve.op(lambda e, c=c: e.tensor_tensor(XT[:, cc(c)], XT[:, cc(c)], BK[3][:, :], ALU.add), [tp])
            free[3] = (tv,)
            x4_t.append(tv)

        part(5)
        xs = []
        for c in range(4):
            th = act.op(lambda e, c=c: e.activation(X16[:, 0, cc(c)], XT[:, cc(c)], ACT.Copy), [x4_t[c], *lq_t])
            xs.append(dve.op(lambda e, c=c: e.tensor_tensor(X16[:, 1, cc(c)], XT[:, cc(c)], X16[:, 0, cc(c)], ALU.subtract), [th]))
        X5 = big(4)
        SU = [WK[:, 0, 256 * i:256 * i + 256] for i in range(3)]
        HG = [WK[:, 1, 256 * i:256 * i + 256] for i in range(3)]
        H16B = big(5)[:, 0:768].bitcast(F16).rearrange("p (r h n) -> p r h n", r=3, h=2)
        eg, hid, hlo, dn2, x5_t = {}, {}, {}, {}, []
        r2 = {}

        def c_ap(b, part_, off):
            return C16[:, bass.ds(r2[b] + (part_ * 768 + off), 128)]

        def mlp_up(b):
            bk = b % 3
            def load(e, b=b):
                r2[b] = nc.tensor.value_load(EIX[0:1, 2, b:b + 1], min_val=0, max_val=7 * 1536)
            pe.op(load, [*c_ready, xs[b // 4], *free[bk]], inc=False)
            for q in range(4):
                for n, (wp, xp) in enumerate(((0, 0), (0, 1), (1, 0))):
                    tp = pe.op(lambda e, b=b, q=q, n=n, wp=wp, xp=xp, bk=bk: e.matmul(
                        BK[bk][:, bb_(q)], c_ap(b, wp, 128 * q), X16[:, xp, bb_(b)], start=(n == 0), stop=(n == 2)), inc=(q == 3 and n == 2))
            for q in range(2):
                ts = act.op(lambda e, b=b, q=q, bk=bk: e.activation(SU[b % 3][:, bb_(q)], BK[bk][:, bb_(q)], ACT.Silu, bias=BSEL[:, q, b:b + 1],
                                                                    scale=1.0 / WS), [tp, t_bsel, hid.get(b - 3), oq[-1]])
            for q in range(2):
                th = dve.op(lambda e, b=b, q=q, bk=bk: e.scalar_tensor_tensor(HG[b % 3][:, bb_(q)], BK[bk][:, bb_(2 + q)], BSEL[:, 2 + q, b:b + 1],
                                                                             SU[b % 3][:, bb_(q)], ALU.add, ALU.mult), [ts, hlo.get(b - 3)])
            hid[b] = th
            free[bk] = (th,)

        def mlp_mid(b):
            h16 = H16B[:, b % 3, :, :]
            th = act.op(lambda e, b=b, h16=h16: e.activation(h16[:, 0, :], HG[b % 3], ACT.Copy, scale=1.0 / WS), [hid[b], dn2.get(b - 3)])
            hlo[b] = dve.op(lambda e, b=b, h16=h16: e.scalar_tensor_tensor(h16[:, 1, :], HG[b % 3], 1.0 / WS, h16[:, 0, :], ALU.mult, ALU.subtract), [th])

        def mlp_down(b):
            h16 = H16B[:, b % 3, :, :]
            bk = 4 + (b // 4) % 2
            waits = [hlo[b], *(free[bk] if b % 4 == 0 else ())]
            for q in range(2):
                for n, (wp, xp) in enumerate(((0, 0), (0, 1), (1, 0))):
                    tp = pe.op(lambda e, b=b, q=q, n=n, wp=wp, xp=xp, bk=bk, h16=h16: e.matmul(
                        BK[bk][:, bb_(b % 4)], c_ap(b, wp, 512 + 128 * q), h16[:, xp, bb_(q)], start=(q == 0 and n == 0), stop=(q == 1 and n == 2)),
                        waits, inc=(q == 1 and n == 2))
                    waits = ()
            dn2[b] = tp
            if b % 4 == 3:
                for i in range(4):
                    bb2 = b - 3 + i
                    tv = act.op(lambda e, bb2=bb2, i=i, bk=bk: e.activation(X5[:, bb_(bb2)], BK[bk][:, bb_(i)], ACT.Identity,
                                                                            bias=BSEL[:, 4, bb2:bb2 + 1], scale=1.0 / WS), [tp])
                free[bk] = (tv,)
                x5_t.append(tv)

        for b in range(18):
            if b < 16:
                mlp_up(b)
            if 0 <= b - 1 < 16:
                mlp_mid(b - 1)
            if 0 <= b - 2:
                mlp_down(b - 2)

        part(6)
        XSQ = big(0)
        RT = WK[:, :, :].rearrange("p a n -> p (a n)")

        def r16(i):
            return RT[:, 256 * i:256 * i + 256].rearrange("p (t e) -> p t e", e=16)
        for c in range(4):
            tq = act.op(lambda e, c=c: e.activation(XSQ[:, cc(c)], X5[:, cc(c)], ACT.Square), [x5_t[c]])
        for t_ in range(16):
            pe.op(lambda e, t_=t_: e.matmul(BK[0][:, 16 * t_:16 * t_ + 16], X5[:, bb_(t_)], SNT, start=True, stop=True), [x5_t[t_ // 4], sn_t, *free[0]], inc=False)
            tp = pe.op(lambda e, t_=t_: e.matmul(BK[1][:, t_:t_ + 1], XSQ[:, bb_(t_)], ONES[:, 0:1], start=True, stop=True), [tq, *free[1]])
        NR = SM[:, 23, :]
        iota16 = pk1("iota16").rearrange("p (t e) -> p t e", e=16)

        def b16(ap):
            return ap.unsqueeze(2).to_broadcast([128, 16, 16])
        t = root(NR, BK[1][:, 0:16], SM[:, 34:36, :], 0.0, 1e-12, [tp])
        free[1] = (t,)
        t = dve.op(lambda e: e.reciprocal(NR, NR), [t])
        L, EQ, O1, L2, O2, HD, GA = (r16(i) for i in range(7))
        t = dve.op(lambda e: e.tensor_tensor(L, BK[0][:, 0:256].rearrange("p (t e) -> p t e", e=16), b16(NR), ALU.mult), [t, dn2[15], hlo[15]])
        free[0] = (t,)
        t = dve.op(lambda e: e.tensor_tensor(L, L, SIG.unsqueeze(1).to_broadcast([128, 16, 16]), ALU.subtract), [t, sg_t])
        M1, J1, M2, J2, RM, IN, SU1 = (SM[:, 24 + i, :] for i in range(7))
        t = first_max(dve, L, iota16, M1, EQ, J1, O1, [t])
        t = dve.op(lambda e: e.scalar_tensor_tensor(L2, O1, NEG, L, ALU.mult, ALU.add), [t])
        t = first_max(dve, L2, iota16, M2, EQ, J2, O2, [t])
        t = dve.op(lambda e: e.tensor_scalar(IN, M1, 0.0, None, ALU.is_le), [t])
        t = dve.op(lambda e: e.tensor_scalar(RM, M1, 0.0, None, ALU.max), [t])
        t = dve.op(lambda e: e.tensor_scalar(HD, L, 0.0, None, ALU.is_gt), [t])
        t = dve.op(lambda e: e.tensor_tensor(O1, O1, O2, ALU.add), [t])
        t = dve.op(lambda e: e.tensor_tensor(O1, O1, b16(IN), ALU.mult), [t])
        t = dve.op(lambda e: e.tensor_tensor(HD, HD, O1, ALU.add), [t])
        t = dve.op(lambda e: e.scalar_tensor_tensor(GA, L, 0.0, b16(RM), ALU.max, ALU.subtract), [t])
        t = act.op(lambda e: e.activation(GA, GA, ACT.Exp), [t])
        t = dve.op(lambda e: e.tensor_tensor(GA, GA, HD, ALU.mult), [t])
        t = dve.op(lambda e: e.tensor_reduce(SU1, GA, X_AX, ALU.add), [t])
        t = dve.op(lambda e: e.reciprocal(SU1, SU1), [t])
        t = dve.op(lambda e: e.tensor_tensor(GA, GA, b16(SU1), ALU.mult), [t])
        W48 = sb("W48", [128, 16, 48], BF16)
        t = dve.op(lambda e: e.tensor_copy(W48[:, :, 0:16], GA), [t])
        t = dve.op(lambda e: e.tensor_tensor(GA, GA, W48[:, :, 0:16], ALU.subtract), [t])
        t = dve.op(lambda e: e.tensor_copy(W48[:, :, 16:32], GA), [t])
        t = dve.op(lambda e: e.tensor_tensor(GA, GA, W48[:, :, 16:32], ALU.subtract), [t])
        t = dve.op(lambda e: e.tensor_copy(W48[:, :, 32:48], GA), [t])
        IDB = sb("IDB", [128, 128], BF16)
        tid = act.op(lambda e: e.activation(IDB[:, :], pk1("ident"), ACT.Copy), [d_pk1])
        W48T = QT[0:48, 0:1024].bitcast(BF16)
        SEL = QT[0:48, 1024:2048].bitcast(F16).rearrange("p (e n) -> p e n", e=16)
        d_sel = dma(SEL, A["sel"], [x2_t[-1]])
        w48_t = []
        for c in range(4):
            bv_ = BK[2 + c][:, :].bitcast(BF16)
            for i in range(4):
                tp = pe.op(lambda e, c=c, i=i, bv_=bv_: e.transpose(bv_[0:48, bb_(i)], W48[:, 4 * c + i, :], IDB[:, :]), [t, tid, *free[2 + c]], inc=(i == 3))
            tv = act.op(lambda e, c=c, bv_=bv_: e.activation(W48T[:, cc(c)], bv_[0:48, 0:512], ACT.Copy), [tp])
            free[2 + c] = (tv,)
            w48_t.append(tv)

        part(7)
        QP, KP, VP = big(0), big(1), big(2)
        OT = big(3)
        ZB = big(5)
        zf = [ZB[:, 512 * i:512 * i + 512] for i in range(4)]
        ZH = X16[:, :, :].rearrange("p a (r n) -> p r a n", n=512)
        zf_free, zh_free = [None] * 4, [None] * 4
        PP, VS = WK[:, 0, :], WK[:, 1, :]
        PTT = X5
        NM, SS, RS = (SM[:, 31 + i, :] for i in range(3))
        ACC = {"q": (0, 1, 2), "o": (3,)}
        qkv_t, vs_t, pt_t, o_t = {}, {}, {}, {}

        def chunk_bank(c, bk, mm, after):
            for i in range(4):
                tp = pe.op(lambda e, i=i: mm(e, BK[bk][:, bb_(i)], 4 * c + i), [*after, *free[bk]], inc=(i == 3))
            return tp

        def attend(c):
            sl = slice(4 * c, 4 * c + 4)

            def values():
                tp = chunk_bank(c, 4, lambda e, o, b: e.transpose(o, VP[:, bb_(b)], pk1("ident")), [qkv_t[c]])
                vs_t[c] = act.op(lambda e: e.activation(VS[:, cc(c)], BK[4][:, :], ACT.Copy), [tp, w48_t[-1]])
                free[4] = (vs_t[c],)

            def scores():
                tp = chunk_bank(c, 5, lambda e, o, b: e.matmul(o, QP[:, bb_(b)], KP[:, bb_(b)], start=True, stop=True), [qkv_t[c]])
                t = dve.op(lambda e: e.tensor_reduce(NM[:, sl], BK[5][:, :].rearrange("p (b n) -> p b n", b=4), X_AX, ALU.max), [tp])
                t = dve.op(lambda e: e.tensor_scalar(NM[:, sl], NM[:, sl], -ISC, None, ALU.mult), [t])
                for i in range(4):
                    b = 4 * c + i
                    te = act.op(lambda e, b=b, i=i: e.activation(PP[:, bb_(b)], BK[5][:, bb_(i)], ACT.Exp, bias=NM[:, b:b + 1], scale=ISC,
                                                                 accum_out=SS[:, b:b + 1]), [t])
                free[5] = (te,)
                pt_t[c] = te

            def norm():
                t = dve.op(lambda e: e.reciprocal(RS[:, sl], SS[:, sl]), [pt_t[c]])
                pp = PP[:, cc(c)].rearrange("p (b n) -> p b n", b=4)
                pt_t[c] = dve.op(lambda e: e.tensor_tensor(pp, pp, RS[:, sl].unsqueeze(2).to_broadcast([128, 4, 128]), ALU.mult), [t])

            def turn():
                tp = chunk_bank(c, 4, lambda e, o, b: e.transpose(o, PP[:, bb_(b)], pk1("ident")), [pt_t[c]])
                pt_t[c] = act.op(lambda e: e.activation(PTT[:, cc(c)], BK[4][:, :], ACT.Copy), [tp])
                free[4] = (pt_t[c],)

            def mix():
                tp = chunk_bank(c, 5, lambda e, o, b: e.matmul(o, VS[:, bb_(b)], PTT[:, bb_(b)], start=True, stop=True), [vs_t[c], pt_t[c]])
                o_t[c] = act.op(lambda e: e.activation(OT[:, cc(c)], BK[5][:, :], ACT.Copy), [tp])
                free[5] = (o_t[c],)
            return values, scores, norm, turn, mix

        def weigh(it):
            kind, c, e1 = it["id"]
            r, wb = it["n"] % 4, 6 + it["n"] % 2
            src, after = (X5, x_done) if kind == "q" else (OT, [o_t[c]])
            tp = pe.op(lambda e: e.matmul(BK[wb][:, :], SEL[:, e1, :], W48T[:, cc(c)], start=True, stop=True), [d_sel, w48_t[c], *free[wb]])
            tz = dve.op(lambda e: e.tensor_tensor(zf[r], src[:, cc(c)], BK[wb][:, :], ALU.mult), [tp, zf_free[r], *after])
            free[wb] = (tz,)
            it["hi"] = act.op(lambda e: e.activation(ZH[:, r, 0, :], zf[r], ACT.Copy), [tz, zh_free[r]])

        def weigh_lo(it):
            r = it["n"] % 4
            q = pool if it["pool"] else dve
            zf_free[r] = it["lo"] = q.op(lambda e: e.tensor_tensor(ZH[:, r, 1, :], zf[r], ZH[:, r, 0, :], ALU.subtract), [it["hi"]])

        def product(it):
            kind, c, e1 = it["id"]
            r = it["n"] % 4
            mats = (0, 1, 2) if kind == "q" else (3,)
            waits = [it["lo"], p_ready[-1]]
            for m, bk in zip(mats, ACC[kind]):
                for n, (wp, xp) in enumerate(((0, 0), (1, 0), (0, 1))):
                    wo = (m * 16 + e1) * 128
                    tk = pe.op(lambda e, wo=wo, bk=bk, wp=wp, xp=xp, n=n: e.matmul(
                        BK[bk][:, :], P16[:, wp, wo:wo + 128], ZH[:, r, xp, :], start=(e1 == 0 and n == 0), stop=(e1 == 15 and n == 2)),
                        [*waits, *(free[bk] if e1 == 0 else ())], inc=(n == 2))
                if e1 == 15 and kind == "q":
                    dst = (QP, KP, VP)[m]
                    qkv_t[c] = act.op(lambda e, bk=bk, dst=dst: e.activation(dst[:, cc(c)], BK[bk][:, :], ACT.Copy), [tk])
                    free[bk] = (qkv_t[c],)
                if e1 == 15 and kind == "o":
                    tv = dve.op(lambda e, bk=bk: e.tensor_tensor(XT[:, cc(c)], XT[:, cc(c)], BK[bk][:, :], ALU.add), [tk])
                    free[bk] = (tv,)
                    dma(out[:, cc(c)], XT[:, cc(c)], [tv], store=True)
            zh_free[r] = tk

        x_done = [x5_t[-1], tq, dn2[15], xs[-1]]
        seq, held = [("q", 0, e1) for e1 in range(16)], []
        for c in range(4):
            steps = [("do", c, i) for i in range(5)]
            nxt = [("q", c + 1, e1) for e1 in range(16)] if c < 3 else []
            n = 0
            while nxt or (c == 3 and (held or steps)):
                seq += nxt[:1] + held[:1]
                nxt, held = nxt[1:], held[1:]
                n += 1
                if n > 3 and steps:
                    seq.append(steps.pop(0))
                    if not steps:
                        held += [("o", c, e1) for e1 in range(16)]
        items = []
        for x in seq:
            if x[0] == "do":
                attend_step = attend(x[1])[x[2]]
                items[-1]["then"].append(attend_step)
            else:
                items.append({"id": x, "n": len(items), "then": [], "pool": False})
        LAG = 3
        for k in range(len(items) + LAG):
            if k < len(items):
                weigh(items[k])
            if 0 <= k - 1 < len(items):
                weigh_lo(items[k - 1])
            if k >= LAG:
                product(items[k - LAG])
            if k < len(items):
                for step in items[k]["then"]:
                    step()
        for t in stores:
            sp.op(lambda e, t=t: e.wait_ge(t.sem, t.val), inc=False)

        block = ctx.enter_context(nc.Block())
        block.sync(sp.run)
        block.gpsimd(pool.run)
        block.scalar(act.run)
        block.vector(dve.run)
        block.tensor(pe.run)


def layout(i):
    f = np.float32
    g = {k: np.asarray(v) for k, v in i.items()}
    A = {}
    A["xT"] = g["x"].reshape(N, D).T
    A["condB"] = np.broadcast_to(g["cond_8"][None], (128, 16, 8))

    def moe(gate, up, down):
        parts = [gate.reshape(128, 4, 128), up.reshape(128, 4, 128), down.reshape(4, 128, 128).transpose(1, 0, 2)]
        return np.stack(parts, 2).reshape(128, 1536)
    A["w0"] = np.stack([moe(g["L0_cond_shared_gate"], g["L0_cond_shared_up"], g["L0_cond_shared_down"])] +
                       [moe(g["L0_cond_skill_gate"][e], g["L0_cond_skill_up"][e], g["L0_cond_skill_down"][e]) for e in range(8)])
    sw = np.r_[64:128, 0:64]
    a = "L0_attn_"
    m = np.arange(128)
    l_, b_ = m // 8, m % 8
    idx = np.clip(63 + l_[:, None] - l_[None, :], 0, 126)
    p0 = {"WuT": g[a + "Wu"].T, "WvT": g[a + "Wv"].T, "WbT": g[a + "Wb"].T, "WbsT": g[a + "Wb"][sw].T,
          "WoT": g[a + "Wo"].T.reshape(2, 128, 128).transpose(1, 0, 2).reshape(128, 256),
          "As": g["L0_cond2_As"].reshape(128, 128), "BsT": g["L0_cond2_Bs"].transpose(0, 2, 1).reshape(128, 128),
          "WbaseT": g["L0_cond2_W_base"].T, "relb": g[a + "w_rel"][idx]}
    A["pk0"] = np.concatenate([p0[k] for k in PK0], 1)
    half = 64
    pos = np.arange(16, dtype=f)
    inv = (f(10000.0) ** (-np.arange(half, dtype=f) / f(half))).astype(f)
    ang = (pos[None, :] * inv[:, None]).astype(f)
    cos, sin = np.cos(ang).astype(f), np.sin(ang).astype(f)
    diff = m[None, :] - m[:, None]
    p1 = {"ident": np.eye(128, dtype=f),
          "decT": np.where(diff >= 0, f(0.96875) ** diff.astype(f), f(0)).astype(f),
          "amask": np.where((b_[:, None] == b_[None, :]) & (l_[:, None] <= l_[None, :]), f(0), f(-1e30)).astype(f),
          "cos": np.concatenate([cos, cos]), "sin": np.concatenate([-sin, sin]),
          "condR": np.repeat(g["cond_8"].T, 16, axis=0), "sim": g["L1_ffn_sim_matrix"],
          "iota16": np.broadcast_to(np.tile(np.arange(16, dtype=f) - 99, 16)[None], (128, 256)),
          "kmask": np.tile(np.eye(16, dtype=f), (8, 1))}
    A["pk1"] = np.concatenate([p1[k] for k in PK1], 1)
    A["pka"] = np.concatenate([np.broadcast_to(np.tile(np.arange(8, dtype=f) - 99, 16)[None], (128, 128)),
                               np.broadcast_to(g["L1_ffn_gates"][None], (128, 16))], 1)
    b = "L1_attn_weight_"
    A["pk2"] = np.concatenate([g[b + "q"].T, g[b + "k"].T, g[b + "v"]], 1)
    c = {"ln_g": g[a + "ln_g"], "ln_b": g[a + "ln_b"], "bu0": g[a + "bu"][:128], "bu1": g[a + "bu"][128:], "bb": g[a + "bb"],
         "bbs": g[a + "bb"][sw], "bo": g[a + "bo"], "b_base": g["L0_cond2_b_base"], "cbias": g["L1_cond_bias"], "theta": g["L1_attn_theta"]}
    for q in ("qq", "qk"):
        for w in "wb":
            c[q + w] = g[a + q + w]
            c[q + w + "s"] = g[a + q + w][sw]
    A["cols"] = np.stack([c[k] for k in COLS], 1)
    d = "L1_cond2_b_"
    A["c2b"] = np.stack([g[d + "up"][:, :128].T, g[d + "up"][:, 128:].T, g[d + "gate"][:, :128].T, g[d + "gate"][:, 128:].T, g[d + "down"].T], 1)
    A["bv"] = g[a + "bv"][None]
    A["fw"] = np.concatenate([g["L0_ffn_w_up"].reshape(3, 128, 128), g["L0_ffn_w_gate"].reshape(3, 128, 128),
                              g["L0_ffn_w_down"].reshape(128, 3, 128).transpose(1, 0, 2)]).transpose(1, 0, 2)
    A["l1w"] = g["L1_cond_weight"].reshape(8, 8, 16, 128).transpose(0, 2, 1, 3).reshape(128, 1024)
    A["l1m"] = np.tile(g["L1_cond_mask"].reshape(8, 16, 128).transpose(1, 0, 2).reshape(16, 1024), (8, 1))
    w = "L1_cond2_W_"
    per = [np.concatenate([g[w + "up"][e].T, g[w + "gate"][e].T, g[w + "down"][e].T.reshape(2, 128, 128).transpose(1, 0, 2).reshape(128, 256)], 1)
           for e in range(8)]
    A["w1"] = np.stack([np.concatenate(per[2 * k:2 * k + 2], 1) for k in range(4)])
    A["w2"] = np.concatenate([g["L1_ffn_" + k].transpose(1, 0, 2).reshape(128, 2048) for k in ("q_proj", "k_proj", "v_proj", "o_proj")], 1)
    A["sel"] = np.broadcast_to(np.tile(np.eye(16, dtype=np.float16), (3, 1))[:, :, None], (48, 16, 128))
    return {k: np.ascontiguousarray(v) for k, v in A.items()}


def kernel(**inputs):
    import concourse.bacc as bacc
    from concourse.bass_utils import run_bass_kernel_spmd

    nc = bacc.Bacc("TRN2", target_bir_lowering=False, num_devices=1)
    arrays = {f"in_{k}": v for k, v in layout(inputs).items()}
    A = {k[3:]: nc.dram_tensor(k, v.shape, mybir.dt.from_np(v.dtype), kind="ExternalInput").ap() for k, v in arrays.items()}
    out = nc.dram_tensor("out_0", (128, N), F32, kind="ExternalOutput").ap()
    program(nc, A, out)
    r = run_bass_kernel_spmd(nc, [arrays], core_ids=[0])
    return np.ascontiguousarray(r.results[0]["out_0"].T.reshape(NB, S, D))
```

```python
from contextlib import ExitStack

import numpy as np

import concourse.bass as bass
from concourse import mybir

F32 = mybir.dt.float32
F16 = mybir.dt.float16
BF16 = mybir.dt.bfloat16
I32 = mybir.dt.int32
I16 = mybir.dt.int16
U16 = mybir.dt.uint16
ALU = mybir.AluOpType
ACT = mybir.ActivationFunctionType
X_AX = mybir.AxisListType.X

NB, S, D = 16, 128, 128
N = NB * S
I0, E0 = 512, 8
WE = 3 * I0
H2 = 256
CE = 3 * H2
E1 = 16
WS = 256.0
AS = 16.0
MAGIC = 12582912.0
QMAX = 32767.0
NEG = -3.0e38
ISC = float(1.0 / np.sqrt(np.float32(D)))

COLS = ["ln_g", "ln_b", "bu0", "bu1", "bb", "bbs", "qqw", "qqb", "qkw", "qkb", "qqws", "qqbs", "qkws",
        "qkbs", "bo", "b_base", "cbias", "theta"]
CI = {n: i for i, n in enumerate(COLS)}
PK0 = {"WuT": (0, 256), "WvT": (256, 512), "WbT": (512, 640), "WbsT": (640, 768), "WoT": (768, 1024),
       "As": (1024, 1152), "BsT": (1152, 1280), "WbaseT": (1280, 1408), "relb": (1408, 1536)}
PK1 = {"ident": (0, 128), "decT": (128, 256), "amask": (256, 384), "cos": (384, 400), "sin": (400, 416),
       "condR": (416, 432), "sim": (432, 448), "iota16": (448, 704), "kmask": (704, 720)}
PK1N = 720
PKA = {"iota8": (0, 128), "gates": (128, 144)}
PK2 = {"WqT": (0, 128), "WkT": (128, 256), "Wv1": (256, 384)}


class Tok:
    def __init__(self, sem, val):
        self.sem, self.val = sem, val


class Queue:

    def __init__(self, new_sem, name):
        self.new_sem, self.name = new_sem, name
        self.todo, self.seen = [], {}
        self.part(0)

    def part(self, n):
        self.sem, self.val = self.new_sem(f"s_{self.name}{n}"), 0

    def op(self, fn, after=(), inc=True):
        for t in after:
            if t is not None and self.seen.get(t.sem, 0) < t.val:
                self.seen[t.sem] = t.val
                self.todo.append(lambda e, t=t: e.wait_ge(t.sem, t.val))
        if not inc:
            self.todo.append(fn)
            return None
        self.val += 1
        sem = self.sem
        self.todo.append(lambda e: fn(e).then_inc(sem, 1))
        return Tok(sem, self.val)

    def run(self, e):
        for f in self.todo:
            f(e)


def program(nc, A, out):
    with ExitStack() as ctx:
        def sb(name, shape, dt=F32):
            return ctx.enter_context(nc.sbuf_tensor(name, shape, dt))

        nsem = [0]

        def sem(name):
            nsem[0] += 1
            return ctx.enter_context(nc.semaphore(f"{name}_{nsem[0]}"))

        pe, act, dve, pool, sp = (Queue(sem, n) for n in ("pe", "act", "dve", "pool", "sp"))

        def part(n):
            for q in (pe, act, dve, pool):
                q.part(n)

        stores = []

        def dma(dst, src, after=(), q=None, store=False, last=None):
            q = q or sp
            s, v = (last.sem, last.val + 16) if last else (sem("d"), 16)
            for t in after:
                if t is not None:
                    q.op(lambda e, t=t: e.wait_ge(t.sem, t.val), inc=False)
            q.op(lambda e: e.dma_start(dst, src() if callable(src) else src).then_inc(s, 16), inc=False)
            t = Tok(s, v)
            if store:
                stores.append(t)
            return t

        BK = [ctx.enter_context(nc.psum_tensor(f"bk{i}", [128, 512], F32)) for i in range(8)]
        free = [() for _ in range(8)]

        RA = sb("RA", [128, 13824])
        RB = sb("RB", [128, 8192])
        RC = sb("RC", [128, 6144])
        STG = sb("STG", [128, 2, 1536])
        XT = sb("XT", [128, N])
        X16 = sb("X16", [128, 2, N], F16)
        QT = sb("QT", [128, N])
        WK = sb("WK", [128, 2, 2048])
        PK0T = sb("PK0T", [128, 1536])
        PK1T = sb("PK1T", [128, PK1N])
        PKAT = sb("PKAT", [128, 144])
        PK2T = sb("PK2T", [128, 384])
        COL = sb("COL", [128, len(COLS)])
        C2B = sb("C2B", [128, 5, 8])
        BV = sb("BV", [3, 256])
        ON3 = sb("ON3", [3, 128], BF16)
        BV3 = sb("BV3", [3, 4, 256], BF16)
        WEFF = sb("WEFF", [128, N])
        WBOT = sb("WBOT", [128, N])
        FW = RB[:, 6656:7808].rearrange("p (k n) -> p k n", k=9)
        FW16 = sb("FW16", [128, 2, 9, 128], F16)
        AW16 = sb("AW16", [128, 2, 640], F16)
        XH = WBOT[:, :].bitcast(F16).rearrange("p (h n) -> p h n", h=2)
        CONDB = sb("CONDB", [128, 16, 8])
        SM = sb("SM", [128, 40, 16])
        SL = RB[:, 1536:3072].rearrange("p (k n) -> p k n", k=12)
        ROPE = sb("ROPE", [128, 8, 16])
        ONESK = sb("ONESK", [128, 128])
        ONES = sb("ONES", [128, 128])
        ATT = sb("ATT", [128, 3, 128])
        WCOL = sb("WCOL", [128, 2, 16])
        EIX = sb("EIX", [128, 3, 16], I32)
        BSEL = sb("BSEL", [128, 5, 16])
        QS = sb("QS", [128, 64])
        ROW = sb("ROW", [1, 16])
        RQ = sb("RQ", [128, 10])

        def pk0(n):
            return PK0T[:, PK0[n][0]:PK0[n][1]]

        def pk1(n):
            return PK1T[:, PK1[n][0]:PK1[n][1]]

        def pka(n):
            return PKAT[:, PKA[n][0]:PKA[n][1]]

        def pk2(n):
            return PK2T[:, PK2[n][0]:PK2[n][1]]

        def col(n):
            return COL[:, CI[n]:CI[n] + 1]

        def cc(c):
            return slice(512 * c, 512 * c + 512)

        def bb_(b):
            return slice(128 * b, 128 * b + 128)

        def big(j):
            return RA[:, 2048 * j:2048 * j + 2048]

        def at(v, off):
            return bass.ds((v * 2 + 2 * off) // 2, 128)

        def root(dst, src, tmp, add, least, after):
            v, s = tmp
            t = dve.op(lambda e: e.tensor_scalar(v, src, add, None, ALU.add), after)
            t = act.op(lambda e: e.activation(s, v, ACT.Sqrt), [t])
            t = dve.op(lambda e: e.tensor_scalar(s, s, least, None, ALU.max), [t])
            t = dve.op(lambda e: e.reciprocal(dst, s), [t])
            t = dve.op(lambda e: e.tensor_tensor(dst, dst, v, ALU.mult), [t])
            t = dve.op(lambda e: e.tensor_tensor(dst, dst, s, ALU.add), [t])
            return dve.op(lambda e: e.tensor_scalar(dst, dst, 0.5, least, ALU.mult, ALU.max), [t])

        d_cond = dma(CONDB[:, :, :], A["condB"])
        d_pka = dma(PKAT[:, :], A["pka"], q=act)
        d_col = dma(COL[:, :], A["cols"], q=act)
        d_c2b = dma(C2B[:, :, :], A["c2b"], q=act)
        d_bv = dma(BV[:, :], A["bv"], q=act)
        slots = [STG[:, 0, :], STG[:, 1, :], WK[:, 0, 0:1536]] + [RC[:, 1536 * i:1536 * i + 1536] for i in range(4)]
        d_x, d_w = [], []
        d_sh = [dma(slots[0][:, 0:768], A["w0"][0][:, 0:768])]
        d_x.append(dma(XT[:, cc(0)], A["xT"][:, cc(0)]))
        d_sh.append(dma(slots[0][:, 768:1536], A["w0"][0][:, 768:1536]))
        d_x.append(dma(XT[:, cc(1)], A["xT"][:, cc(1)]))
        d_w.append(dma(slots[1], A["w0"][1]))
        d_x.append(dma(XT[:, cc(2)], A["xT"][:, cc(2)]))
        d_w.append(dma(slots[2], A["w0"][2]))
        d_x.append(dma(XT[:, cc(3)], A["xT"][:, cc(3)]))
        L1W = RB[:, 4608:5632]
        L1M = RB[:, 5632:6656]
        BSC = WBOT[:, :]
        KRF = RB[:, 7808:8064]

        c_ones = dve.op(lambda e: e.memset(ONES[:, :], 1.0))
        c_onesk = dve.op(lambda e: e.memset(ONESK[:, :], 1.0 / 128))

        iota8 = pka("iota8").rearrange("p (b e) -> p b e", e=8)

        def first_max(q, lg, iota, m, eq, ix, oh, after):
            nb, ne = lg.shape[1], lg.shape[2]
            t = q.op(lambda e: e.tensor_reduce(m, lg, X_AX, ALU.max), after)
            t = q.op(lambda e: e.tensor_tensor(eq, lg, m.unsqueeze(2).to_broadcast([128, nb, ne]), ALU.is_equal), [t])
            t = q.op(lambda e: e.tensor_tensor(eq, eq, iota, ALU.mult), [t])
            t = q.op(lambda e: e.tensor_reduce(ix, eq, X_AX, ALU.min), [t])
            return q.op(lambda e: e.tensor_tensor(oh, iota, ix.unsqueeze(2).to_broadcast([128, nb, ne]), ALU.is_equal), [t])

        def sl8(i):
            return SL[:, i, :].rearrange("p (b e) -> p b e", e=8)

        t = first_max(dve, CONDB[:, :, :], iota8, SM[:, 0, :], sl8(0), SM[:, 1, :], sl8(1), [d_cond, d_pka])
        oh1_t = t
        t = dve.op(lambda e: e.scalar_tensor_tensor(sl8(2), sl8(1), NEG, CONDB[:, :, :], ALU.mult, ALU.add), [t])
        t = first_max(dve, sl8(2), iota8, SM[:, 2, :], sl8(0), SM[:, 3, :], sl8(3), [t])
        t = dve.op(lambda e: e.tensor_scalar(SM[:, 1:4:2, :], SM[:, 1:4:2, :], -92.0, -99.0, ALU.min, ALU.max), [t])
        t = dve.op(lambda e: e.tensor_scalar(EIX[:, 0:2, :], SM[:, 1:4:2, :], 99.0, 3072.0, ALU.add, ALU.mult), [t])
        t_eix = dve.op(lambda e: e.tensor_scalar(EIX[:, 2, :], SM[:, 1, :], 99.0, 128.0, ALU.add, ALU.mult), [t])
        t = dve.op(lambda e: e.tensor_tensor(sl8(4), CONDB[:, :, :], SM[:, 0, :].unsqueeze(2).to_broadcast([128, 16, 8]),
                                             ALU.subtract), [t_eix])
        t2 = dve.op(lambda e: e.tensor_tensor(SM[:, 4, :], SM[:, 2, :], SM[:, 0, :], ALU.subtract), [t])
        W16 = RA[:, :].bitcast(F16)

        def split_hi(dst, src, after):
            return act.op(lambda e: e.activation(dst, src, ACT.Copy, scale=WS), after)

        x_lo, w_ready = [], []

        def split_x(c):
            th = act.op(lambda e: e.activation(X16[:, 0, cc(c)], XT[:, cc(c)], ACT.Copy), [d_x[c]])
            x_lo.append(dve.op(lambda e: e.tensor_tensor(X16[:, 1, cc(c)], XT[:, cc(c)], X16[:, 0, cc(c)], ALU.subtract), [th]))

        def split_shared(h):
            src = slots[0][:, 768 * h:768 * h + 768]
            o = 8 * 3072 + 768 * h
            th = split_hi(W16[:, o:o + 768], src, [d_sh[h]])
            return dve.op(lambda e: e.scalar_tensor_tensor(W16[:, o + 1536:o + 2304], src, WS, W16[:, o:o + 768], ALU.mult, ALU.subtract), [th])

        sh_ready = [split_shared(0)]
        split_x(0)
        t_e = act.op(lambda e: e.activation(sl8(5), sl8(4), ACT.Exp), [t2])
        t_e = act.op(lambda e: e.activation(SM[:, 5, :], SM[:, 4, :], ACT.Exp), [t_e])
        SIG = SM[:, 22, :]
        t = dve.op(lambda e: e.tensor_scalar(QS[:, 0:1], col("theta"), 0.0, None, ALU.mult), [d_col])
        t_th = act.op(lambda e: e.activation(QS[:, 1:2], QS[:, 0:1], ACT.Exp), [t])
        sh_ready.append(split_shared(1))
        split_x(1)

        late = {}

        chosen = [pool.op(lambda e, k=k: e.tensor_tensor(sl8(6 + k), sl8(1), C2B[:, k, :].unsqueeze(1).to_broadcast([128, 16, 8]), ALU.mult),
                          [oh1_t, d_c2b]) for k in range(5)]

        def routing():
            t = dve.op(lambda e: e.tensor_reduce(SM[:, 6, :], sl8(5), X_AX, ALU.add), [t_e])
            yield
            t = dve.op(lambda e: e.reciprocal(SM[:, 7, :], SM[:, 6, :]), [t])
            yield
            t = dve.op(lambda e: e.tensor_tensor(SM[:, 8, :], SM[:, 5, :], SM[:, 7, :], ALU.mult), [t])
            yield
            t = dve.op(lambda e: e.tensor_tensor(SM[:, 9, :], SM[:, 7, :], SM[:, 8, :], ALU.add), [t])
            yield
            t = dve.op(lambda e: e.reciprocal(SM[:, 9, :], SM[:, 9, :]), [t])
            yield
            t = dve.op(lambda e: e.tensor_tensor(SM[:, 10:12, :], SM[:, 7:9, :], SM[:, 9, :].unsqueeze(1).to_broadcast([128, 2, 16]),
                                                 ALU.mult), [t])
            yield
            t = dve.op(lambda e: e.tensor_scalar(SM[:, 12:14, :], SM[:, 10:12, :], 1.0 / 12, None, ALU.mult), [t])
            yield
            t = dve.op(lambda e: e.scalar_tensor_tensor(SM[:, 10:12, :], SM[:, 10:12, :], 1.0 - 1.0 / 12, SM[:, 12:14, :],
                                                        ALU.mult, ALU.add), [t])
            yield
            t = dve.op(lambda e: e.tensor_scalar(WCOL[:, :, :], SM[:, 10:12, :], 1.0 / WS, None, ALU.mult), [t])
            late["w"] = t
            yield
            for k in range(5):
                t = dve.op(lambda e, k=k: e.tensor_reduce(BSEL[:, k, :], sl8(6 + k), X_AX, ALU.add), [chosen[k]])
                yield
            late["sl"] = late["bsel"] = t

        regs = {}

        def load(g):
            _, v = nc.values_load_multi_w_load_instructions(EIX[0:1, 0:2, 4 * g:4 * g + 4], [mybir.EngineType.PE], min_val=0, max_val=7 * 3072, skip_runtime_bounds_check_because="held in range above")
            for j in range(2):
                for i in range(4):
                    regs[(4 * g + i, j)] = v[4 * j + i]

        slot_free = [sh_ready[1]] + [None] * 6

        def expert(e1):
            sl = (e1 + 1) % 7
            src = slots[sl]
            hi, lo = W16[:, e1 * 3072:e1 * 3072 + 1536], W16[:, e1 * 3072 + 1536:(e1 + 1) * 3072]
            th = split_hi(hi, src, [d_w[e1]])
            if e1 in (0, 2, 4, 6):
                t = pool.op(lambda e: e.tensor_scalar(src, src, WS, 1.0, ALU.mult, ALU.mult), [th])
                t = pool.op(lambda e: e.tensor_tensor(lo, src, hi, ALU.subtract), [t])
            else:
                t = dve.op(lambda e: e.scalar_tensor_tensor(lo, src, WS, hi, ALU.mult, ALU.subtract), [th])
            w_ready.append(t)
            slot_free[sl] = t

        def fetch(e1):
            sl = (e1 + 1) % 7
            d_w.append(dma(slots[sl], A["w0"][e1 + 1], [slot_free[sl]]))

        for e1 in range(2, 7):
            fetch(e1)
        order = [("sh", g, j) for g in range(4) for j in range(4)]
        for g in range(4):
            ex = [("ex", 4 * g + bi, s) for bi in range(4) for s in range(2)]
            if g:
                ex[6:6] = [("var", g - 1, 0)]
                ex[4:4] = [("mean", g - 1, 0)]
            order += ex
        nu = len(order)
        real = [k for k in range(nu) if order[k][0] in ("sh", "ex")]
        idx = {k: u for u, k in enumerate(real)}
        ge = [WK[:, 1, 512 * i:512 * i + 512] for i in range(3)]
        hf = [RB[:, 512 * i:512 * i + 512] for i in range(3)]
        H16 = RB[:, 3072:4608].bitcast(F16).rearrange("p (r h n) -> p r h n", r=3, h=2)
        SQ = WK[:, 0, :]
        LNV = SM[:, 14, :]
        up_t, ge_t, mul_t, hi_t, lo_t, dn_t = {}, {}, {}, {}, {}, {}
        pair_free = {}
        q_t, mean_t, var_t, xq_t = [None] * 4, {}, {}, {}

        def w_ap(kind, v, off, part):
            if kind == "sh":
                o = 8 * 3072 + part * 1536 + off
                return W16[:, o:o + 128]
            return W16[:, at(v, part * 1536 + off)]

        def up(k):
            kind, a, j = order[k]
            gb, ub = BK[2 * (k % 3)], BK[2 * (k % 3) + 1]
            for g in {0: (0, 1), 16: (2, 3)}.get(k, ()):
                pe.op(lambda e, g=g: load(g), [t_eix], inc=False)
            waits = [pair_free.get(k - 3), *([sh_ready[j // 2], x_lo[a]] if kind == "sh" else [*w_ready, *x_lo])]
            for half, bank in ((0, gb), (1, ub)):
                if kind == "sh":
                    tiles = [(j, slice(0, 512), slice(512 * a, 512 * a + 512))]
                else:
                    tiles = [(jj, slice(128 * jj, 128 * jj + 128), bb_(a)) for jj in range(4)]
                for jj, oc, xc in tiles:
                    for n, (wp, xp) in enumerate(((0, 0), (0, 1), (1, 0))):
                        last = half == 1 and n == 2 and oc.stop == 512

                        def mm(e, bank=bank, oc=oc, xc=xc, wp=wp, xp=xp, off=384 * jj + half * 128, n=n):
                            return e.matmul(bank[:, oc], w_ap(kind, regs.get((a, j)), off, wp), X16[:, xp, xc],
                                            start=(n == 0), stop=(n == 2))
                        tk = pe.op(mm, waits, inc=last)
                        waits = ()
            up_t[k] = tk

        def down(k):
            kind, a, j = order[k]
            g = a if kind == "sh" else a // 4
            bk = 6 + g % 2
            waits = [lo_t[k], *free[bk]]
            if kind == "sh":
                tiles = [(j, slice(0, 512), slice(0, 512))]
                begin, end = j == 0, j == 3
            else:
                tiles = [(jj, slice(128 * jj, 128 * jj + 128), bb_(a % 4)) for jj in range(4)]
                begin, end = j == 0, j == 1
            h16 = H16[:, idx[k] % 3, :, :]
            for jj, hc, oc in tiles:
                for n, (wp, xp) in enumerate(((0, 0), (0, 1), (1, 0))):
                    first = begin and n == 0 and hc.start == 0
                    final = end and n == 2 and hc.stop == 512

                    def mm(e, wp=wp, xp=xp, off=384 * jj + 256, hc=hc, oc=oc, first=first, final=final):
                        return e.matmul(BK[bk][:, oc], w_ap(kind, regs.get((a, j)), off, wp), h16[:, xp, hc],
                                        start=first, stop=final, skip_group_check=True)
                    tk = pe.op(mm, waits, inc=(n == 2 and hc.stop == 512))
                    waits = ()
            dn_t[idx[k]] = tk
            if kind == "sh" and end:
                q_t[g] = act.op(lambda e: e.activation(QT[:, cc(g)], BK[bk][:, :], ACT.Copy, scale=1.0 / WS), [tk])
                free[bk] = (q_t[g],)
            if kind == "ex" and end and a % 4 == 3:
                q_t[g] = dve.op(lambda e: e.scalar_tensor_tensor(QT[:, cc(g)], BK[bk][:, :], 1.0 / WS, QT[:, cc(g)], ALU.mult, ALU.add),
                                [tk, q_t[g]])
                free[bk] = (q_t[g],)
                xq_t[g] = dve.op(lambda e: e.tensor_tensor(XT[:, cc(g)], XT[:, cc(g)], QT[:, cc(g)], ALU.add), [q_t[g], x_lo[g]])

        def mean(c, bank, after):
            tp = pe.op(lambda e: e.matmul(bank[:, :], ONESK[:, :], QT[:, cc(c)], start=True, stop=True), [q_t[c], c_onesk, *after])
            td = dve.op(lambda e: e.tensor_tensor(QT[:, cc(c)], QT[:, cc(c)], bank[:, :], ALU.subtract), [tp, xq_t[c]])
            mean_t[c] = (td, act.op(lambda e: e.activation(SQ[:, cc(c)], QT[:, cc(c)], ACT.Square), [td, *w_ready]))
            return td

        def var(c, bank, after):
            for i in range(4):
                tp = pe.op(lambda e, i=i: e.matmul(bank[:, i:i + 1], SQ[:, bb_(4 * c + i)], ONESK[:, 0:1], start=True, stop=True),
                           [mean_t[c][1], *after], inc=(i == 3))
            if c == 2:
                tp = pe.op(lambda e: e.matmul(bank[:, 16:32], ONES[:, :], SM[:, 20, :], start=True, stop=True), [late["sn"], c_ones])
            var_t[c] = dve.op(lambda e: e.tensor_scalar(LNV[:, 4 * c:4 * c + 4], bank[:, 0:4], 1e-5, None, ALU.add), [tp])
            if c == 2:
                return dve.op(lambda e: e.tensor_copy(SM[:, 15, :], bank[:, 16:32]), [tp])
            return var_t[c]

        g_stg = [9]
        d_stg = {}
        stg_free = slot_free

        def loads():
            late["pk1"] = dma(PK1T[:, :], A["pk1"])
            late["pk0"] = dma(PK0T[:, :], A["pk0"])
            late["fw"] = dma(FW[:, :, :], A["fw"])
            late["l1"] = [dma(L1W, A["l1w"]), dma(L1M, A["l1m"])]
            late["pk2"] = dma(PK2T[:, :], A["pk2"])

        def stage_load(src, n):
            g = g_stg[0]
            d_stg[g] = dma(STG[:, g % 2, 0:n], src, [stg_free[g % 2]])
            g_stg[0] += 1
            return g

        KR = KRF.rearrange("p (b j) -> p b j", b=16)

        def prep_pool():
            late["l1p"] = pool.op(lambda e: e.tensor_tensor(L1W, L1W, L1M, ALU.mult), late["l1"])

        def prep_lora():
            condR = pk1("condR")
            late["bsc"] = dve.op(lambda e: e.scalar_tensor_tensor(
                BSC.rearrange("p (b o) -> p b o", b=16), pk0("BsT").unsqueeze(1).to_broadcast([128, 16, 128]), 2.0,
                condR.unsqueeze(2).to_broadcast([128, 16, 128]), ALU.mult, ALU.mult), [late["pk0"], late["pk1"]])
            late["kr"] = dve.op(lambda e: e.tensor_tensor(KR, pk1("kmask").unsqueeze(1).to_broadcast([128, 16, 16]),
                                                          condR.unsqueeze(2).to_broadcast([128, 16, 16]), ALU.mult))

        def prep_attn():
            w = PK0T[:, 0:640]
            t = act.op(lambda e: e.activation(AW16[:, 0, :], w, ACT.Copy, scale=AS), [late["pk0"]])
            late["aw"] = dve.op(lambda e: e.scalar_tensor_tensor(AW16[:, 1, :], w, AS, AW16[:, 0, :], ALU.mult, ALU.subtract), [t])

        FB = QS[:, 16:52]
        FR = SM[:, 36:39, :].rearrange("p a b -> p (a b)")[:, 0:36]
        fw3 = FW[:, :, :].rearrange("p t (k i) -> p (t k) i", i=32)

        def prep_fw(part_):
            if part_ == 0:
                t = dve.op(lambda e: e.tensor_reduce(FB, fw3, X_AX, ALU.max, apply_absolute_value=True), [late["fw"]])
                t = dve.op(lambda e: e.tensor_scalar(FB, FB, 1.0 / 7.0, 1e-12, ALU.mult, ALU.max), [t])
                t = dve.op(lambda e: e.reciprocal(FR, FB), [t])
            elif part_ == 1:
                t = dve.op(lambda e: e.tensor_tensor(fw3, fw3, FR.unsqueeze(2).to_broadcast([128, 36, 32]), ALU.mult), [late["fq"]])
            elif part_ == 2:
                t = dve.op(lambda e: e.tensor_scalar(fw3, fw3, MAGIC, MAGIC, ALU.add, ALU.subtract), [late["fq"]])
                t = dve.op(lambda e: e.tensor_scalar(fw3, fw3, -8.0, 7.0, ALU.max, ALU.min), [t])
            else:
                t = dve.op(lambda e: e.tensor_tensor(fw3, fw3, FB.unsqueeze(2).to_broadcast([128, 36, 32]), ALU.mult), [late["fq"]])
            late["fq"] = t

        def prep_bv():
            t = d_bv
            for i in range(3):
                t = dve.op(lambda e, i=i: e.tensor_copy(BV3[:, i, :], BV[:, :]), [t])
                if i < 2:
                    t = dve.op(lambda e, i=i: e.tensor_tensor(BV[:, :], BV[:, :], BV3[:, i, :], ALU.subtract), [t])
            late["on3"] = dve.op(lambda e: e.tensor_scalar(ON3[:, :], ONES[0:3, :], AS, None, ALU.mult), [c_ones])
            idt = pk1("ident")
            t = dve.op(lambda e: e.tensor_scalar(BV3[:, 3, :], BV3[:, 0, :], idt[0:3, 0:1], None, ALU.mult), [t, late["pk1"]])
            for i in (1, 2):
                t = dve.op(lambda e, i=i: e.scalar_tensor_tensor(BV3[:, 3, :], BV3[:, i, :], idt[0:3, i:i + 1], BV3[:, 3, :], ALU.mult, ALU.add), [t])
            late["bv"] = t

        def prep_theta():
            late["th"] = dve.op(lambda e: e.tensor_scalar(ATT[:, 1, :], pk2("WkT"), QS[:, 1:2], QS[:, 1:2], ALU.mult, ALU.mult), [t_th, late["pk2"]])
            late["sn"] = dve.op(lambda e: e.tensor_tensor(SM[:, 20, :], pk1("sim"), pk1("sim"), ALU.mult), [late["pk1"]])

        route = routing()
        side = {0: [lambda: split_x(2)], 1: [lambda: split_x(3)]}
        for e1, k in enumerate((2, 3, 5, 6, 8, 9, 11, 12)):
            side.setdefault(k, []).append(lambda e1=e1: expert(e1))
        side[3].append(lambda: fetch(7))
        side[16] = [loads]
        side[21] = [prep_pool]
        side[22] = [prep_lora]
        side[23] = [prep_attn]
        for i in range(4):
            side.setdefault(25 + i, []).append(lambda i=i: prep_fw(i))
        side.setdefault(30, []).append(prep_theta)
        side.setdefault(32, []).append(prep_bv)
        for k in range(nu + 3):
            if k < nu:
                kind, a, j = order[k]
                if kind in ("mean", "var"):
                    pair_free[k] = (mean if kind == "mean" else var)(a, BK[2 * (k % 3)], [pair_free.get(k - 3)])
                else:
                    u = idx[k]
                    r, gb, ub = u % 3, BK[2 * (k % 3)], BK[2 * (k % 3) + 1]
                    up(k)
                    ge_t[u] = act.op(lambda e, r=r, gb=gb: e.activation(ge[r], gb[:, :], ACT.Gelu_apprx_tanh, scale=1.0 / WS),
                                     [up_t[k], mul_t.get(u - 3)])
                    w = (1.0 / WS) if kind == "sh" else WCOL[:, j, a:a + 1]
                    mul_t[u] = dve.op(lambda e, r=r, w=w, ub=ub: e.scalar_tensor_tensor(hf[r], ge[r], w, ub[:, :], ALU.mult, ALU.mult),
                                      [ge_t[u], late.get("w") if kind == "ex" else None, lo_t.get(real[u - 3]) if u >= 3 else None])
                    pair_free[k] = mul_t[u]
            p = k - 1
            if p in idx:
                r = idx[p] % 3
                hi_t[p] = act.op(lambda e, r=r: e.activation(H16[:, r, 0, :], hf[r], ACT.Copy), [mul_t[idx[p]], dn_t.get(idx[p] - 3)])
                lo_t[p] = dve.op(lambda e, r=r: e.tensor_tensor(H16[:, r, 1, :], hf[r], H16[:, r, 0, :], ALU.subtract), [hi_t[p]])
            for fn in side.get(k, ()):
                fn()
            for _ in range(2):
                next(route, None)
            if k - 3 in idx:
                down(k - 3)
        lu = len(real) - 1
        moe_end = [dn_t[lu], q_t[3]]
        for i in range(6):
            free[i] = tuple(pair_free[nu - 1 - n] for n in range(3))
        d_pk0, d_pk1, d_pk2 = late["pk0"], late["pk1"], late["pk2"]

        part(1)
        weff_t = []

        def weff(c):
            tp = pe.op(lambda e: e.matmul(BK[2 + c % 2][:, :], pk0("As"), BSC[:, cc(c)], start=True, stop=True), [late["bsc"], *free[2 + c % 2]])
            tv = dve.op(lambda e: e.tensor_tensor(WEFF[:, cc(c)].rearrange("p (b o) -> p b o", b=4),
                                                  BK[2 + c % 2][:, :].rearrange("p (b o) -> p b o", b=4),
                                                  pk0("WbaseT").unsqueeze(1).to_broadcast([128, 4, 128]), ALU.add), [tp])
            free[2 + c % 2] = (tv,)
            weff_t.append(tv)

        wbot_t = []

        def wbot(o):
            bi = 4 + o % 2
            tp = pe.op(lambda e: e.matmul(BK[bi][:, 0:256], L1W[:, 128 * o:128 * o + 128], KRF, start=True, stop=True),
                       [late["l1p"], late["kr"], *free[bi]])
            tv = act.op(lambda e: e.activation(WBOT[:, :].rearrange("p (b o j) -> p b o j", b=16, o=8)[:, :, o, :],
                                               BK[bi][:, 0:256].rearrange("p (b j) -> p b j", b=16), ACT.Copy), [tp, quad_t[-1]])
            free[bi] = (tv,)
            wbot_t.append(tv)

        fw_t = []

        def fwt(i):
            for k in range(3):
                tp = pe.op(lambda e, k=k: e.transpose(BK[i][:, 128 * k:128 * k + 128], FW[:, 3 * i + k, :], pk1("ident")),
                           [late["fq"], *free[i]], inc=(k == 2))
            rows = BK[i][:, 0:384].rearrange("p (k n) -> p k n", k=3)
            hi, lo = (FW16[:, h, 3 * i:3 * i + 3, :] for h in range(2))
            tv = act.op(lambda e: e.activation(hi, rows, ACT.Copy, scale=WS), [tp])
            tv = dve.op(lambda e: e.scalar_tensor_tensor(lo, rows, WS, hi, ALU.mult, ALU.subtract), [tv])
            free[i] = (tv,)
            fw_t.append(tv)

        weff(0)
        free[0] = (mean(3, BK[0], free[0]),)
        weff(1)
        weff(2)
        weff(3)
        free[1] = (var(3, BK[1], free[1]),)
        NRM = SM[:, 34:36, :]
        LNS = NRM[:, 0, :]
        t = root(NRM, SM[:, 14:16, :], (SM[:, 16:18, :], SM[:, 18:20, :]), 0.0, 1e-12, [var_t[3]])
        t = dve.op(lambda e: e.reciprocal(NRM, NRM), [t])
        SNT = SM[:, 21, :]
        BSW = big(4)
        dT = big(0)
        xn_t = []
        warm = act.op(lambda e: e.activation(RQ[:, 8:9], ONES[:, 0:1], ACT.Silu), [c_ones])

        def rstd_mat(c):
            return dve.op(lambda e: e.tensor_tensor(BSW[:, cc(c)].rearrange("p (t n) -> p t n", t=4),
                                                    pk1("ident").unsqueeze(1).to_broadcast([128, 4, 128]),
                                                    LNS[:, 4 * c:4 * c + 4].unsqueeze(2).to_broadcast([128, 4, 128]), ALU.mult), [t, *moe_end])

        xh_t = []

        def xn_lo(c):
            xn_t.append(dve.op(lambda e: e.scalar_tensor_tensor(XH[:, 1, cc(c)], dT[:, cc(c)], col("ln_b"), XH[:, 0, cc(c)], ALU.add, ALU.subtract), [xh_t[c]]))

        diag_t = [rstd_mat(0), rstd_mat(1)]
        for c in range(4):
            bk = 2 + c % 2
            bsw_free = pe.op(lambda e, c=c, bk=bk: e.matmul(BK[bk][:, :], ONES[:, :], BSW[:, cc(c)], start=True, stop=True), [diag_t[c], c_ones, *free[bk]])
            tx = dve.op(lambda e, c=c, bk=bk: e.scalar_tensor_tensor(dT[:, cc(c)], QT[:, cc(c)], col("ln_g"), BK[bk][:, :], ALU.mult, ALU.mult),
                        [bsw_free, mean_t[c][1], *moe_end])
            free[bk] = (tx,)
            xh_t.append(act.op(lambda e, c=c: e.activation(XH[:, 0, cc(c)], dT[:, cc(c)], ACT.Identity, bias=col("ln_b")), [tx, weff_t[-1]]))
            if c < 2:
                diag_t.append(rstd_mat(c + 2))
            if c > 0:
                xn_lo(c - 1)
        xn_lo(3)
        sn_t = dve.op(lambda e: e.tensor_tensor(SNT, pk1("sim"), NRM[:, 1, :], ALU.mult), [t])
        def prep_rest():
            for i in range(3):
                fwt(i)
            tp = pe.op(lambda e: e.matmul(BK[6][:, 0:128], pk2("WqT"), ATT[:, 1, :], start=True, stop=True), [late["th"], *free[6]])
            a_t = act.op(lambda e: e.activation(ATT[:, 2, :], BK[6][:, 0:128], ACT.Copy), [tp])
            free[6] = (a_t,)
            late["a"] = a_t

        rp = ROPE
        cosT, sinT = pk1("cos"), pk1("sin")
        rope_t = []
        for i, q in enumerate(("qq", "qk")):
            o = 4 * i
            pool.op(lambda e, q=q, o=o: e.tensor_scalar(rp[:, o, :], cosT, col(q + "w"), None, ALU.mult), [d_pk1, d_col])
            pool.op(lambda e, q=q, o=o: e.tensor_scalar(rp[:, o + 1, :], sinT, col(q + "ws"), None, ALU.mult))
            ta = pool.op(lambda e, q=q, o=o: e.tensor_scalar(rp[:, o + 2, :], cosT, col(q + "b"), None, ALU.mult))
            tb = pool.op(lambda e, q=q, o=o: e.tensor_scalar(rp[:, o + 3, :], sinT, col(q + "bs"), None, ALU.mult))
            rope_t.append(pool.op(lambda e, o=o: e.tensor_tensor(rp[:, o + 2, :], rp[:, o + 2, :], rp[:, o + 3, :], ALU.add), [tb]))
        relm_t = pool.op(lambda e: e.tensor_tensor(ATT[:, 0, :], pk0("relb"), pk1("amask"), ALU.add), [d_pk0, d_pk1])

        part(2)
        _, U0, U1, BASE, _, QQ = (big(j) for j in range(6))
        XF = X16[:, :, :].rearrange("p a n -> p (a n)").bitcast(F32)
        QK = XF
        VT = WK[:, :, :].rearrange("p a n -> p (a n)").rearrange("p (t f) -> p t f", t=16)
        U = [U0, U1]
        base_t, quad_t = [], []

        cos_t = {}

        def rope_cos(c):
            for l in range(4 * c, 4 * c + 4):
                for o, dst in ((0, QQ), (4, QK)):
                    cos_t[l, o] = pool.op(lambda e, l=l, o=o, dst=dst: e.tensor_scalar(dst[:, bb_(l)], BASE[:, bb_(l)], rp[:, o, l:l + 1], rp[:, o + 2, l:l + 1],
                                                                                     ALU.mult, ALU.add), [base_t[c][0], rope_t[1], *moe_end])

        def rope_sin(c):
            for o, dst in ((0, QQ), (4, QK)):
                for l in range(4 * c, 4 * c + 4):
                    quad_t.append(dve.op(lambda e, o=o, dst=dst, l=l: e.scalar_tensor_tensor(
                        dst[:, bb_(l)], BSW[:, bb_(l)], rp[:, o + 1, l:l + 1], dst[:, bb_(l)], ALU.mult, ALU.add),
                        [cos_t[l, o], *base_t[c][1:]]))

        SPLIT = ((0, 0), (1, 0), (0, 1))
        for w, b, dst in ((512, "bb", BASE), (0, "bu0", U0), (128, "bu1", U1)):
            for c in range(4):
                bk = 4 + c
                for n, (wp, xp) in enumerate(SPLIT):
                    tp = pe.op(lambda e, c=c, w=w, bk=bk, n=n, wp=wp, xp=xp: e.matmul(BK[bk][:, :], AW16[:, wp, w:w + 128], XH[:, xp, cc(c)],
                                                                                      start=(n == 0), stop=(n == 2)),
                               [xn_t[c], late["aw"], *free[bk]], inc=(n == 2))
                tv = act.op(lambda e, c=c, b=b, dst=dst, bk=bk: e.activation(dst[:, cc(c)], BK[bk][:, :], ACT.Silu, bias=col(b), scale=1.0 / AS), [tp])
                free[bk] = (tv,)
                if dst is BASE:
                    base_t.append([tv, dma(BSW[0:64, cc(c)], BASE[64:128, cc(c)], [tv, bsw_free]), dma(BSW[64:128, cc(c)], BASE[0:64, cc(c)])])
                elif dst is U0:
                    rope_cos(c)
                    if c:
                        rope_sin(c - 1)
            if dst is BASE:
                prep_rest()
            elif dst is U0:
                rope_sin(3)
        u_t = tv
        xnv = [XH[:, h, :].rearrange("p (m t) -> p t m", t=16) for h in range(2)]
        v_t = []
        for t2_ in range(8):
            bk = t2_ % 4
            for h in range(2):
                t_ = 2 * t2_ + h
                for n, (wp, xp) in enumerate(SPLIT):
                    pe.op(lambda e, t_=t_, bk=bk, h=h, n=n, wp=wp, xp=xp: e.matmul(BK[bk][:, 256 * h:256 * h + 256], xnv[xp][:, t_, :], AW16[:, wp, 256:512],
                                                                                   start=(n == 0), stop=False), [*xn_t, *free[bk]], inc=False)
                tp = pe.op(lambda e, bk=bk, h=h: e.matmul(BK[bk][:, 256 * h:256 * h + 256], ON3[:, :], BV3[:, 3, :], start=False, stop=True),
                           [late["bv"], late["on3"]], inc=(h == 1))
            tv = act.op(lambda e, t2_=t2_, bk=bk: e.activation(VT[:, 2 * t2_:2 * t2_ + 2, :], BK[bk][:, :].rearrange("p (t f) -> p t f", t=2), ACT.Silu, scale=1.0 / AS),
                        [tp, mean_t[3][1], var_t[3]])
            free[bk] = (tv,)
            v_t.append(tv)
        qqv = QQ.rearrange("p (m t) -> p t m", t=16)
        qkv = QK.rearrange("p (m t) -> p t m", t=16)
        KT = BASE.rearrange("p (t n) -> p t n", t=16)
        k_t = []
        for c in range(4):
            for i in range(4):
                t_ = 4 * c + i
                tp = pe.op(lambda e, t_=t_, i=i, c=c: e.matmul(BK[c % 2][:, bb_(i)], qkv[:, t_, :], qqv[:, t_, :], start=True, stop=True),
                           [quad_t[-1], quad_t[-2], *free[c % 2]], inc=(i == 3))
            ta = dve.op(lambda e, c=c: e.scalar_tensor_tensor(KT[:, 4 * c:4 * c + 4, :], BK[c % 2][:, :].rearrange("p (t n) -> p t n", t=4),
                                                              1.0 / 64, ATT[:, 0, :].unsqueeze(1).to_broadcast([128, 4, 128]), ALU.mult, ALU.add),
                        [tp, relm_t, quad_t[-1]])
            free[c % 2] = (ta,)
            k_t.append(dve.op(lambda e, c=c: e.scalar_tensor_tensor(KT[:, 4 * c:4 * c + 4, :], KT[:, 4 * c:4 * c + 4, :], 0.0,
                                                                    KT[:, 4 * c:4 * c + 4, :], ALU.max, ALU.mult), [ta]))
        g_t = []
        for c in range(4):
            for ch in range(2):
                bk = 2 + 2 * (c % 2) + ch
                for i in range(4):
                    t_ = 4 * c + i
                    tp = pe.op(lambda e, t_=t_, i=i, ch=ch, bk=bk: e.matmul(BK[bk][:, bb_(i)], VT[:, t_, 128 * ch:128 * ch + 128], KT[:, t_, :],
                                                                           start=True, stop=True), [k_t[c], v_t[-1], *free[bk]], inc=(i == 3))
                uv = U[ch].rearrange("p (m t) -> p t m", t=16)[:, 4 * c:4 * c + 4, :]
                tg = dve.op(lambda e, uv=uv, bk=bk: e.tensor_tensor(uv, uv, BK[bk][:, :].rearrange("p (t m) -> p t m", t=4), ALU.mult), [tp, u_t])
                free[bk] = (tg,)
                g_t.append(tg)
        x1_t = []
        for c in range(4):
            bk = 6 + c % 2
            for ch in range(2):
                tp = pe.op(lambda e, c=c, ch=ch, bk=bk: e.matmul(BK[bk][:, :], pk0("WoT")[:, 128 * ch:128 * ch + 128], U[ch][:, cc(c)],
                                                                 start=(ch == 0), stop=(ch == 1)), [g_t[-1], *free[bk]], inc=(ch == 1))
            tv = dve.op(lambda e, c=c, bk=bk: e.scalar_tensor_tensor(XT[:, cc(c)], BK[bk][:, :], col("bo"), XT[:, cc(c)], ALU.add, ALU.add),
                        [tp, xq_t[c]])
            free[bk] = (tv,)
            x1_t.append(tv)

        PASSES = ((0, 0), (0, 1), (1, 0))
        part(3)
        LT = XF
        MX = QS
        def batch_mm(W, src, evac, waits, banks):
            toks = []
            for c in range(4):
                bk = banks[c % len(banks)]
                for i in range(4):
                    b = 4 * c + i
                    tp = pe.op(lambda e, b=b, i=i, bk=bk: e.matmul(BK[bk][:, bb_(i)], W[:, bb_(b)], src[:, bb_(b)], start=True, stop=True),
                               [*waits[c], *free[bk]], inc=(i == 3))
                tv = evac(c, BK[bk], tp)
                free[bk] = (tv,)
                toks.append(tv)
            return toks

        def lora_evac(c, bk, tp):
            return act.op(lambda e: e.activation(LT[:, cc(c)], bk[:, :], ACT.Identity, bias=col("b_base")), [tp, k_t[-1]])

        l_t = batch_mm(WEFF, XT, lora_evac, [[x1_t[c], weff_t[-1], k_t[-1]] for c in range(4)], [0, 1, 2, 3])

        def absmax(dst, src, after):
            return dve.op(lambda e: e.tensor_reduce(dst, src, X_AX, ALU.max, apply_absolute_value=True), after)

        for o in range(4):
            wbot(o)

        def quant_stages(parts, k, after, unit=None):
            bk = 7
            b0 = k - 60
            t = dve.op(lambda e: e.tensor_reduce(QS[:, 56 + b0:57 + b0], parts, X_AX, ALU.max), after)
            tp = pe.op(lambda e: e.transpose(BK[bk][0:1, 0:128], QS[:, 56 + b0:57 + b0], pk1("ident")), [t, *free[bk]])
            yield None
            t = dve.op(lambda e: e.tensor_reduce(ROW[:, b0:b0 + 1], BK[bk][0:1, 0:128], X_AX, ALU.max), [tp])
            tp = pe.op(lambda e: e.matmul(BK[bk][:, 128:129], ONES[0:1, :], ROW[:, b0:b0 + 1], start=True, stop=True), [t])
            yield None
            per = 1.0 / QMAX if unit is None else unit
            t = dve.op(lambda e: e.tensor_scalar(QS[:, k:k + 1], BK[bk][:, 128:129], per, 1e-12, ALU.mult, ALU.max), [tp])
            free[bk] = (t,)
            t = dve.op(lambda e: e.reciprocal(RQ[:, b0:b0 + 1], QS[:, k:k + 1]), [t])
            if unit is not None:
                t = dve.op(lambda e: e.tensor_scalar(RQ[:, b0:b0 + 1], RQ[:, b0:b0 + 1], unit, QMAX, ALU.mult, ALU.mult), [t])
            yield t

        def quant_scale(*args):
            return [*quant_stages(*args)][-1]

        def steps16(dst, src, k, after):
            return act.op(lambda e: e.activation(dst, src, ACT.Identity, scale=RQ[:, k - 60:k - 59]), after)

        def steps16v(dst, src, k, after):
            return dve.op(lambda e: e.tensor_scalar(dst, src, RQ[:, k - 60:k - 59], None, ALU.mult), after)

        mx = [absmax(MX[:, c:c + 1], LT[:, cc(c)], [l_t[c], fw_t[-1]]) for c in range(4)]
        stages = quant_stages(MX[:, 0:4], 60, mx)
        next(stages)
        for o in range(4, 6):
            wbot(o)
        for o in range(6, 8):
            wbot(o)
        next(stages)
        s = next(stages)
        rb_free = [quad_t[-1], fw_t[-1], dn_t[lu], wbot_t[-1], late["sl"]]
        P16 = RB[:, :].bitcast(F16).rearrange("p (h n) -> p h n", h=2)
        p_ready = []
        for i in range(8):
            g = stage_load(A["w2"][:, 1024 * i:1024 * i + 1024], 1024)
            src = STG[:, g % 2, 0:1024]
            hi, lo = P16[:, 0, 1024 * i:1024 * i + 1024], P16[:, 1, 1024 * i:1024 * i + 1024]
            th = pool.op(lambda e, hi=hi, src=src: e.tensor_scalar(hi, src, 1.0, 1.0, ALU.mult, ALU.mult), [d_stg[g], *rb_free])
            tl = pool.op(lambda e, hi=hi, lo=lo, src=src: e.tensor_tensor(lo, src, hi, ALU.subtract), [th])
            stg_free[g % 2] = tl
            p_ready.append(tl)
        SLW = RQ[:, 4:5]
        sl_t = dve.op(lambda e: e.tensor_scalar(SLW, QS[:, 60:61], 1.0 / WS, None, ALU.mult), [s])
        lq_t = []
        L16 = QT[:, 0:1024].bitcast(I16)
        LH = [WK[:, 0, 1024 * i:1024 * i + 1024].bitcast(F16) for i in range(2)]
        for c in range(4):
            t = steps16(L16[:, cc(c)], LT[:, cc(c)], 60, [s, x1_t[-1]])
            t = dve.op(lambda e, c=c: e.tensor_copy(LH[0][:, cc(c)], L16[:, cc(c)]), [t])
            lq_t.append(dve.op(lambda e, c=c: e.tensor_tensor(LH[1][:, cc(c)], L16[:, cc(c)], LH[0][:, cc(c)], ALU.subtract), [t]))
        UP = [big(j) for j in range(3)]
        GT = [big(j) for j in range(3, 6)]
        G16 = [WK[:, 0, 0:1024].bitcast(I16), WK[:, 0, 1024:2048].bitcast(I16), WK[:, 1, 0:1024].bitcast(I16)]
        S16 = [WK[:, 1, 1024:2048].bitcast(U16), QT[:, 0:1024].bitcast(U16), QT[:, 1024:2048].bitcast(U16)]
        U16Q = [RC[:, 1024 * j:1024 * j + 1024].bitcast(I16) for j in range(3)]
        npj = [0]

        def project(dst, wi, mx0, j):
            toks = []
            for c in range(4):
                bk = npj[0] % 7
                npj[0] += 1
                for n, (wp, xp) in enumerate(PASSES):
                    tp = pe.op(lambda e, c=c, bk=bk, n=n, wp=wp, xp=xp: e.matmul(BK[bk][:, :], FW16[:, wp, 3 * wi + j, :], LH[xp][:, cc(c)],
                                                                                 start=(n == 0), stop=(n == 2)),
                               [lq_t[c], fw_t[wi], *free[bk]], inc=(n == 2))
                tv = act.op(lambda e, c=c, bk=bk: e.activation(dst[j][:, cc(c)], BK[bk][:, :], ACT.Identity, scale=SLW), [tp, sl_t, x1_t[-1]])
                toks.append(absmax(MX[:, mx0 + 4 * j + c:mx0 + 4 * j + c + 1], dst[j][:, cc(c)], [tv]))
                free[bk] = (tv,)
            return tv, toks[-1]

        um = [project(UP, 0, 0, j) for j in range(3)]
        gm = [project(GT, 1, 12, j) for j in range(3)]
        sg_t = act.op(lambda e: e.activation(SIG, pka("gates"), ACT.Sigmoid), [d_pka])
        s = quant_scale(MX[:, 12:24], 61, [gm[-1][1]])
        U2 = RQ[:, 5:6]
        U3 = RQ[:, 6:7]
        u2 = dve.op(lambda e: e.tensor_scalar(U2, QS[:, 61:62], 1.0 / 65536, 1.0 / QMAX, ALU.mult, ALU.mult), [s])

        def product_of(dst, a, b, after):
            return dve.op(lambda e: e.tensor_tensor(dst, a, b, ALU.mult), after)

        pieces = [(0, slice(0, 1024)), (0, slice(1024, 2048)), (1, slice(0, 2048)), (2, slice(0, 2048))]
        gq, sq, g2m = [], [], []
        for i, (j, h) in enumerate(pieces):
            gq.append(steps16v(G16[j][:, h], GT[j][:, h], 61, [s, gm[j][0], lq_t[-1]]))
            t = act.op(lambda e, j=j, h=h: e.activation(GT[j][:, h], G16[j][:, h], ACT.Sigmoid, scale=QS[:, 61:62]), [gq[i]])
            sq.append(act.op(lambda e, j=j, h=h: e.activation(S16[j][:, h], GT[j][:, h], ACT.Copy, scale=65536.0), [t, lq_t[-1]]))
        up_scale = quant_stages(MX[:, 0:12], 62, [um[-1][1]])
        next(up_scale)
        for i, (j, h) in enumerate(pieces):
            t = product_of(GT[j][:, h], G16[j][:, h], S16[j][:, h], [sq[i]])
            if i == 0:
                next(up_scale)
            g2m.append(absmax(MX[:, 24 + i:25 + i], GT[j][:, h], [t]))
            if i == 0:
                s_up = next(up_scale)
                uq = {k: steps16(U16Q[k], UP[k], 62, [s_up, um[k][0], *w_ready]) for k in range(3)}
        s2 = quant_scale(MX[:, 24:28], 63, [g2m[-1], u2], U2)
        u3 = dve.op(lambda e: e.tensor_scalar(U3, QS[:, 62:63], QS[:, 63:64], 1.0 / QMAX, ALU.mult, ALU.mult), [s2, s_up])
        g3 = [(steps16 if i else steps16v)(G16[j][:, h], GT[j][:, h], 63, [s2]) for i, (j, h) in enumerate(pieces)]
        ot, om = [], []
        for i, (j, h) in enumerate(pieces):
            ot.append(product_of(GT[j][:, h], G16[j][:, h], U16Q[j][:, h], [g3[i], uq[j]]))
            om.append(absmax(MX[:, 30 + i:31 + i], GT[j][:, h], [ot[i]]))
        s3 = quant_scale(MX[:, 30:34], 60, [om[-1], u3, lq_t[-1]], U3)
        sd_t = dve.op(lambda e: e.tensor_scalar(SLW, QS[:, 60:61], 1.0 / WS, None, ALU.mult), [s3])
        OH = [[UP[j][:, 1024 * i:1024 * i + 1024].bitcast(F16) for i in range(2)] for j in range(3)]
        x2_t, out_t, o16 = [], [], {}
        for j in range(3):
            for c in range(4):
                o16[j, c] = steps16(G16[j][:, cc(c)], GT[j][:, cc(c)], 60, [s3])
        for j in range(3):
            for c in range(4):
                t = dve.op(lambda e, c=c, j=j: e.tensor_copy(OH[j][0][:, cc(c)], G16[j][:, cc(c)]), [o16[j, c]])
                t = dve.op(lambda e, c=c, j=j: e.tensor_tensor(OH[j][1][:, cc(c)], G16[j][:, cc(c)], OH[j][0][:, cc(c)], ALU.subtract), [t])
                for n, (wp, xp) in enumerate(PASSES):
                    tp = pe.op(lambda e, c=c, j=j, n=n, wp=wp, xp=xp: e.matmul(BK[c][:, :], FW16[:, wp, 6 + j, :], OH[j][xp][:, cc(c)],
                                                                              start=(j == 0 and n == 0), stop=(j == 2 and n == 2)),
                               [t, fw_t[2], *(free[c] if j == 0 else ())], inc=(n == 2))
                if j == 2:
                    oq = [t]
                    out_t.append(tp)
        for c in range(4):
            tv = dve.op(lambda e, c=c: e.scalar_tensor_tensor(XT[:, cc(c)], BK[c][:, :], SLW, XT[:, cc(c)], ALU.mult, ALU.add), [out_t[c], sd_t])
            free[c] = (tv,)
            x2_t.append(tv)
        C2W = [WEFF[:, CE * i:CE * i + CE] for i in range(2)] + [PK0T[:, CE * i:CE * i + CE] for i in range(2)]
        C2W += [STG[:, i // 2, CE * (i % 2):CE * (i % 2) + CE] for i in range(4)] + [RC[:, CE * i:CE * i + CE] for i in range(8)]
        r2, d_c2w = {}, {}

        def load2(e):
            _, v = nc.values_load_multi_w_load_instructions(EIX[0:1, 2, :], [mybir.EngineType.SP], min_val=0, max_val=7 * 128, skip_runtime_bounds_check_because="held in range above")
            r2.update(enumerate(v))

        def fetch2(b, after):
            d_c2w[b] = dma(C2W[b], lambda: A["w1"][bass.ds(r2[b], 128), :], after)
        sp.op(load2, [t_eix], inc=False)
        for b in (12, 13, 14, 15, 8, 9, 10, 11, 0, 1, 2, 3, 4, 5, 6, 7):
            fetch2(b, w_ready if b >= 12 else ot if b >= 8 else [u3] if b < 4 else [p_ready[-1]])

        part(4)
        X3, ZT, PT, VV = big(0), big(1), big(2), big(3)

        def mix_evac(c, bk, tp):
            return act.op(lambda e: e.activation(X3[:, cc(c)], bk[:, :], ACT.Identity, bias=col("cbias")), [tp, x2_t[-1]])

        x3_t = batch_mm(WBOT, XT, mix_evac, [[x2_t[c], wbot_t[-1]] for c in range(4)], [4, 5])
        x4_t, vv_t, pp_t = [], [], []

        def decayed(c):
            tp = pe.op(lambda e: e.matmul(BK[0][:, :], ATT[:, 2, :], X3[:, cc(c)], start=True, stop=True), [x3_t[c], late["a"], *free[0]])
            z_t = act.op(lambda e: e.activation(ZT[:, cc(c)], BK[0][:, :], ACT.Copy), [tp])
            free[0] = (z_t,)
            for i in range(4):
                tp = pe.op(lambda e, i=i: e.matmul(BK[1][:, bb_(i)], X3[:, bb_(4 * c + i)], pk2("Wv1"), start=True, stop=True), [*free[1]], inc=(i == 3))
            vv_t.append(act.op(lambda e: e.activation(VV[:, cc(c)], BK[1][:, :], ACT.Copy), [tp]))
            free[1] = (vv_t[c],)
            for i in range(4):
                tp = pe.op(lambda e, i=i: e.matmul(BK[2][:, bb_(i)], X3[:, bb_(4 * c + i)], ZT[:, bb_(4 * c + i)], start=True, stop=True),
                           [z_t, *free[2]], inc=(i == 3))
            pp_t.append(dve.op(lambda e: e.tensor_tensor(PT[:, cc(c)].rearrange("p (b n) -> p b n", b=4), BK[2][:, :].rearrange("p (b n) -> p b n", b=4),
                                                         pk1("decT").unsqueeze(1).to_broadcast([128, 4, 128]), ALU.mult), [tp]))
            free[2] = (pp_t[c],)

        def attended(c):
            for i in range(4):
                tp = pe.op(lambda e, i=i: e.matmul(BK[3][:, bb_(i)], VV[:, bb_(4 * c + i)], PT[:, bb_(4 * c + i)], start=True, stop=True),
                           [vv_t[c], pp_t[c], *free[3]], inc=(i == 3))
            tv = dve.op(lambda e: e.tensor_tensor(XT[:, cc(c)], XT[:, cc(c)], BK[3][:, :], ALU.add), [tp])
            free[3] = (tv,)
            x4_t.append(tv)

        for c in range(5):
            if c < 4:
                decayed(c)
            if c > 0:
                attended(c - 1)

        part(5)
        X5 = big(4)
        SU = [WK[:, 0, 256 * i:256 * i + 256] for i in range(3)]
        HG = [WK[:, 1, 256 * i:256 * i + 256] for i in range(3)]
        hid, dn2, x5_t = {}, {}, []

        def mlp_up(b):
            bk = b % 3
            waits = [d_c2w[b], x4_t[b // 4], *free[bk]]
            for q in range(4):
                tp = pe.op(lambda e, q=q: e.matmul(BK[bk][:, bb_(q)], C2W[b][:, 128 * q:128 * q + 128], XT[:, bb_(b)], start=True, stop=True), waits, inc=(q == 3))
                waits = ()
            for q in range(2):
                ts = act.op(lambda e, q=q: e.activation(SU[b % 3][:, bb_(q)], BK[bk][:, bb_(q)], ACT.Silu, bias=BSEL[:, q, b:b + 1]),
                            [tp, late["bsel"], hid.get(b - 3), oq[-1]])
            for q in range(2):
                th = dve.op(lambda e, q=q: e.scalar_tensor_tensor(HG[b % 3][:, bb_(q)], BK[bk][:, bb_(2 + q)], BSEL[:, 2 + q, b:b + 1],
                                                                  SU[b % 3][:, bb_(q)], ALU.add, ALU.mult), [ts, dn2.get(b - 3)])
            hid[b] = th
            free[bk] = (th,)

        def mlp_down(b):
            bk = 4 + (b // 4) % 2
            waits = [hid[b], *(free[bk] if b % 4 == 0 else ())]
            for q in range(2):
                tp = pe.op(lambda e, q=q: e.matmul(BK[bk][:, bb_(b % 4)], C2W[b][:, 512 + 128 * q:640 + 128 * q], HG[b % 3][:, bb_(q)],
                                                   start=(q == 0), stop=(q == 1)), waits, inc=(q == 1))
                waits = ()
            dn2[b] = tp
            if b % 4 == 3:
                for i in range(4):
                    bb2 = b - 3 + i
                    tv = act.op(lambda e, bb2=bb2, i=i: e.activation(X5[:, bb_(bb2)], BK[bk][:, bb_(i)], ACT.Identity, bias=BSEL[:, 4, bb2:bb2 + 1]), [tp])
                free[bk] = (tv,)
                x5_t.append(tv)

        XSQ = big(0)
        NR, M1, J1, M2, J2, RM, IN, SU1 = (SM[:, 23 + i, :] for i in range(8))
        iota16 = pk1("iota16").rearrange("p (t e) -> p t e", e=16)
        WTS = RA[0:16, 12288:13824]
        WR = [WEFF[:, 512 * i:512 * i + 512] for i in range(4)] + [QT[:, 512 * i:512 * i + 512] for i in range(4)]
        WR += [STG[:, i // 3, 512 * (i % 3):512 * (i % 3) + 512] for i in range(6)] + [PK0T[:, 512 * i:512 * i + 512] for i in range(3)]
        WR += [WBOT[:, 512 * i:512 * i + 512] for i in range(4)] + [RC[:, 512 * i:512 * i + 512] for i in range(12)]
        wd = nc.dram_tensor("expert_weights", (16, N), F32, kind="Internal")
        lg_t, sq_t, w_tok, wts_t, wst, wr_t, wr_free = {}, {}, {}, {}, {}, {}, {}

        def r16(i):
            o = 768 + 256 * (i % 5)
            return WK[:, i // 5, o:o + 256].rearrange("p (t e) -> p t e", e=16)

        def squares(c):
            for i in range(4):
                tp = pe.op(lambda e, i=i: e.transpose(BK[7][:, bb_(i)], X5[:, bb_(4 * c + i)], pk1("ident")), [x5_t[c], *free[7]], inc=(i == 3))
            for i in range(4):
                t_ = 4 * c + i
                sq_t[c] = act.op(lambda e, i=i, t_=t_: e.activation(XSQ[:, bb_(t_)], BK[7][:, bb_(i)], ACT.Square,
                                                                  accum_out=SM[:, 34, t_:t_ + 1]), [tp, x4_t[-1]])
            free[7] = (sq_t[c],)

        def logits(c):
            bk = 6 if c == 0 else 3
            for t_ in range(4 * c, 4 * c + 4):
                lg_t[c] = pe.op(lambda e, t_=t_: e.matmul(BK[bk][:, 16 * t_:16 * t_ + 16], X5[:, bb_(t_)], SNT, start=True, stop=True),
                      [x5_t[c], sn_t, *free[bk]], inc=(t_ == 4 * c + 3))

        def router(c0, c1):
            bk = 6 if c0 == 0 else 3
            ts = slice(4 * c0, 4 * c1)
            nt = 4 * (c1 - c0)
            nr, m1, j1, m2, j2, rm, inn, su1, v, sq = (x[:, ts] for x in (NR, M1, J1, M2, J2, RM, IN, SU1, SM[:, 34, :], SM[:, 35, :]))
            L, EQ, O1, L2, O2, HD, GA = (r16(i)[:, ts, :] for i in range(7))
            iota = iota16[:, ts, :]

            def b16(ap):
                return ap.unsqueeze(2).to_broadcast([128, nt, 16])

            def op(*a):
                return dve.op(*a)
            t = act.op(lambda e: e.activation(sq, v, ACT.Sqrt), [sq_t[c1 - 1]])
            yield "wait"
            t = dve.op(lambda e: e.tensor_scalar(sq, sq, 1e-12, None, ALU.max), [t])
            yield
            t = dve.op(lambda e: e.reciprocal(nr, sq), [t])
            yield
            t = dve.op(lambda e: e.tensor_tensor(nr, nr, v, ALU.mult), [t])
            yield
            t = dve.op(lambda e: e.tensor_tensor(nr, nr, sq, ALU.add), [t])
            yield
            t = dve.op(lambda e: e.tensor_scalar(nr, nr, 0.5, 1e-12, ALU.mult, ALU.max), [t])
            yield
            t = dve.op(lambda e: e.reciprocal(nr, nr), [t])
            yield
            t = dve.op(lambda e: e.tensor_tensor(L, BK[bk][:, 64 * c0:64 * c1].rearrange("p (t e) -> p t e", e=16), b16(nr), ALU.mult), [t, lg_t[c1 - 1]])
            free[bk] = (t,)
            yield
            t = dve.op(lambda e: e.tensor_tensor(L, L, SIG.unsqueeze(1).to_broadcast([128, nt, 16]), ALU.subtract), [t, sg_t])
            yield
            for src, m, ix, oh in ((L, m1, j1, O1), (L2, m2, j2, O2)):
                if src is L2:
                    t = dve.op(lambda e: e.scalar_tensor_tensor(L2, O1, NEG, L, ALU.mult, ALU.add), [t])
                    yield
                t = dve.op(lambda e, m=m, src=src: e.tensor_reduce(m, src, X_AX, ALU.max), [t])
                yield
                if src is L:
                    t = dve.op(lambda e: e.tensor_scalar(rm, m1, 0.0, None, ALU.max), [t])
                    yield
                    t = dve.op(lambda e: e.scalar_tensor_tensor(GA, L, 0.0, b16(rm), ALU.max, ALU.subtract), [t])
                    ta = act.op(lambda e: e.activation(GA, GA, ACT.Exp), [t])
                    yield
                t = dve.op(lambda e, m=m, src=src: e.tensor_tensor(EQ, src, b16(m), ALU.is_equal), [t])
                yield
                t = dve.op(lambda e: e.tensor_tensor(EQ, EQ, iota, ALU.mult), [t])
                yield
                t = dve.op(lambda e, ix=ix: e.tensor_reduce(ix, EQ, X_AX, ALU.min), [t])
                yield
                t = dve.op(lambda e, ix=ix, oh=oh: e.tensor_tensor(oh, iota, b16(ix), ALU.is_equal), [t])
                yield
            t = dve.op(lambda e: e.tensor_scalar(inn, m1, 0.0, None, ALU.is_le), [t])
            yield
            t = dve.op(lambda e: e.tensor_tensor(O1, O1, O2, ALU.add), [t])
            yield
            t = dve.op(lambda e: e.tensor_tensor(O1, O1, b16(inn), ALU.mult), [t])
            yield
            t = dve.op(lambda e: e.scalar_tensor_tensor(HD, L, 0.0, O1, ALU.is_gt, ALU.add), [t])
            yield
            t = dve.op(lambda e: e.tensor_tensor(GA, GA, HD, ALU.mult), [t, ta])
            yield
            t = dve.op(lambda e: e.tensor_reduce(su1, GA, X_AX, ALU.add), [t])
            yield
            t = dve.op(lambda e: e.reciprocal(su1, su1), [t])
            yield
            t = dve.op(lambda e: e.tensor_tensor(GA, GA, b16(su1), ALU.mult), [t])
            yield
            w_tok[c1 - 1] = t

        def spread(c, e1):
            row = bass.AP(tensor=wd, offset=e1 * N + 512 * c, ap=[[0, 128], [1, 512]])
            wr_t[c, e1] = dma(WR[16 * (c % 2) + e1], row, [wst[c], x2_t[-1], p_ready[-1], x3_t[-1], dn2[15 if c % 2 else 7], wr_free.get((c - 2, e1))], last=wr_t.get((c - 2, e1)))

        def turn_weights(c, tok, bk):
            for i in range(4):
                tp = pe.op(lambda e, i=i: e.transpose(BK[bk][0:16, bb_(i)], r16(6)[:, 4 * c + i, :], pk1("ident")), [tok, *free[bk]], inc=(i == 3))
            return tp

        def send_weights(c, tp, bk):
            w = WTS[:, 512 * (c % 3):512 * (c % 3) + 512]
            wts_t[c] = act.op(lambda e: e.activation(w, BK[bk][0:16, :], ACT.Copy), [tp, wst.get(c - 3)])
            free[bk] = (wts_t[c],)
            wst[c] = dma(wd.ap()[:, cc(c)], w, [wts_t[c]], store=True)
            if c < 2:
                for e1 in range(16):
                    spread(c, e1)

        R_OPS, LAG2, n_wait, LG, SQR = 8, 2, 2, 4, 3
        first = None
        for b in range(20):
            if b < 16:
                mlp_up(b)
            if 0 <= b - LAG2 < 16:
                mlp_down(b - LAG2)
            if (b - LG) % 4 == 0 and b >= 4 + LG:
                logits((b - LG) // 4 - 1)
            if (b - SQR) % 4 == 0 and b >= 4 + SQR:
                squares((b - SQR) // 4 - 1)
            if b == 4 + LG:
                first = router(0, 1)
            if first is not None:
                for _ in range(R_OPS):
                    if next(first, "end") in ("wait", "end"):
                        break
            if 0 in w_tok and 0 not in wst:
                if n_wait == 0:
                    send_weights(0, turn_weights(0, w_tok[0], 7), 7)
                n_wait -= 1
        others = router(1, 4)

        part(7)
        QP, KP, VP = big(0), big(1), big(2)
        OT = big(3)
        ZB = big(5)
        zf = [ZB[:, 512 * i:512 * i + 512] for i in range(4)]
        ZH = X16[:, :, :].rearrange("p a (r n) -> p r a n", n=512)
        zf_free, zh_free = [None] * 4, [None] * 4
        PP, VS = WK[:, 0, :], WK[:, 1, :]
        PTT = X5
        NM, SS, RS = (SM[:, 31 + i, :] for i in range(3))
        ACC = {"q": (0, 1, 2), "o": (3,)}
        qkv_t, vs_t, pt_t, o_t = {}, {}, {}, {}

        def chunk_bank(c, bk, mm, after):
            for i in range(4):
                tp = pe.op(lambda e, i=i: mm(e, BK[bk][:, bb_(i)], 4 * c + i), [*after, *free[bk]], inc=(i == 3))
            return tp

        def attend(c):
            sl = slice(4 * c, 4 * c + 4)

            def values():
                tp = chunk_bank(c, 4, lambda e, o, b: e.transpose(o, VP[:, bb_(b)], pk1("ident")), [qkv_t[c]])
                vs_t[c] = act.op(lambda e: e.activation(VS[:, cc(c)], BK[4][:, :], ACT.Copy), [tp, wts_t[3]])
                free[4] = (vs_t[c],)

            def scores():
                tp = chunk_bank(c, 5, lambda e, o, b: e.matmul(o, QP[:, bb_(b)], KP[:, bb_(b)], start=True, stop=True), [qkv_t[c]])
                t = dve.op(lambda e: e.tensor_reduce(NM[:, sl], BK[5][:, :].rearrange("p (b n) -> p b n", b=4), X_AX, ALU.max), [tp])
                t = dve.op(lambda e: e.tensor_scalar(NM[:, sl], NM[:, sl], -ISC, None, ALU.mult), [t])
                for i in range(4):
                    b = 4 * c + i
                    te = act.op(lambda e, b=b, i=i: e.activation(PP[:, bb_(b)], BK[5][:, bb_(i)], ACT.Exp, bias=NM[:, b:b + 1], scale=ISC,
                                                                 accum_out=SS[:, b:b + 1]), [t])
                free[5] = (te,)
                pt_t[c] = te

            def norm():
                t = dve.op(lambda e: e.reciprocal(RS[:, sl], SS[:, sl]), [pt_t[c]])
                pp = PP[:, cc(c)].rearrange("p (b n) -> p b n", b=4)
                pt_t[c] = dve.op(lambda e: e.tensor_tensor(pp, pp, RS[:, sl].unsqueeze(2).to_broadcast([128, 4, 128]), ALU.mult), [t])

            def turn():
                tp = chunk_bank(c, 4, lambda e, o, b: e.transpose(o, PP[:, bb_(b)], pk1("ident")), [pt_t[c]])
                pt_t[c] = act.op(lambda e: e.activation(PTT[:, cc(c)], BK[4][:, :], ACT.Copy), [tp])
                free[4] = (pt_t[c],)

            def mix():
                tp = chunk_bank(c, 5, lambda e, o, b: e.matmul(o, VS[:, bb_(b)], PTT[:, bb_(b)], start=True, stop=True), [vs_t[c], pt_t[c]])
                o_t[c] = act.op(lambda e: e.activation(OT[:, cc(c)], BK[5][:, :], ACT.Copy), [tp])
                free[5] = (o_t[c],)
            return values, scores, norm, turn, mix

        def weigh(it):
            kind, c, e1 = it["id"]
            r = it["n"] % 4
            src, after = (X5, [x5_t[c]]) if kind == "q" else (OT, [o_t[c]])
            w = WR[16 * (c % 2) + e1]
            tz = dve.op(lambda e: e.tensor_tensor(zf[r], src[:, cc(c)], w, ALU.mult), [wr_t[c, e1], zf_free[r], *after])
            if kind == "o" and c < 2:
                wr_free[c, e1] = tz
                spread(c + 2, e1)
            it["hi"] = act.op(lambda e: e.activation(ZH[:, r, 0, :], zf[r], ACT.Copy), [tz, zh_free[r]])

        def weigh_lo(it):
            r = it["n"] % 4
            q = pool if it["pool"] else dve
            zf_free[r] = it["lo"] = q.op(lambda e: e.tensor_tensor(ZH[:, r, 1, :], zf[r], ZH[:, r, 0, :], ALU.subtract), [it["hi"]])

        def product(it):
            kind, c, e1 = it["id"]
            r = it["n"] % 4
            mats = (0, 1, 2) if kind == "q" else (3,)
            waits = [it["lo"], p_ready[-1]]
            for m, bk in zip(mats, ACC[kind]):
                for n, (wp, xp) in enumerate(((0, 0), (1, 0), (0, 1))):
                    wo = (m * 16 + e1) * 128
                    tk = pe.op(lambda e, wo=wo, bk=bk, wp=wp, xp=xp, n=n: e.matmul(
                        BK[bk][:, :], P16[:, wp, wo:wo + 128], ZH[:, r, xp, :], start=(e1 == 0 and n == 0), stop=(e1 == 15 and n == 2)),
                        [*waits, *(free[bk] if e1 == 0 else ())], inc=(n == 2))
                if e1 == 15 and kind == "q":
                    dst = (QP, KP, VP)[m]
                    qkv_t[c] = act.op(lambda e, bk=bk, dst=dst: e.activation(dst[:, cc(c)], BK[bk][:, :], ACT.Copy), [tk])
                    free[bk] = (qkv_t[c],)
                if e1 == 15 and kind == "o":
                    tv = dve.op(lambda e, bk=bk: e.tensor_tensor(XT[:, cc(c)], XT[:, cc(c)], BK[bk][:, :], ALU.add), [tk])
                    free[bk] = (tv,)
                    dma(out[:, cc(c)], XT[:, cc(c)], [tv], store=True)
            zh_free[r] = tk

        HOLD, TP = 10, 3
        seq, held = [("q", 0, e1) for e1 in range(16)], []
        for c in range(4):
            steps = [("do", c, i) for i in range(5)]
            nxt = [("q", c + 1, e1) for e1 in range(16)] if c < 3 else []
            n = 0
            while nxt or (c == 3 and (held or steps)):
                seq += nxt[:1]
                nxt = nxt[1:]
                if held and (held[0][1] < 2 or not nxt or len(held) > HOLD):
                    seq += held[:1]
                    held = held[1:]
                n += 1
                if n > 3 and steps:
                    seq.append(steps.pop(0))
                    if not steps:
                        held += [("o", c, e1) for e1 in range(16)]
        last_q = max(n for n, x in enumerate(y for y in seq if y[0] != "do") if x[0] == "q")

        def by_pool(x, n):
            if n > last_q:
                return n % TP > 0
            return x[0] == "o" or (x[1] == 0 and x[2] % 2 == 1)
        items = []
        for x in seq:
            if x[0] == "do":
                attend_step = attend(x[1])[x[2]]
                items[-1]["then"].append(attend_step)
            else:
                items.append({"id": x, "n": len(items), "then": [], "pool": by_pool(x, len(items))})
        LAG, M_OPS, turned = 3, 5, None
        for k in range(len(items) + LAG):
            if k < len(items):
                weigh(items[k])
            if k == 1:
                squares(3)
                logits(3)
            for _ in range(M_OPS if k >= 3 else 0):
                if next(others, "end") in ("wait", "end"):
                    break
            if turned is None and 3 in w_tok:
                turned = k
            if turned is not None and k == turned + 2:
                tps = [turn_weights(c, w_tok[3], 4 + c) for c in (1, 2, 3)]
            if turned is not None and k == turned + 2 + LAG:
                for c in (1, 2, 3):
                    send_weights(c, tps[c - 1], 4 + c)
            if 0 <= k - 1 < len(items):
                weigh_lo(items[k - 1])
            if k >= LAG:
                product(items[k - LAG])
            if k < len(items):
                for step in items[k]["then"]:
                    step()
        for t in stores:
            sp.op(lambda e, t=t: e.wait_ge(t.sem, t.val), inc=False)

        block = ctx.enter_context(nc.Block())
        block.sync(sp.run)
        block.gpsimd(pool.run)
        block.scalar(act.run)
        block.vector(dve.run)
        block.tensor(pe.run)


def layout(i):
    f = np.float32
    g = {k: np.asarray(v) for k, v in i.items()}
    A = {}
    A["xT"] = g["x"].reshape(N, D).T
    A["condB"] = np.broadcast_to(g["cond_8"][None], (128, 16, 8))

    def moe(gate, up, down):
        parts = [gate.reshape(128, 4, 128), up.reshape(128, 4, 128), down.reshape(4, 128, 128).transpose(1, 0, 2)]
        return np.stack(parts, 2).reshape(128, 1536)
    A["w0"] = np.stack([moe(g["L0_cond_shared_gate"], g["L0_cond_shared_up"], g["L0_cond_shared_down"])] +
                       [moe(g["L0_cond_skill_gate"][e], g["L0_cond_skill_up"][e], g["L0_cond_skill_down"][e]) for e in range(8)])
    sw = np.r_[64:128, 0:64]
    a = "L0_attn_"
    m = np.arange(128)
    l_, b_ = m // 8, m % 8
    idx = np.clip(63 + l_[:, None] - l_[None, :], 0, 126)
    p0 = {"WuT": g[a + "Wu"].T, "WvT": g[a + "Wv"].T, "WbT": g[a + "Wb"].T, "WbsT": g[a + "Wb"][sw].T,
          "WoT": g[a + "Wo"].T.reshape(2, 128, 128).transpose(1, 0, 2).reshape(128, 256),
          "As": g["L0_cond2_As"].reshape(128, 128), "BsT": g["L0_cond2_Bs"].transpose(0, 2, 1).reshape(128, 128),
          "WbaseT": g["L0_cond2_W_base"].T, "relb": g[a + "w_rel"][idx]}
    A["pk0"] = np.concatenate([p0[k] for k in PK0], 1)
    half = 64
    pos = np.arange(16, dtype=f)
    inv = (f(10000.0) ** (-np.arange(half, dtype=f) / f(half))).astype(f)
    ang = (pos[None, :] * inv[:, None]).astype(f)
    cos, sin = np.cos(ang).astype(f), np.sin(ang).astype(f)
    diff = m[None, :] - m[:, None]
    p1 = {"ident": np.eye(128, dtype=f),
          "decT": np.where(diff >= 0, f(0.96875) ** diff.astype(f), f(0)).astype(f),
          "amask": np.where((b_[:, None] == b_[None, :]) & (l_[:, None] <= l_[None, :]), f(0), f(-1e30)).astype(f),
          "cos": np.concatenate([cos, cos]), "sin": np.concatenate([-sin, sin]),
          "condR": np.repeat(g["cond_8"].T, 16, axis=0), "sim": g["L1_ffn_sim_matrix"],
          "iota16": np.broadcast_to(np.tile(np.arange(16, dtype=f) - 99, 16)[None], (128, 256)),
          "kmask": np.tile(np.eye(16, dtype=f), (8, 1))}
    A["pk1"] = np.concatenate([p1[k] for k in PK1], 1)
    A["pka"] = np.concatenate([np.broadcast_to(np.tile(np.arange(8, dtype=f) - 99, 16)[None], (128, 128)),
                               np.broadcast_to(g["L1_ffn_gates"][None], (128, 16))], 1)
    b = "L1_attn_weight_"
    A["pk2"] = np.concatenate([g[b + "q"].T, g[b + "k"].T, g[b + "v"]], 1)
    c = {"ln_g": g[a + "ln_g"], "ln_b": g[a + "ln_b"], "bu0": g[a + "bu"][:128], "bu1": g[a + "bu"][128:], "bb": g[a + "bb"],
         "bbs": g[a + "bb"][sw], "bo": g[a + "bo"], "b_base": g["L0_cond2_b_base"], "cbias": g["L1_cond_bias"], "theta": g["L1_attn_theta"]}
    for q in ("qq", "qk"):
        for w in "wb":
            c[q + w] = g[a + q + w]
            c[q + w + "s"] = g[a + q + w][sw]
    A["cols"] = np.stack([c[k] for k in COLS], 1)
    d = "L1_cond2_b_"
    A["c2b"] = np.stack([g[d + "up"][:, :128].T, g[d + "up"][:, 128:].T, g[d + "gate"][:, :128].T, g[d + "gate"][:, 128:].T, g[d + "down"].T], 1)
    A["bv"] = np.broadcast_to(g[a + "bv"][None], (3, 256))
    A["fw"] = np.concatenate([g["L0_ffn_w_up"].reshape(3, 128, 128), g["L0_ffn_w_gate"].reshape(3, 128, 128),
                              g["L0_ffn_w_down"].reshape(128, 3, 128).transpose(1, 0, 2)]).transpose(1, 0, 2)
    A["l1w"] = g["L1_cond_weight"].reshape(8, 8, 16, 128).transpose(0, 2, 1, 3).reshape(128, 1024)
    A["l1m"] = np.tile(g["L1_cond_mask"].reshape(8, 16, 128).transpose(1, 0, 2).reshape(16, 1024), (8, 1))
    w = "L1_cond2_W_"
    per = [np.concatenate([g[w + "up"][e].T, g[w + "gate"][e].T, g[w + "down"][e].T.reshape(2, 128, 128).transpose(1, 0, 2).reshape(128, 256)], 1)
           for e in range(8)]
    A["w1"] = np.concatenate(per, 0)
    A["w2"] = np.concatenate([g["L1_ffn_" + k].transpose(1, 0, 2).reshape(128, 2048) for k in ("q_proj", "k_proj", "v_proj", "o_proj")], 1)
    return {k: np.ascontiguousarray(v) for k, v in A.items()}


def kernel(**inputs):
    import concourse.bacc as bacc
    from concourse.bass_utils import run_bass_kernel_spmd

    nc = bacc.Bacc("TRN2", target_bir_lowering=False, num_devices=1)
    arrays = {f"in_{k}": v for k, v in layout(inputs).items()}
    A = {k[3:]: nc.dram_tensor(k, v.shape, mybir.dt.from_np(v.dtype), kind="ExternalInput").ap() for k, v in arrays.items()}
    out = nc.dram_tensor("out_0", (128, N), F32, kind="ExternalOutput").ap()
    program(nc, A, out)
    r = run_bass_kernel_spmd(nc, [arrays], core_ids=[0])
    return np.ascontiguousarray(r.results[0]["out_0"].T.reshape(NB, S, D))
```
